# Optimizing a Trainium2 kernel written in Bass

```python
import numpy as np
import jax
import jax.numpy as jnp

def _softmax(x, axis=-1):
    return jax.nn.softmax(x, axis=axis)

def _gelu(x):
    return jax.nn.gelu(x, approximate=True)

def _silu(x):
    return jax.nn.silu(x)

def _sigmoid(x):
    return jax.nn.sigmoid(x)

def _layernorm(x, axis=-1, eps=1e-05):
    m = jnp.mean(x, axis=axis, keepdims=True)
    v = jnp.var(x, axis=axis, keepdims=True)
    return (x - m) / jnp.sqrt(v + eps)

def _scatter_add(tgt, idx, src, axis=0):
    return tgt.at[idx].add(src)

def _segment_sum(src, seg, n):
    return jax.ops.segment_sum(src, seg, n)
kernel_name = 'mk_flamingo_gated_d1_seqx_r8_40e133'

def setup_inputs(seed: int=0):
    np.random.seed(seed)
    _w = jnp.asarray

    def _rec_inputs():
        import jax
        import jax.numpy as jnp
        _rk = jax.random.key(seed)
        x = -0.0002928 + 1 * jax.random.normal(jax.random.fold_in(_rk, 1), (32, 128, 128), jnp.float32)
        _lenS = 128 - jax.random.randint(jax.random.fold_in(_rk, 7), (32,), 0, max(1, 128 // 4) + 1, jnp.int32)
        _lenS2 = 128 - jax.random.randint(jax.random.fold_in(_rk, 8), (32,), 0, max(1, 128 // 4) + 1, jnp.int32)
        _ctx_1024P = jax.random.normal(jax.random.fold_in(_rk, 11), (32, 16, 128), jnp.float32)
        _ctx_1024c = jax.random.dirichlet(jax.random.fold_in(_rk, 511), 0.3 * jnp.ones((16,), jnp.float32), (32, 128))
        _ctx_1024t = jnp.einsum('bsk,bkd->bsd', _ctx_1024c, _ctx_1024P)
        _ctx_1024t = _ctx_1024t * jax.lax.rsqrt(jnp.mean(jnp.square(_ctx_1024t)) + 1e-12) * 0.953939
        ctx_1024 = -1.39393e-06 + 0.999914 * (_ctx_1024t + 0.3 * jax.random.normal(jax.random.fold_in(_rk, 611), (32, 128, 128), jnp.float32))
        _g = jax.random.normal(jax.random.fold_in(_rk, 9001), (2, 1), jnp.float32)
        _g = jnp.sign(_g) * jnp.maximum(jnp.abs(_g), 1.0) + (_g == 0) * 1.0
        g_xattn = _g[0]
        g_ffn = _g[1]
        return (x, ctx_1024, g_xattn, g_ffn)
    x, ctx_1024, g_xattn, g_ffn = _rec_inputs()

    def _L0_xattn_setup():
        import jax, jax.numpy as jnp
        import numpy as np
        D_MODEL = 128
        NUM_HEADS = 16
        D_K = D_MODEL // NUM_HEADS
        BASE = 10000.0

        def _rope_tables(seq_len, d_model, dtype):
            pos = jnp.arange(1, seq_len + 1, dtype=dtype)[:, None]
            theta = BASE ** (-2.0 * jnp.arange(d_model // 2, dtype=dtype) / d_model)
            m_theta = pos * theta
            return (jnp.cos(m_theta), jnp.sin(m_theta))

        def _rotate_half(x):
            d = x.shape[-1]
            return jnp.concatenate([-x[..., d // 2:], x[..., :d // 2]], axis=-1)

        def _apply_rope(x):
            S, D = (x.shape[1], x.shape[2])
            cos, sin = _rope_tables(S, D, x.dtype)
            cos_ri = jnp.repeat(cos, 2, axis=-1)
            sin_ri = jnp.repeat(sin, 2, axis=-1)
            return jax.lax.stop_gradient(x * cos_ri + _rotate_half(x) * sin_ri)
        key = jax.random.key(seed)
        ks = jax.random.split(key, 11)
        B, S, D = (2, 256, D_MODEL)
        scale = 1.0 / np.sqrt(D)
        return {'q': jax.random.normal(ks[0], (B, S, D), jnp.float32), 'k': jax.random.normal(ks[1], (B, S, D), jnp.float32), 'v': jax.random.normal(ks[2], (B, S, D), jnp.float32), 'Wq_w': jax.random.normal(ks[3], (D, D), jnp.float32) * scale, 'Wq_b': jnp.zeros((D,), jnp.float32), 'Wk_w': jax.random.normal(ks[4], (D, D), jnp.float32) * scale, 'Wk_b': jnp.zeros((D,), jnp.float32), 'Wv_w': jax.random.normal(ks[5], (D, D), jnp.float32) * scale, 'Wv_b': jnp.zeros((D,), jnp.float32), 'Wo_w': jax.random.normal(ks[6], (D, D), jnp.float32) * scale, 'Wo_b': jnp.zeros((D,), jnp.float32)}
    _L0_xattn_all = _L0_xattn_setup()
    _L0_xattn_in = {k: v for k, v in _L0_xattn_all.items() if k in ('Wq_w', 'Wq_b', 'Wk_w', 'Wk_b', 'Wv_w', 'Wv_b', 'Wo_w', 'Wo_b')}
    del _L0_xattn_all

    def _L0_ffn_setup():
        import jax, jax.numpy as jnp
        import numpy as np
        EPS = 1e-06
        TOP_K = 2

        def rms_norm(x, scale, eps=EPS):
            xf = x.astype(jnp.float32)
            mean_sq = jnp.mean(xf * xf, axis=-1, keepdims=True)
            return (xf * (scale.astype(jnp.float32) * jax.lax.rsqrt(mean_sq + eps))).astype(x.dtype)
        key = jax.random.key(seed)
        k0, k1, k2, k3 = jax.random.split(key, 4)
        B, S, D, H, E = (2, 256, 128, 352, 8)
        x = jax.random.normal(k0, (B, S, D), dtype=jnp.float32)
        norm_scale = jnp.ones((D,), dtype=jnp.float32)
        w_router = jax.random.normal(k1, (E, D), dtype=jnp.float32) * 0.02
        w_up = jax.random.normal(k2, (E, 2 * H, D), dtype=jnp.float32) * 0.02
        w_down = jax.random.normal(k3, (E, D, H), dtype=jnp.float32) * 0.02
        return {'x': x, 'norm_scale': norm_scale, 'w_router': w_router, 'w_up': w_up, 'w_down': w_down}
    _L0_ffn_all = _L0_ffn_setup()
    _L0_ffn_in = {k: v for k, v in _L0_ffn_all.items() if k in ('norm_scale', 'w_router', 'w_up', 'w_down')}
    del _L0_ffn_all
    return {'x': x, 'ctx_1024': ctx_1024, 'g_xattn': g_xattn, 'g_ffn': g_ffn, 'L0_xattn_Wq_w': _L0_xattn_in['Wq_w'], 'L0_xattn_Wq_b': _L0_xattn_in['Wq_b'], 'L0_xattn_Wk_w': _L0_xattn_in['Wk_w'], 'L0_xattn_Wk_b': _L0_xattn_in['Wk_b'], 'L0_xattn_Wv_w': _L0_xattn_in['Wv_w'], 'L0_xattn_Wv_b': _L0_xattn_in['Wv_b'], 'L0_xattn_Wo_w': _L0_xattn_in['Wo_w'], 'L0_xattn_Wo_b': _L0_xattn_in['Wo_b'], 'L0_ffn_norm_scale': _L0_ffn_in['norm_scale'], 'L0_ffn_w_router': _L0_ffn_in['w_router'], 'L0_ffn_w_up': _L0_ffn_in['w_up'], 'L0_ffn_w_down': _L0_ffn_in['w_down']}

def reference(x, ctx_1024, g_xattn, g_ffn, L0_xattn_Wq_w, L0_xattn_Wq_b, L0_xattn_Wk_w, L0_xattn_Wk_b, L0_xattn_Wv_w, L0_xattn_Wv_b, L0_xattn_Wo_w, L0_xattn_Wo_b, L0_ffn_norm_scale, L0_ffn_w_router, L0_ffn_w_up, L0_ffn_w_down):
    import jax
    import jax.numpy as jnp

    def _L0_xattn_ref(q, k, v, Wq_w, Wq_b, Wk_w, Wk_b, Wv_w, Wv_b, Wo_w, Wo_b):
        import jax, jax.numpy as jnp
        import numpy as np
        D_MODEL = 128
        NUM_HEADS = 16
        D_K = D_MODEL // NUM_HEADS
        BASE = 10000.0

        def _rope_tables(seq_len, d_model, dtype):
            pos = jnp.arange(1, seq_len + 1, dtype=dtype)[:, None]
            theta = BASE ** (-2.0 * jnp.arange(d_model // 2, dtype=dtype) / d_model)
            m_theta = pos * theta
            return (jnp.cos(m_theta), jnp.sin(m_theta))

        def _rotate_half(x):
            d = x.shape[-1]
            return jnp.concatenate([-x[..., d // 2:], x[..., :d // 2]], axis=-1)

        def _apply_rope(x):
            S, D = (x.shape[1], x.shape[2])
            cos, sin = _rope_tables(S, D, x.dtype)
            cos_ri = jnp.repeat(cos, 2, axis=-1)
            sin_ri = jnp.repeat(sin, 2, axis=-1)
            return jax.lax.stop_gradient(x * cos_ri + _rotate_half(x) * sin_ri)
        B, S, D = q.shape
        q = _apply_rope(q)
        k = _apply_rope(k)

        def split_heads(x):
            return x.reshape(B, S, NUM_HEADS, D_K).transpose(0, 2, 1, 3)
        Q = split_heads(q @ Wq_w.T + Wq_b)
        K = split_heads(k @ Wk_w.T + Wk_b)
        V = split_heads(v @ Wv_w.T + Wv_b)
        scores = jnp.einsum('bhqd,bhkd->bhqk', Q, K) / jnp.sqrt(jnp.float32(D_K))
        attn = jax.nn.softmax(scores, axis=-1)
        out = jnp.einsum('bhqk,bhkd->bhqd', attn, V)
        out = out.transpose(0, 2, 1, 3).reshape(B, S, D)
        return out @ Wo_w.T + Wo_b

    def _L0_ffn_ref(x, norm_scale, w_router, w_up, w_down):
        import jax, jax.numpy as jnp
        import numpy as np
        EPS = 1e-06
        TOP_K = 2

        def rms_norm(x, scale, eps=EPS):
            xf = x.astype(jnp.float32)
            mean_sq = jnp.mean(xf * xf, axis=-1, keepdims=True)
            return (xf * (scale.astype(jnp.float32) * jax.lax.rsqrt(mean_sq + eps))).astype(x.dtype)
        skip = x
        xn = rms_norm(x, norm_scale)
        scores = jnp.einsum('bsd,ed->bse', xn, w_router)
        _, ids = jax.lax.top_k(scores, TOP_K)
        probs = jax.nn.softmax(scores, axis=-1)
        c = jnp.take_along_axis(probs, ids, axis=-1)
        h = jnp.einsum('bsd,ehd->bseh', xn, w_up)
        val, gate = jnp.split(h, 2, axis=-1)
        h = val * jax.nn.silu(gate)
        y = jnp.einsum('bseh,edh->bsed', h, w_down)
        yk = jnp.take_along_axis(y, ids[..., None], axis=2)
        out = jnp.sum(yk * c[..., None], axis=2)
        return out + skip
    x = x + jnp.tanh(g_xattn[0]) * _L0_xattn_ref(_layernorm(x, axis=-1), ctx_1024, ctx_1024, L0_xattn_Wq_w, L0_xattn_Wq_b, L0_xattn_Wk_w, L0_xattn_Wk_b, L0_xattn_Wv_w, L0_xattn_Wv_b, L0_xattn_Wo_w, L0_xattn_Wo_b)
    x = x + jnp.tanh(g_ffn[0]) * _L0_ffn_ref(_layernorm(x, axis=-1), L0_ffn_norm_scale, L0_ffn_w_router, L0_ffn_w_up, L0_ffn_w_down)
    return x

_drawn_inputs = setup_inputs


def setup_inputs(seed=0):
    import zlib

    import numpy as np

    out = dict(_drawn_inputs(seed))
    spreads = {'L0_xattn_Wq_b': (0.0, 0.48),
     'L0_xattn_Wk_b': (0.0, 0.8),
     'L0_xattn_Wv_b': (0.0, 0.1),
     'L0_xattn_Wo_b': (0.0, 0.1),
     'L0_ffn_norm_scale': (1.0, 0.6)}
    factors = {'L0_ffn_w_router': 5.371, 'L0_ffn_w_up': 4.673, 'L0_ffn_w_down': 4.678}
    for name, (base, spread) in spreads.items():
        noise = np.random.default_rng([zlib.crc32(name.encode()), seed]).standard_normal(out[name].shape)
        drawn = base * np.exp(spread * noise) if base else spread * noise
        out[name] = jnp.asarray(drawn.astype(out[name].dtype))
    for name, factor in factors.items():
        out[name] = (out[name] * factor).astype(out[name].dtype)
    return out
```

```python
import concourse.bass as bass
import numpy as np
from concourse import mybir
from contextlib import ExitStack

F32 = mybir.dt.float32
BF16 = mybir.dt.bfloat16
U32 = mybir.dt.uint32
I32 = mybir.dt.int32
ALU = mybir.AluOpType
ACT = mybir.ActivationFunctionType
AX = mybir.AxisListType

B, S, D = 32, 128, 128
NH, DK = 16, 8
NI = NH // 2
E, H = 8, 352
CH = 4
NCH = B // CH
CT = CH * S
COMBO_Q = (0, 0, 0, 1, 1, 2)
COMBO_K = (0, 1, 2, 0, 1, 0)
ROWS = len(COMBO_Q) * 2 * DK
NMAX = 2
HC = -(-H // 128)
CAP = B * S + 128
TRASH = E * CAP
NT = -(-(2 * B * S + E * 127) // 128)
NT += -NT % 4
RW = 132
PAD_ROW = 2 * B * S
SCORE_SCALE = float(1.0 / np.sqrt(np.float32(DK)))


def counts(value):
    return not isinstance(value, int) or value > 0


def apart(eng, sem):
    eng.sem_inc(sem, 1)


class Chain:

    def __init__(self, eng, sem, base):
        self.eng, self.sem, self.base, self.n = eng, sem, base, 0

    def link(self, ins):
        self.n += 1
        ins.then_inc(self.sem, 1)
        self.eng.wait_ge(self.sem, self.base + self.n)


def later(j, u, k):
    return j + (u + k) // 8, (u + k) % 8


def inside(j, u):
    return not isinstance(j, int) or 0 <= 8 * j + u < B


def flamingo(nc, x, ctx_in, gates, consts, wqk, bqk, wv, bvb, wo, bob, nscale, wr, wup, wdn, tokrow, out):
    ctx = ExitStack()
    with ctx:
        def sb(name, shape, dt=F32):
            return ctx.enter_context(nc.sbuf_tensor(name, shape, dt))

        def sem(name):
            return ctx.enter_context(nc.semaphore(name))

        slots_dram = nc.dram_tensor("slots_dram", [TRASH + 128, RW], F32, kind="Internal").ap()
        result_dram = nc.dram_tensor("result_dram", [2 * B * S, D], F32, kind="Internal").ap()

        con = sb("con", [128, 5 * 128 + 64 + 2 + 2 * NT])
        ident, cosT, sinT = con[:, 0:128], con[:, 128:256], con[:, 256:384]
        upper, ones = con[:, 384:512], con[:, 512:640]
        iota4 = con[:, 640:672].rearrange("p (k e) -> p k e", k=CH)
        ebase4 = con[:, 672:704].rearrange("p (k e) -> p k e", k=CH)
        exp_no, exp_row = con[0:E, 704:705], con[0:E, 705:706]
        tile_no, tile_row = con[0:E, 706:706 + NT], con[0:E, 706 + NT:706 + 2 * NT]
        conb = sb("conb", [128, 3, 128], BF16)
        identb, upperb, onesb = conb[:, 0, :], conb[:, 1, :], conb[:, 2, :]
        wqk_sb = sb("wqk_sb", [128, 4, 128])
        bqk_sb = sb("bqk_sb", [128, 2])
        wv_sb, bv_sb = sb("wv_sb", [128, 128]), sb("bv_sb", [128, 128])
        wo_sb, bo_sb = sb("wo_sb", [128, 128]), sb("bo_sb", [128, 128])
        gate_sb = sb("gate_sb", [128, 2])
        ns_sb = sb("ns_sb", [128, 1])
        wr_sb = sb("wr_sb", [128, E])
        tok_sb = sb("tok_sb", [128, B, 2], U32)
        tg = sb("tg", [128, 2])
        mhalf = sb("mhalf", [128, CH])

        x_sb = sb("x_sb", [128, B, D])
        ctx_sb = sb("ctx_sb", [128, 2, CH, D])
        xh = sb("xh", [128, CH, D])
        xTs, cTs = sb("xTs", [128, CT]), sb("cTs", [128, CT])
        qa, qb, ka, kb = (sb(n, [128, CT]) for n in ("qa", "qb", "ka", "kb"))
        r1 = sb("r1", [128, 2, CT])
        parts = sb("parts", [128, 2, 3, CT], BF16)
        qz = sb("qz", [128, 2, NI, 2, CT], BF16)
        kp = sb("kp", [128, 2, NI, CT], BF16)
        v9 = sb("v9", [128, 2, CH, NH, DK + 1])
        nmx = sb("nmx", [128, NH])
        mh = sb("mh", [128, 2 * NH], BF16)
        mTs = sb("mTs", [2 * NH, 2, S], BF16)
        pt = sb("pt", [128, NH, S])
        rc = sb("rc", [128, NH])
        on, onT = sb("on", [128, D]), sb("onT", [128, D])
        st6, mv, ve, rs, nmr = (sb("st6", [128, CH, 6]), sb("mv", [128, CH, 2]), sb("ve", [128, CH]),
                                sb("rs", [128, CH]), sb("nmr", [128, CH]))
        st6b, mv2, ve2, rs2 = (sb("st6b", [128, CH, 6]), sb("mv2", [128, CH, 2]), sb("ve2", [128, CH]),
                               sb("rs2", [128, CH]))
        t1, t2, rr, sc2, nb2 = (sb(n, [128, CH]) for n in ("t1", "t2", "rr", "sc2", "nb2"))
        fscale, fbias = sb("fscale", [128, B]), sb("fbias", [128, B])
        cg = sb("cg", [128, B, 2])
        xr = sb("xr", [128, 2, CH, 2, RW])
        nTs = sb("nTs", [128, CT])
        sc, top = sb("sc", [128, CH, E]), sb("top", [128, CH, E])
        idx = sb("idx", [128, CH, E], U32)
        idxf = sb("idxf", [128, CH, 2])
        sub, ee = sb("sub", [128, CH, E]), sb("ee", [128, CH, E])
        m1, m2, msum = sb("m1", [128, CH, E]), sb("m2", [128, CH, E]), sb("msum", [128, CH, E])
        mb = sb("mb", [128, CH, E], BF16)
        carry = sb("carry", [128, E], BF16)
        cs = sb("cs", [128, E])
        tp, tm1, tm2 = (sb(n, [128, CH, E]) for n in ("tp", "tm1", "tm2"))
        slf = sb("slf", [128, 2, CH])
        slu = sb("slu", [128, 2, CH, 2], U32)
        sume, rsum = sb("sume", [128, CH]), sb("rsum", [128, CH])

        wup_sb = sb("wup_sb", [128, E * 2 * H])
        wdn_sb = sb("wdn_sb", [128, HC, E * D])
        cnt_i, nt_i = sb("cnt_i", [E, 1], I32), sb("nt_i", [E, 1], I32)
        ntf, tsf, tef, tc = (sb(n, [E, 1]) for n in ("ntf", "tsf", "tef", "tc"))
        s1, sel = sb("s1", [E, NT]), sb("sel", [E, NT])
        tabv = sb("tabv", [E, 2, NT])
        tab = sb("tab", [1, 2, NT], I32)
        padrow = sb("padrow", [1, E], I32)
        pad_sb = sb("pad_sb", [128, RW])
        xs = sb("xs", [128, 4, RW])
        xT = sb("xT", [128, 2, 128])
        sg, hh = sb("sg", [128, 2, H]), sb("hh", [128, 2, H])
        hT = sb("hT", [128, 2, HC * 128])
        ys = sb("ys", [128, 4, D])
        yi = sb("yi", [128, 4], U32)
        yl = sb("yl", [128, 2, CH, 2, D])

        bank = [ctx.enter_context(nc.psum_tensor(f"bank{i}", [128, 512], F32)) for i in range(8)]
        SB, STB, PVB, SMALL, PA, PB = bank[0:2], bank[2:4], bank[4], bank[5], bank[6], bank[7]
        mT_ps = SMALL[0:2 * NH, 256:320].bitcast(BF16)

        NWL = 10
        w_in, zeroed, cast = sem("w_in"), sem("zeroed"), sem("cast")
        chunk_in = [sem("chunk_in0"), sem("chunk_in1")]
        stack_in = [sem("stack_in0"), sem("stack_in1")]
        m_in = [sem("m_in0"), sem("m_in1")]
        scattered = [sem("scattered0"), sem("scattered1")]
        pe_s, pe_st, pe_pv, pe_mT, pe_aT, pe_o = map(sem, ("pe_s", "pe_st", "pe_pv", "pe_mT", "pe_aT", "pe_o"))
        pe_xT, pe_qk, pe_v, pe_nT, pe_r, pe_pos = map(sem, ("pe_xT", "pe_qk", "pe_v", "pe_nT", "pe_r", "pe_pos"))
        a_tg, a_xh, a_xT, a_hi, a_mid, a_exp, a_aT, a_xn, a_nT, a_e = map(
            sem, ("a_tg", "a_xh", "a_xT", "a_hi", "a_mid", "a_exp", "a_aT", "a_xn", "a_nT", "a_e"))
        d_max, d_mh, d_m, d_mT, d_rc, d_on, d_x1, d_q, d_r1, d_v = map(
            sem, ("d_max", "d_mh", "d_m", "d_mT", "d_rc", "d_on", "d_x1", "d_q", "d_r1", "d_v"))
        d_stat, d_ve, d_rs, d_stat2, d_ve2, d_t2, d_sc2, d_rt, d_top, d_m12, d_slot, d_sl, d_pr = map(
            sem, ("d_stat", "d_ve", "d_rs", "d_stat2", "d_ve2", "d_t2", "d_sc2", "d_rt", "d_top", "d_m12",
                  "d_slot", "d_sl", "d_pr"))
        p_gbo, p_rs, p_k, p_lo, p_xb, p_rs2, p_rr = map(
            sem, ("p_gbo", "p_rs", "p_k", "p_lo", "p_xb", "p_rs2", "p_rr"))
        d_mb, d_cg, d_zero, a_base = map(sem, ('d_mb', 'd_cg', 'd_zero', 'a_base'))
        out_sem, d_apart, p_apart, s_apart = map(sem, ("out_sem", "d_apart", "p_apart", "s_apart"))
        wf_in, padded = sem("wf_in"), sem("padded")
        pe_cnt, pe_ts, pe_tab, d_nt, d_ts, d_tab, d_tc = map(
            sem, ("pe_cnt", "pe_ts", "pe_tab", "d_nt", "d_ts", "d_tab", "d_tc"))
        tile_in = [sem(f"tile_in{r}") for r in range(4)]
        sent = [sem(f"sent{r}") for r in range(4)]
        f_x, f_up, f_hT, f_y = map(sem, ("f_x", "f_up", "f_hT", "f_y"))
        fa_x, fa_g, fa_y, fd_i, fd_h, fd_hT = map(sem, ("fa_x", "fa_g", "fa_y", "fd_i", "fd_h", "fd_hT"))
        back_in = [sem("back_in0"), sem("back_in1")]
        d_o, d_o1 = sem("d_o"), sem("d_o1")

        def tile_after(q, r, k):
            return q + (r + k) // 4, (r + k) % 4

        def is_tile(q, r):
            return not isinstance(q, int) or 4 * q + r < NT

        def blocks(eng, body):
            body(0)
            with eng.Fori(1, B // 8 - 1) as j:
                body(j)
            body(B // 8 - 1)

        block = ctx.enter_context(nc.Block())

        @block.sync
        def _(sp):
            def load(j, cc):
                c = 2 * j + cc
                if counts(2 * c - 2):
                    sp.wait_ge(pe_xT, 2 * c - 2)
                sp.dma_start(x_sb[:, bass.ds(CH * c, CH), :], x[bass.ds(CH * c, CH), :, :].rearrange("b s d -> s b d"))\
                    .then_inc(chunk_in[cc], 16)
                sp.dma_start(ctx_sb[:, cc, :, :], ctx_in[bass.ds(CH * c, CH), :, :].rearrange("b s d -> s b d"))\
                    .then_inc(chunk_in[cc], 16)

            def stack_q(cc, combos):
                for n in combos:
                    for half in range(2):
                        row = n * 2 * DK + half * DK
                        sp.dma_start(qz[row:row + DK, cc, :, half, :],
                                     parts[half * 64:half * 64 + 64, 0, COMBO_Q[n], :]).then_inc(stack_in[cc], 16)

            def stack_k(cc, combos):
                for n in combos:
                    sp.dma_start(kp[n * 2 * DK:(n + 1) * 2 * DK, cc, :, :],
                                 parts[:, 1, COMBO_K[n], :]).then_inc(stack_in[cc], 16)

            def stack_first(j, cc):
                c = 2 * j + cc
                if counts(16 * (c - 1)):
                    sp.wait_ge(pe_st, 16 * (c - 1))
                apart(sp, s_apart)
                sp.wait_ge(a_hi, 2 * c + 1)
                stack_q(cc, (0, 1, 2))

            def stack_rest(j, cc):
                c = 2 * j + cc
                sp.wait_ge(a_hi, 2 * c + 2)
                stack_k(cc, (0, 3, 5))
                sp.wait_ge(a_mid, 2 * c + 2)
                stack_q(cc, (3, 4))
                stack_k(cc, (1, 4))
                sp.wait_ge(p_lo, 2 * c + 2)
                stack_q(cc, (5,))
                stack_k(cc, (2,))

            def maxima(j, u):
                sp.wait_ge(d_mT, 8 * j + u + 1)
                t0 = (u % CH) * S
                sp.dma_start(qz[ROWS:ROWS + NMAX, u // CH, :, :, t0:t0 + S].rearrange("r i h t -> r (i h) t"),
                             mTs[:, u % 2, :]).then_inc(m_in[u % 2], 16)

            def store(c):
                sp.wait_ge(d_o, c + 1)
                sp.dma_start(out[CH * c:CH * (c + 1), :, :].rearrange("b s d -> s b d"), x_sb[:, CH * c:CH * (c + 1), :])\
                    .then_inc(out_sem, 16)

            for dst, src in ((con[:, :], consts), (wqk_sb[:, :, :], wqk), (bqk_sb[:, :], bqk), (wv_sb[:, :], wv),
                             (bv_sb[:, :], bvb), (wo_sb[:, :], wo), (bo_sb[:, :], bob), (gate_sb[:, :], gates),
                             (ns_sb[:, :], nscale), (wr_sb[:, :], wr)):
                sp.dma_start(dst, src).then_inc(w_in, 16)
            load(0, 0)
            load(0, 1)
            sp.wait_ge(d_zero, 3)
            sp.wait_ge(zeroed, 3)
            stack_first(0, 0)
            stack_rest(0, 0)
            maxima(0, 0)

            sp.dma_start(wup_sb[:, :], wup).then_inc(wf_in, 16)
            for n in range(HC):
                rows_n = min(128, H - 128 * n)
                sp.dma_start(wdn_sb[0:rows_n, n, :], wdn[128 * n:128 * n + rows_n, :]).then_inc(wf_in, 16)

            def body(j):
                for u in range(8):
                    uu, cc = u % CH, u // CH
                    nj, ncc = (j, 1) if cc == 0 else (j + 1, 0)
                    if uu == 0 and inside(j + 1, 4 * cc):
                        load(j + 1, cc)
                    if uu == 1 and inside(nj, 4 * ncc):
                        stack_first(nj, ncc)
                    if inside(*later(j, u, 1)):
                        maxima(*later(j, u, 1))
                    if uu == 1 and inside(nj, 4 * ncc):
                        stack_rest(nj, ncc)

            blocks(sp, body)
            sp.wait_ge(d_nt, 1)
            sp.wait_ge(zeroed, 5)
            for e in range(E):
                row = sp.value_load(padrow[0:1, e:e + 1], min_val=0, max_val=TRASH - 128)
                sp.dma_start(slots_dram[bass.ds(row, 128), :], pad_sb[:, :]).then_inc(padded, 16)
            sp.wait_ge(padded, 16 * E)
            sp.wait_ge(scattered[0], 16 + 128 * (B // 8))
            sp.wait_ge(scattered[1], 16 + 128 * (B // 8))
            sp.wait_ge(d_tab, 1)

            def body(q):
                for r in range(4):
                    t = 4 * q + r
                    row = sp.value_load(tab[0:1, 0, bass.ds(t, 1)], min_val=0, max_val=TRASH)
                    if counts(t - 3):
                        sp.wait_ge(f_x, t - 3)
                    if counts(t - 3):
                        sp.wait_ge(fd_i, t - 3)
                    sp.dma_start(xs[:, r, :], slots_dram[bass.ds(row, 128), :]).then_inc(tile_in[r], 16)

            body(0)
            with sp.Fori(1, NT // 4) as q:
                body(q)
            for r in range(4):
                sp.wait_ge(sent[r], 16 * (NT // 4))
            for c in range(NCH):
                if counts(c - 1):
                    sp.wait_ge(d_o, c - 1)
                sp.dma_start(yl[:, c % 2, :, :, :], result_dram[c * 2 * CT:(c + 1) * 2 * CT, :]
                             .rearrange("(b s k) d -> s b k d", s=S, k=2)).then_inc(back_in[c % 2], 16)
                if c > 0:
                    store(c - 1)
            store(NCH - 1)
            sp.wait_ge(out_sem, 16 * NCH)

        @block.gpsimd
        def _(pool):
            def power(j, cc):
                c = 2 * j + cc
                pool.wait_ge(d_ve, c + 1)
                if counts(c):
                    pool.wait_ge(a_xh, c)
                nc.gpsimd.tensor_tensor(rs[:, :], ve[:, :], mhalf[:, :], ALU.pow).then_inc(p_rs, 1)

            def rotate_k(j, cc):
                c = 2 * j + cc
                pool.wait_ge(a_xT, 2 * c + 2)
                if counts(2 * c):
                    pool.wait_ge(pe_qk, 2 * c)
                for dst, tab in ((ka, cosT), (kb, sinT)):
                    last = nc.gpsimd.tensor_tensor(dst[:, :].rearrange("p (k s) -> p k s", k=CH),
                                                   cTs[:, :].rearrange("p (k s) -> p k s", k=CH),
                                                   tab.unsqueeze(1).to_broadcast([128, CH, S]), ALU.mult)
                last.then_inc(p_k, 1)

            def low(j, cc):
                c = 2 * j + cc
                for t in range(2):
                    pool.wait_ge(a_mid, 2 * c + t + 1)
                    nc.gpsimd.tensor_tensor(parts[:, t, 2, :], r1[:, t, :], parts[:, t, 1, :], ALU.subtract)\
                        .then_inc(p_lo, 1)

            def add_bias(j, cc):
                c = 2 * j + cc
                pool.wait_ge(a_xh, c + 1)
                nc.gpsimd.tensor_tensor(x_sb[:, bass.ds(CH * c, CH), :], x_sb[:, bass.ds(CH * c, CH), :],
                                        bo_sb[:, :].unsqueeze(1).to_broadcast([128, CH, D]), ALU.add).then_inc(p_xb, 1)

            def power2a(j, cc):
                c = 2 * j + cc
                pool.wait_ge(d_ve2, c + 1)
                nc.gpsimd.tensor_tensor(rs2[:, :], ve2[:, :], mhalf[:, :], ALU.pow).then_inc(p_rs2, 1)

            def power2b(j, cc):
                c = 2 * j + cc
                pool.wait_ge(d_t2, c + 1)
                nc.gpsimd.tensor_tensor(rr[:, :], t2[:, :], mhalf[:, :], ALU.pow).then_inc(p_rr, 1)

            def scatter(j, cc, batches):
                c = 2 * j + cc
                pool.wait_ge(d_slot, c + 1)
                pool.wait_ge(a_xn, c + 1)
                apart(pool, p_apart)
                for k in batches:
                    for kk in range(2):
                        nc.gpsimd.indirect_dma_start(
                            out=slots_dram, out_offset=bass.IndirectOffsetOnAxis(ap=slu[:, cc, k, kk:kk + 1], axis=0),
                            in_=xr[:, cc, k, kk, :], in_offset=None).then_inc(scattered[cc], 16)

            nc.gpsimd.memset(kp[96:128, :, :, :], 1.0).then_inc(zeroed, 1)
            pool.wait_ge(zeroed, 1)
            nc.gpsimd.memset(xr[:, :, :, :, :], 0.0).then_inc(zeroed, 1)
            nc.gpsimd.memset(mhalf[:, :], -0.5).then_inc(zeroed, 1)
            nc.gpsimd.memset(pad_sb[:, :], 0.0).then_inc(zeroed, 1)
            pool.wait_ge(zeroed, 4)
            nc.gpsimd.memset(pad_sb[:, D:D + 1].bitcast(U32), PAD_ROW).then_inc(zeroed, 1)
            pool.wait_ge(zeroed, 5)
            pool.dma_start(slots_dram[TRASH:TRASH + 128, :], pad_sb[:, :]).then_inc(scattered[0], 16)
            pool.dma_start(tok_sb[:, :, :], tokrow).then_inc(scattered[1], 16)
            pool.wait_ge(w_in, 16 * NWL)
            pool.wait_ge(a_tg, 1)
            nc.gpsimd.tensor_scalar(bo_sb[:, :], bo_sb[:, :], tg[:, 0:1], None, ALU.mult).then_inc(p_gbo, 1)
            pool.wait_ge(p_gbo, 1)
            pool.wait_ge(zeroed, 3)
            power(0, 0)
            rotate_k(0, 0)
            low(0, 0)
            add_bias(0, 0)
            power(0, 1)
            add_bias(0, 1)

            def body(j):
                for u in range(8):
                    uu, cc = u % CH, u // CH
                    nj, ncc = (j, 1) if cc == 0 else (j + 1, 0)
                    pj, pcc = (j - 1, 1) if cc == 0 else (j, 0)
                    if uu == 0:
                        if inside(nj, 4 * ncc):
                            rotate_k(nj, ncc)
                        if inside(pj, 4 * pcc):
                            power2a(pj, pcc)
                    if uu == 1:
                        if inside(nj, 4 * ncc):
                            low(nj, ncc)
                        if inside(pj, 4 * pcc):
                            power2b(pj, pcc)
                    if uu == 2:
                        if inside(j + 1, 4 * cc):
                            power(j + 1, cc)
                        if inside(j - 1, 4 * cc):
                            scatter(j - 1, cc, (0, 1))
                    if uu == 3:
                        if inside(j + 1, 4 * cc):
                            add_bias(j + 1, cc)
                        if inside(j - 1, 4 * cc):
                            scatter(j - 1, cc, (2, 3))

            blocks(pool, body)
            J = B // 8 - 1
            power2a(J, 1)
            power2b(J, 1)
            scatter(J, 0, range(CH))
            scatter(J, 1, range(CH))

            def send(q):
                for r in range(4):
                    pool.wait_ge(fa_y, 4 * q + r + 1)
                    apart(pool, p_apart)
                    nc.gpsimd.indirect_dma_start(
                        out=result_dram, out_offset=bass.IndirectOffsetOnAxis(ap=yi[:, r:r + 1], axis=0),
                        in_=ys[:, r, :], in_offset=None, bounds_check=PAD_ROW - 1, oob_is_err=False)\
                        .then_inc(sent[r], 16)

            with pool.Fori(0, NT // 4) as q:
                send(q)

        @block.scalar
        def _(act):
            def normalise(j, cc):
                c = 2 * j + cc
                act.wait_ge(d_rs, c + 1)
                if counts(2 * c - 1):
                    act.wait_ge(pe_xT, 2 * c - 1)
                for k in range(CH):
                    last = nc.scalar.activation(xh[:, k, :], x_sb[:, bass.ds(CH * c + k, 1), :], ACT.Identity,
                                                bias=nmr[:, k:k + 1], scale=rs[:, k:k + 1])
                last.then_inc(a_xh, 1)

            def transposed(j, cc):
                c = 2 * j + cc
                act.wait_ge(pe_xT, 2 * c + 1)
                if counts(c):
                    act.wait_ge(d_q, c)
                nc.scalar.activation(xTs[:, :], PA[:, :], ACT.Copy).then_inc(a_xT, 1)
                act.wait_ge(pe_xT, 2 * c + 2)
                if counts(c):
                    act.wait_ge(p_k, c)
                if counts(c):
                    act.wait_ge(pe_v, c)
                nc.scalar.activation(cTs[:, :], PB[:, :], ACT.Copy).then_inc(a_xT, 1)

            def high(j, cc):
                c = 2 * j + cc
                if counts(288 * (j + cc)):
                    act.wait_ge(stack_in[1 - cc], 288 * (j + cc))
                for t, ps in ((0, PA), (1, PB)):
                    act.wait_ge(pe_qk, 2 * c + t + 1)
                    nc.scalar.activation(parts[:, t, 0, :], ps[:, :], ACT.Identity, bias=bqk_sb[:, t:t + 1])\
                        .then_inc(a_hi, 1)

            def middle(j, cc):
                c = 2 * j + cc
                for t in range(2):
                    act.wait_ge(d_r1, 2 * c + t + 1)
                    nc.scalar.activation(parts[:, t, 1, :], r1[:, t, :], ACT.Copy).then_inc(a_mid, 1)

            def exponent(j, u, g):
                b = 8 * j + u
                act.wait_ge(pe_st, 4 * b + g + 1)
                if counts(4 * (b - 1) + g + 1):
                    act.wait_ge(pe_pv, 4 * (b - 1) + g + 1)
                nc.scalar.activation(pt[:, 4 * g:4 * g + 4, :], STB[g % 2][:, :].rearrange("p (h s) -> p h s", h=4),
                                     ACT.Exp, scale=SCORE_SCALE).then_inc(a_exp, 1)

            def attended(j, u):
                b = 8 * j + u
                act.wait_ge(pe_aT, b + 1)
                if counts(b):
                    act.wait_ge(pe_o, b)
                nc.scalar.activation(onT[:, :], SMALL[:, 0:D], ACT.Copy).then_inc(a_aT, 1)

            def rows(j, cc):
                c = 2 * j + cc
                act.wait_ge(d_sc2, c + 1)
                act.wait_ge(scattered[cc], 16 + 128 * j)
                for k in range(CH):
                    for kk in range(2):
                        last = nc.scalar.activation(xr[:, cc, k, kk, 0:D], x_sb[:, bass.ds(CH * c + k, 1), :], ACT.Identity,
                                                    bias=nb2[:, k:k + 1], scale=sc2[:, k:k + 1])
                last.then_inc(a_xn, 1)
                act.wait_ge(a_xn, c + 1)
                for k in range(CH):
                    last = nc.scalar.activation(x_sb[:, bass.ds(CH * c + k, 1), :], x_sb[:, bass.ds(CH * c + k, 1), :],
                                                ACT.Identity, bias=fbias[:, bass.ds(CH * c + k, 1)],
                                                scale=fscale[:, bass.ds(CH * c + k, 1)])
                last.then_inc(a_base, 1)

            def rows_transposed(j, cc):
                c = 2 * j + cc
                act.wait_ge(pe_nT, c + 1)
                if counts(c):
                    act.wait_ge(pe_r, c)
                nc.scalar.activation(nTs[:, :], PA[:, :], ACT.Identity, scale=ns_sb[:, 0:1]).then_inc(a_nT, 1)

            def expert_exp(j, cc):
                act.wait_ge(d_top, 2 * j + cc + 1)
                nc.scalar.activation(ee[:, :, :], sub[:, :, :], ACT.Exp).then_inc(a_e, 1)

            act.wait_ge(w_in, 16 * NWL)
            act.wait_ge(zeroed, 3)
            nc.scalar.activation(tg[:, :], gate_sb[:, :], ACT.Tanh).then_inc(a_tg, 1)
            normalise(0, 0)
            transposed(0, 0)
            high(0, 0)
            middle(0, 0)
            normalise(0, 1)

            def body(j):
                for u in range(8):
                    uu, cc = u % CH, u // CH
                    nj, ncc = (j, 1) if cc == 0 else (j + 1, 0)
                    pj, pcc = (j - 1, 1) if cc == 0 else (j, 0)
                    if uu == 0 and inside(j - 1, 4 * cc):
                        expert_exp(j - 1, cc)
                    if inside(*later(j, u, -1)):
                        attended(*later(j, u, -1))
                    if uu == 0 and inside(nj, 4 * ncc):
                        transposed(nj, ncc)
                    if uu == 1 and inside(nj, 4 * ncc):
                        high(nj, ncc)
                        middle(nj, ncc)
                    if uu == 2 and inside(pj, 4 * pcc):
                        rows(pj, pcc)
                    if uu == 3:
                        if inside(j + 1, 4 * cc):
                            normalise(j + 1, cc)
                        if inside(pj, 4 * pcc):
                            rows_transposed(pj, pcc)
                    for g in range(4):
                        exponent(j, u, g)

            blocks(act, body)
            J = B // 8 - 1
            expert_exp(J, 0)
            attended(J, 7)
            rows(J, 1)
            rows_transposed(J, 1)
            expert_exp(J, 1)

            def rows_up(q, r):
                t = 4 * q + r
                act.wait_ge(f_x, t + 1)
                if counts(2 * (t - 1)):
                    act.wait_ge(f_up, 2 * (t - 1))
                nc.scalar.activation(xT[:, r % 2, :], bank[4][:, 0:128], ACT.Identity, scale=ns_sb[:, 0:1])\
                    .then_inc(fa_x, 1)

            def gate(q, r):
                t = 4 * q + r
                act.wait_ge(f_up, 2 * t + 1)
                if counts(t - 1):
                    act.wait_ge(fd_h, t - 1)
                nc.scalar.activation(sg[:, r % 2, :], bank[2 * (r % 2)][:, 0:H], ACT.Silu).then_inc(fa_g, 1)

            def result(q, r):
                t = 4 * q + r
                act.wait_ge(f_y, t + 1)
                if counts(16 * q):
                    act.wait_ge(sent[r], 16 * q)
                nc.scalar.activation(ys[:, r, :], bank[6 + r % 2][:, 0:D], ACT.Copy).then_inc(fa_y, 1)

            for r in range(3):
                rows_up(0, r)
                if r:
                    gate(0, r - 1)

            def body(q):
                for r in range(4):
                    if is_tile(*tile_after(q, r, 3)):
                        rows_up(*tile_after(q, r, 3))
                    if is_tile(*tile_after(q, r, 2)):
                        gate(*tile_after(q, r, 2))
                    result(q, r)

            body(0)
            with act.Fori(1, NT // 4 - 1) as q:
                body(q)
            body(NT // 4 - 1)

        @block.vector
        def _(dve):
            def statistics(j, cc):
                c = 2 * j + cc
                dve.wait_ge(chunk_in[cc], 32 * (j + 1))
                ch = Chain(dve, d_stat, 2 * c)
                for k in range(CH):
                    last = nc.vector.bn_stats(st6[:, k, :], x_sb[:, bass.ds(CH * c + k, 1), :])
                ch.link(last)
                if counts(c):
                    dve.wait_ge(a_xh, c)
                apart(dve, d_apart)
                for k in range(CH):
                    last = nc.vector.bn_aggr(mv[:, k, :], st6[:, k, :])
                ch.link(last)
                nc.vector.tensor_scalar(ve[:, :], mv[:, :, 1], 1e-5, None, ALU.add).then_inc(d_ve, 1)
                dve.wait_ge(p_rs, c + 1)
                nc.vector.scalar_tensor_tensor(nmr[:, :], mv[:, :, 0], -1.0, rs[:, :], ALU.mult, ALU.mult)\
                    .then_inc(d_rs, 1)

            def rotate_q(j, cc):
                c = 2 * j + cc
                dve.wait_ge(a_xT, 2 * c + 1)
                if counts(2 * c - 1):
                    dve.wait_ge(pe_qk, 2 * c - 1)
                for dst, tab in ((qa, cosT), (qb, sinT)):
                    last = nc.vector.tensor_tensor(dst[:, :].rearrange("p (k s) -> p k s", k=CH),
                                                   xTs[:, :].rearrange("p (k s) -> p k s", k=CH),
                                                   tab.unsqueeze(1).to_broadcast([128, CH, S]), ALU.mult)
                last.then_inc(d_q, 1)

            def remainder(j, cc):
                c = 2 * j + cc
                for t, ps in ((0, PA), (1, PB)):
                    dve.wait_ge(a_hi, 2 * c + t + 1)
                    if counts(2 * c - 1 + t):
                        dve.wait_ge(p_lo, 2 * c - 1 + t)
                    nc.vector.scalar_tensor_tensor(r1[:, t, :], ps[:, :], bqk_sb[:, t:t + 1], parts[:, t, 0, :],
                                                   ALU.add, ALU.subtract).then_inc(d_r1, 1)

            def values(j, cc):
                c = 2 * j + cc
                dve.wait_ge(pe_v, c + 1)
                if counts(16 * (c - 1)):
                    dve.wait_ge(pe_pv, 16 * (c - 1))
                nc.vector.tensor_tensor(v9[:, cc, :, :, 0:DK],
                                        PA[:, :].rearrange("p (k h d) -> p k h d", k=CH, h=NH),
                                        bv_sb[:, :].rearrange("p (h d) -> p h d", h=NH).unsqueeze(1)
                                        .to_broadcast([128, CH, NH, DK]), ALU.add).then_inc(d_v, 1)

            def maximum(j, u, g):
                b = 8 * j + u
                dve.wait_ge(pe_s, 4 * b + g + 1)
                if g == 0:
                    if counts(b):
                        dve.wait_ge(d_m, b)
                nc.vector.tensor_reduce(nmx[:, 4 * g:4 * g + 4], SB[g % 2][:, :].rearrange("p (h s) -> p h s", h=4),
                                        AX.X, ALU.max, negate=True).then_inc(d_max, 1)

            def split_maximum(j, u):
                b = 8 * j + u
                dve.wait_ge(d_max, 4 * b + 4)
                if counts(b):
                    dve.wait_ge(pe_mT, b)
                nc.vector.tensor_copy(mh[:, 0:NH], nmx[:, :]).then_inc(d_mh, 1)
                dve.wait_ge(d_mh, b + 1)
                nc.vector.tensor_tensor(mh[:, NH:2 * NH], nmx[:, :], mh[:, 0:NH], ALU.subtract).then_inc(d_m, 1)

            def maximum_transposed(j, u):
                b = 8 * j + u
                dve.wait_ge(pe_mT, b + 1)
                if counts(16 * (4 * j + u // 2)):
                    dve.wait_ge(m_in[u % 2], 16 * (4 * j + u // 2))
                nc.vector.tensor_copy(mTs[:, u % 2, :], mT_ps).then_inc(d_mT, 1)

            def divide(j, u):
                b = 8 * j + u
                dve.wait_ge(pe_pv, 4 * b + 4)
                pv = PVB[:, 0:NH * (DK + 1)].rearrange("p (h d) -> p h d", h=NH)
                nc.vector.reciprocal(rc[:, :], pv[:, :, DK]).then_inc(d_rc, 1)
                dve.wait_ge(d_rc, b + 1)
                if counts(b):
                    dve.wait_ge(pe_aT, b)
                nc.vector.tensor_tensor(on[:, :].rearrange("p (h d) -> p h d", h=NH), pv[:, :, 0:DK],
                                        rc[:, :].unsqueeze(2).to_broadcast([128, NH, DK]), ALU.mult).then_inc(d_on, 1)

            def add_attention(j, u):
                b = 8 * j + u
                dve.wait_ge(pe_o, b + 1)
                dve.wait_ge(p_xb, 2 * j + u // CH + 1)
                nc.vector.scalar_tensor_tensor(x_sb[:, bass.ds(b, 1), :].rearrange("p b d -> p (b d)"), SMALL[:, D:2 * D], tg[:, 0:1], x_sb[:, bass.ds(b, 1), :].rearrange("p b d -> p (b d)"),
                                               ALU.mult, ALU.add).then_inc(d_x1, 1)

            def statistics2(j, cc):
                c = 2 * j + cc
                dve.wait_ge(d_x1, CH * (c + 1))
                if counts(c):
                    dve.wait_ge(a_xn, c)
                ch = Chain(dve, d_stat2, 2 * c)
                for k in range(CH):
                    last = nc.vector.bn_stats(st6b[:, k, :], x_sb[:, bass.ds(CH * c + k, 1), :])
                ch.link(last)
                apart(dve, d_apart)
                for k in range(CH):
                    last = nc.vector.bn_aggr(mv2[:, k, :], st6b[:, k, :])
                ch.link(last)
                nc.vector.tensor_scalar(ve2[:, :], mv2[:, :, 1], 1e-5, None, ALU.add).then_inc(d_ve2, 1)

            def scales2(j, cc):
                c = 2 * j + cc
                ch = Chain(dve, d_rt, 6 * c)
                dve.wait_ge(p_rs2, c + 1)
                ch.link(nc.vector.tensor_tensor(t1[:, :], mv2[:, :, 1], rs2[:, :], ALU.mult))
                ch.link(nc.vector.tensor_tensor(t1[:, :], t1[:, :], rs2[:, :], ALU.mult))
                nc.vector.tensor_scalar(t2[:, :], t1[:, :], 1e-6, None, ALU.add).then_inc(d_t2, 1)
                fs, fb = fscale[:, bass.ds(CH * c, CH)], fbias[:, bass.ds(CH * c, CH)]
                nc.vector.tensor_scalar(fs, rs2[:, :], tg[:, 1:2], 1.0, ALU.mult, ALU.add)
                ch.link(nc.vector.scalar_tensor_tensor(nb2[:, :], mv2[:, :, 0], -1.0, rs2[:, :], ALU.mult, ALU.mult))
                ch.link(nc.vector.tensor_scalar(fb, nb2[:, :], tg[:, 1:2], None, ALU.mult))
                dve.wait_ge(p_rr, c + 1)
                ch.link(nc.vector.tensor_tensor(nb2[:, :], nb2[:, :], rr[:, :], ALU.mult))
                ch.link(nc.vector.tensor_tensor(sc2[:, :], rs2[:, :], rr[:, :], ALU.mult))
                nc.vector.tensor_copy(t1[:, 0:1], sc2[:, 0:1]).then_inc(d_sc2, 1)

            def choose(j, cc):
                c = 2 * j + cc
                ch = Chain(dve, d_m12, 5 * c)
                dve.wait_ge(pe_r, c + 1)
                if counts(c):
                    dve.wait_ge(pe_pos, c)
                if counts(c):
                    dve.wait_ge(a_e, c)
                ch.link(nc.vector.tensor_copy(sc[:, :, :], PB[:, 0:CH * E].rearrange("p (k e) -> p k e", k=CH)))
                apart(dve, d_apart)
                for k in range(CH):
                    last = nc.vector.max(top[:, k, :], sc[:, k, :])
                ch.link(last)
                apart(dve, d_apart)
                for k in range(CH):
                    last = nc.vector.max_index(idx[:, k, :], top[:, k, :], sc[:, k, :])
                nc.vector.tensor_tensor(sub[:, :, :], top[:, :, :], top[:, :, 0:1].to_broadcast([128, CH, E]),
                                        ALU.subtract).then_inc(d_top, 1)
                dve.wait_ge(d_top, c + 1)
                ch.link(nc.vector.tensor_copy(idxf[:, :, :], idx[:, :, 0:2]))
                nc.vector.tensor_tensor(m1[:, :, :], iota4, idxf[:, :, 0:1].to_broadcast([128, CH, E]), ALU.is_equal)
                ch.link(nc.vector.tensor_tensor(m2[:, :, :], iota4, idxf[:, :, 1:2].to_broadcast([128, CH, E]), ALU.is_equal))
                ch.link(nc.vector.tensor_tensor(msum[:, :, :], m1[:, :, :], m2[:, :, :], ALU.add))
                nc.vector.tensor_copy(mb[:, :, :], msum[:, :, :]).then_inc(d_mb, 1)

            def place(j, cc):
                c = 2 * j + cc
                ch = Chain(dve, d_sl, 6 * c)
                dve.wait_ge(pe_pos, c + 1)
                ch.link(nc.vector.tensor_tensor(tp[:, :, :], PB[:, 64:64 + CH * E].rearrange("p (k e) -> p k e", k=CH), ebase4, ALU.add))
                nc.vector.tensor_tensor(tm1[:, :, :], tp[:, :, :], m1[:, :, :], ALU.mult)
                ch.link(nc.vector.tensor_tensor(tm2[:, :, :], tp[:, :, :], m2[:, :, :], ALU.mult))
                nc.vector.tensor_reduce(slf[:, 0, :], tm1[:, :, :], AX.X, ALU.add)
                ch.link(nc.vector.tensor_reduce(slf[:, 1, :], tm2[:, :, :], AX.X, ALU.add))
                dve.wait_ge(scattered[cc], 16 + 128 * j)
                nc.vector.tensor_copy(xr[:, cc, :, :, D:D + 1].bitcast(U32), tok_sb[:, bass.ds(CH * c, CH), :].unsqueeze(3))
                ch.link(nc.vector.tensor_copy(slu[:, cc, :, :], slf[:, :, :].rearrange("p a k -> p k a")))
                ch.link(nc.vector.tensor_reduce(cs[:, :], msum[:, :, :].rearrange("p k e -> p e k"), AX.X, ALU.add))
                ch.link(nc.vector.tensor_tensor(carry[:, :], carry[:, :], cs[:, :], ALU.add))
                nc.vector.tensor_copy(cs[:, 0:1], carry[:, 0:1]).then_inc(d_slot, 1)

            def probabilities(j, cc):
                c = 2 * j + cc
                ch = Chain(dve, d_pr, 2 * c)
                dve.wait_ge(a_e, c + 1)
                ch.link(nc.vector.tensor_reduce(sume[:, :], ee[:, :, :], AX.X, ALU.add))
                ch.link(nc.vector.reciprocal(rsum[:, :], sume[:, :]))
                nc.vector.scalar_tensor_tensor(cg[:, bass.ds(CH * c, CH), :], ee[:, :, 0:2], tg[:, 1:2],
                                               rsum[:, :].unsqueeze(2).to_broadcast([128, CH, 2]), ALU.mult, ALU.mult).then_inc(d_cg, 1)

            nc.vector.memset(qz[:, :, :, :, :].bitcast(U32), 0).then_inc(d_zero, 1)
            nc.vector.memset(v9[:, :, :, :, :], 1.0).then_inc(d_zero, 1)
            nc.vector.memset(carry[:, :], 0.0).then_inc(d_zero, 1)
            dve.wait_ge(scattered[1], 16)
            dve.wait_ge(w_in, 16 * NWL)
            nc.vector.tensor_copy(identb, ident)
            nc.vector.tensor_copy(upperb, upper)
            nc.vector.tensor_copy(onesb, ones).then_inc(cast, 1)
            dve.wait_ge(d_zero, 3)
            dve.wait_ge(a_tg, 1)
            statistics(0, 0)
            rotate_q(0, 0)
            remainder(0, 0)
            values(0, 0)
            statistics(0, 1)
            for g in range(4):
                maximum(0, 0, g)
            split_maximum(0, 0)
            maximum_transposed(0, 0)

            def body(j):
                for u in range(8):
                    uu, cc = u % CH, u // CH
                    nj, ncc = (j, 1) if cc == 0 else (j + 1, 0)
                    pj, pcc = (j - 1, 1) if cc == 0 else (j, 0)
                    nxt, prv = later(j, u, 1), later(j, u, -1)
                    if uu == 0 and inside(j - 1, 4 * cc):
                        place(j - 1, cc)
                        probabilities(j - 1, cc)
                    if inside(*nxt):
                        maximum(*nxt, 0)
                        maximum(*nxt, 1)
                    if inside(*prv):
                        divide(*prv)
                    if inside(nj, 4 * ncc):
                        if uu == 0:
                            rotate_q(nj, ncc)
                        if uu == 1:
                            remainder(nj, ncc)
                        if uu == 2:
                            values(nj, ncc)
                    if inside(*nxt):
                        maximum(*nxt, 2)
                        maximum(*nxt, 3)
                        split_maximum(*nxt)
                    if inside(*prv):
                        add_attention(*prv)
                    if inside(*nxt):
                        maximum_transposed(*nxt)
                    if uu == 0 and inside(pj, 4 * pcc):
                        statistics2(pj, pcc)
                    if uu == 1 and inside(pj, 4 * pcc):
                        scales2(pj, pcc)
                    if uu == 2 and inside(j + 1, 4 * cc):
                        statistics(j + 1, cc)
                    if uu == 3 and inside(pj, 4 * pcc):
                        choose(pj, pcc)

            blocks(dve, body)
            J = B // 8 - 1
            place(J, 0)
            probabilities(J, 0)
            divide(J, 7)
            add_attention(J, 7)
            statistics2(J, 1)
            scales2(J, 1)
            choose(J, 1)
            place(J, 1)

            ch = Chain(dve, d_tc, 0)
            dve.wait_ge(pe_cnt, 1)
            ch.link(nc.vector.tensor_scalar(cnt_i[:, :], PB[0:E, 0:1], 127.0, None, ALU.add))
            ch.link(nc.vector.tensor_scalar(nt_i[:, :], cnt_i[:, :], 7, None, ALU.arith_shift_right))
            nc.vector.tensor_tensor(padrow[:, :], PB[0:1, 8:8 + E], ebase4[0:1, 0, :], ALU.add)
            nc.vector.tensor_copy(ntf[:, :], nt_i[:, :]).then_inc(d_nt, 1)
            dve.wait_ge(pe_ts, 1)
            ch.link(nc.vector.tensor_copy(tsf[:, :], PB[0:E, 16:17]))
            nc.vector.scalar_tensor_tensor(tc[:, :], tsf[:, :], -128.0, exp_row, ALU.mult, ALU.add)
            ch.link(nc.vector.tensor_tensor(tef[:, :], tsf[:, :], ntf[:, :], ALU.add))
            ch.link(nc.vector.tensor_scalar(s1[:, :], tile_no, tsf[:, 0:1], None, ALU.is_ge))
            ch.link(nc.vector.scalar_tensor_tensor(sel[:, :], tile_no, tef[:, 0:1], s1[:, :], ALU.is_lt, ALU.mult))
            nc.vector.scalar_tensor_tensor(tabv[:, 0, :], tile_row, tc[:, 0:1], sel[:, :], ALU.add, ALU.mult)
            nc.vector.tensor_scalar(tabv[:, 1, :], sel[:, :], exp_no, None, ALU.mult).then_inc(d_ts, 1)
            dve.wait_ge(pe_tab, 1)
            nc.vector.tensor_scalar(tab[:, 0, :], PB[0:1, 32:32 + NT], float(TRASH), None, ALU.add)
            nc.vector.tensor_copy(tab[:, 1, :], PB[0:1, 32 + NT:32 + 2 * NT]).then_inc(d_tab, 1)
            probabilities(J, 1)

            def result_rows(q, r):
                t = 4 * q + r
                dve.wait_ge(tile_in[r], 16 * (q + 1))
                if counts(16 * q):
                    dve.wait_ge(sent[r], 16 * q)
                nc.vector.tensor_copy(yi[:, r:r + 1], xs[:, r, D:D + 1].bitcast(U32)).then_inc(fd_i, 1)

            def hidden(q, r):
                t = 4 * q + r
                dve.wait_ge(fa_g, t + 1)
                dve.wait_ge(f_up, 2 * t + 2)
                if counts(t - 1):
                    dve.wait_ge(f_hT, t - 1)
                nc.vector.tensor_tensor(hh[:, r % 2, :], sg[:, r % 2, :], bank[2 * (r % 2) + 1][:, 0:H], ALU.mult)\
                    .then_inc(fd_h, 1)

            def hidden_down(q, r):
                t = 4 * q + r
                dve.wait_ge(f_hT, t + 1)
                if counts(t - 1):
                    dve.wait_ge(f_y, t - 1)
                nfull = H // 128 * 128
                nc.vector.tensor_copy(hT[:, r % 2, 0:nfull], bank[5][:, 0:nfull])
                nc.vector.tensor_copy(hT[0:H - nfull, r % 2, nfull:nfull + 128], bank[5][0:H - nfull, nfull:nfull + 128])\
                    .then_inc(fd_hT, 1)

            for r in range(3):
                result_rows(0, r)
            for r in range(2):
                hidden(0, r)

            def body(q):
                for r in range(4):
                    hidden_down(q, r)
                    if is_tile(*tile_after(q, r, 3)):
                        result_rows(*tile_after(q, r, 3))
                    if is_tile(*tile_after(q, r, 2)):
                        hidden(*tile_after(q, r, 2))

            body(0)
            with dve.Fori(1, NT // 4 - 1) as q:
                body(q)
            body(NT // 4 - 1)

            dve.wait_ge(a_base, NCH)
            for c in range(NCH):
                dve.wait_ge(back_in[c % 2], 16 * (c // 2 + 1))
                for k in range(CH):
                    b = CH * c + k
                    last = nc.vector.scalar_tensor_tensor(x_sb[:, b, :], yl[:, c % 2, k, 0, :], cg[:, b, 0:1], x_sb[:, b, :],
                                                          ALU.mult, ALU.add)
                last.then_inc(d_o1, 1)
                dve.wait_ge(d_o1, c + 1)
                for k in range(CH):
                    b = CH * c + k
                    last = nc.vector.scalar_tensor_tensor(x_sb[:, b, :], yl[:, c % 2, k, 1, :], cg[:, b, 1:2], x_sb[:, b, :],
                                                          ALU.mult, ALU.add)
                last.then_inc(d_o, 1)

        @block.tensor
        def _(pe):
            mm = nc.tensor.matmul

            def transposes(j, cc):
                c = 2 * j + cc
                pe.wait_ge(a_xh, c + 1)
                if counts(c - 2):
                    pe.wait_ge(a_nT, c - 2)
                for k in range(CH):
                    last = nc.tensor.transpose(PA[:, k * S:(k + 1) * S], xh[:, k, :], ident)
                last.then_inc(pe_xT, 1)
                pe.wait_ge(chunk_in[cc], 32 * (j + 1))
                if counts(c - 2):
                    pe.wait_ge(d_slot, c - 2)
                for k in range(CH):
                    last = nc.tensor.transpose(PB[:, k * S:(k + 1) * S], ctx_sb[:, cc, k, :], ident)
                last.then_inc(pe_xT, 1)

            def project_qk(j, cc):
                c = 2 * j + cc
                for t, ps, a, b_, ready in ((0, PA, qa, qb, d_q), (1, PB, ka, kb, p_k)):
                    pe.wait_ge(ready, c + 1)
                    mm(ps[:, :], wqk_sb[:, 2 * t, :], a[:, :], start=True, stop=False)
                    mm(ps[:, :], wqk_sb[:, 2 * t + 1, :], b_[:, :], start=False, stop=True).then_inc(pe_qk, 1)

            def project_v(j, cc):
                c = 2 * j + cc
                pe.wait_ge(d_r1, 2 * c + 1)
                for k in range(CH):
                    last = mm(PA[:, k * D:(k + 1) * D], cTs[:, k * S:(k + 1) * S], wv_sb[:, :], start=True, stop=True)
                last.then_inc(pe_v, 1)

            def scores(j, u, g):
                b, cc, t0 = 8 * j + u, u // CH, (u % CH) * S
                if g == 0 and u % CH == 0:
                    pe.wait_ge(stack_in[cc], 288 * (j + 1))
                if counts(4 * b + g - 1):
                    pe.wait_ge(d_max, 4 * b + g - 1)
                for k in range(4):
                    i, half = 2 * g + k // 2, k % 2
                    last = mm(SB[g % 2][:, k * S:(k + 1) * S], qz[0:ROWS, cc, i, half, t0:t0 + S],
                              kp[0:ROWS, cc, i, t0:t0 + S], start=True, stop=True)
                last.then_inc(pe_s, 1)

            def scores_by_key(j, u, g):
                b, cc, t0 = 8 * j + u, u // CH, (u % CH) * S
                if g == 0:
                    pe.wait_ge(m_in[u % 2], 16 * (4 * j + u // 2 + 1))
                if counts(4 * b + g - 1):
                    pe.wait_ge(a_exp, 4 * b + g - 1)
                for k in range(2):
                    i = 2 * g + k
                    last = mm(STB[g % 2][:, k * 2 * S:(k + 1) * 2 * S].rearrange("p (h s) -> p h s", h=2),
                              kp[0:ROWS + NMAX, cc, i, t0:t0 + S],
                              qz[0:ROWS + NMAX, cc, i, :, t0:t0 + S], start=True, stop=True)
                last.then_inc(pe_st, 1)

            def weighted_values(j, u, g):
                b = 8 * j + u
                pe.wait_ge(a_exp, 4 * b + g + 1)
                if g == 0:
                    pe.wait_ge(d_v, 2 * j + u // CH + 1)
                    if counts(b):
                        pe.wait_ge(d_on, b)
                for k in range(4):
                    h = 4 * g + k
                    last = mm(PVB[:, h * (DK + 1):(h + 1) * (DK + 1)], pt[:, h, :], v9[:, u // CH, u % CH, h, :],
                              start=True, stop=True)
                last.then_inc(pe_pv, 1)

            def transpose_maximum(j, u):
                b = 8 * j + u
                pe.wait_ge(d_m, b + 1)
                if counts(b - 1):
                    pe.wait_ge(d_x1, b - 1)
                nc.tensor.transpose(mT_ps, mh[:, :], identb).then_inc(pe_mT, 1)

            def transpose_attended(j, u):
                b = 8 * j + u
                pe.wait_ge(d_on, b + 1)
                pe.wait_ge(d_mT, min(b + 2, B) if isinstance(b, int) else b + 2)
                nc.tensor.transpose(SMALL[:, 0:D], on[:, :], ident).then_inc(pe_aT, 1)

            def project_out(j, u):
                b = 8 * j + u
                pe.wait_ge(a_aT, b + 1)
                mm(SMALL[:, D:2 * D], onT[:, :], wo_sb[:, :], start=True, stop=True).then_inc(pe_o, 1)

            def transpose_rows(j, cc):
                c = 2 * j + cc
                pe.wait_ge(a_xn, c + 1)
                pe.wait_ge(d_v, min(c + 3, NCH) if isinstance(c, int) else c + 3)
                for k in range(CH):
                    last = nc.tensor.transpose(PA[:, k * S:(k + 1) * S], xr[:, cc, k, 0, 0:D], ident)
                last.then_inc(pe_nT, 1)

            def router(j, cc):
                c = 2 * j + cc
                pe.wait_ge(a_nT, c + 1)
                pe.wait_ge(d_r1, min(2 * c + 6, 2 * NCH) if isinstance(c, int) else 2 * c + 6)
                for k in range(CH):
                    last = mm(PB[:, k * E:(k + 1) * E], nTs[:, k * S:(k + 1) * S], wr_sb[:, :], start=True, stop=True)
                last.then_inc(pe_r, 1)

            def positions(j, cc):
                c = 2 * j + cc
                pe.wait_ge(d_mb, c + 1)
                for k in range(CH):
                    dst = PB[:, 64 + k * E:64 + (k + 1) * E]
                    mm(dst, upperb, mb[:, k, :], start=True, stop=False)
                    for kk in range(k):
                        mm(dst, onesb, mb[:, kk, :], start=False, stop=False)
                    last = mm(dst, onesb, carry[:, :], start=False, stop=True)
                last.then_inc(pe_pos, 1)

            pe.wait_ge(w_in, 16 * NWL)
            pe.wait_ge(cast, 1)
            pe.wait_ge(d_zero, 3)
            pe.wait_ge(zeroed, 3)
            transposes(0, 0)
            project_qk(0, 0)
            project_v(0, 0)
            for g in range(4):
                scores(0, 0, g)
            transpose_maximum(0, 0)

            def body(j):
                for u in range(8):
                    uu, cc = u % CH, u // CH
                    nj, ncc = (j, 1) if cc == 0 else (j + 1, 0)
                    pj, pcc = (j - 1, 1) if cc == 0 else (j, 0)
                    nxt, prv = later(j, u, 1), later(j, u, -1)
                    if uu == 0 and inside(j - 1, 4 * cc):
                        positions(j - 1, cc)
                    if inside(*nxt):
                        scores(*nxt, 0)
                        scores(*nxt, 1)
                    if inside(*prv):
                        transpose_attended(*prv)
                    if inside(nj, 4 * ncc):
                        if uu == 0:
                            transposes(nj, ncc)
                        if uu == 1:
                            project_qk(nj, ncc)
                        if uu == 2:
                            project_v(nj, ncc)
                    if uu == 3 and inside(pj, 4 * pcc):
                        transpose_rows(pj, pcc)
                        router(pj, pcc)
                    if inside(*nxt):
                        scores(*nxt, 2)
                        scores(*nxt, 3)
                    if inside(*prv):
                        project_out(*prv)
                    scores_by_key(j, u, 0)
                    scores_by_key(j, u, 1)
                    if inside(*nxt):
                        transpose_maximum(*nxt)
                    weighted_values(j, u, 0)
                    scores_by_key(j, u, 2)
                    weighted_values(j, u, 1)
                    scores_by_key(j, u, 3)
                    weighted_values(j, u, 2)
                    weighted_values(j, u, 3)

            blocks(pe, body)
            J = B // 8 - 1
            positions(J, 0)
            transpose_attended(J, 7)
            project_out(J, 7)
            transpose_rows(J, 1)
            router(J, 1)
            positions(J, 1)

            pe.wait_ge(d_slot, NCH)
            mm(PB[0:E, 0:1], carry[:, :], onesb[:, 0:1], start=True, stop=True)
            mm(PB[0:1, 8:8 + E], onesb[:, 0:1], carry[:, :], start=True, stop=True).then_inc(pe_cnt, 1)
            pe.wait_ge(d_nt, 1)
            mm(PB[0:E, 16:17], upper[0:E, 0:E], ntf[:, :], start=True, stop=True).then_inc(pe_ts, 1)
            pe.wait_ge(d_ts, 1)
            mm(PB[0:1, 32:32 + 2 * NT], ones[0:E, 0:1], tabv[:, :, :].rearrange("p a t -> p (a t)"), start=True, stop=True)\
                .then_inc(pe_tab, 1)
            pe.wait_ge(d_tab, 1)
            pe.wait_ge(wf_in, 16 * (1 + HC))

            def expert_of(q, r):
                return pe.value_load(tab[0:1, 1, bass.ds(4 * q + r, 1)], min_val=0, max_val=E - 1)

            def transpose_tile(q, r):
                t = 4 * q + r
                pe.wait_ge(tile_in[r], 16 * (q + 1))
                if counts(t):
                    pe.wait_ge(fa_x, t)
                nc.tensor.transpose(bank[4][:, 0:128], xs[:, r, 0:D], ident).then_inc(f_x, 1)

            def up(q, r):
                t = 4 * q + r
                e = expert_of(q, r)
                pe.wait_ge(fa_x, t + 1)
                if counts(t - 1):
                    pe.wait_ge(fd_h, t - 1)
                mm(bank[2 * (r % 2)][:, 0:H], xT[:, r % 2, :], wup_sb[:, bass.ds(e * (2 * H) + H, H)], start=True, stop=True)\
                    .then_inc(f_up, 1)
                mm(bank[2 * (r % 2) + 1][:, 0:H], xT[:, r % 2, :], wup_sb[:, bass.ds(e * (2 * H), H)], start=True, stop=True)\
                    .then_inc(f_up, 1)

            def transpose_hidden(q, r):
                t = 4 * q + r
                pe.wait_ge(fd_h, t + 1)
                if counts(t):
                    pe.wait_ge(fd_hT, t)
                for n in range(HC):
                    w = min(128, H - 128 * n)
                    last = nc.tensor.transpose(bank[5][0:w, 128 * n:128 * n + 128], hh[:, r % 2, 128 * n:128 * n + w], ident)
                last.then_inc(f_hT, 1)

            def down(q, r):
                t = 4 * q + r
                e = expert_of(q, r)
                pe.wait_ge(fd_hT, t + 1)
                if counts(t - 1):
                    pe.wait_ge(fa_y, t - 1)
                for n in range(HC):
                    w = min(128, H - 128 * n)
                    last = mm(bank[6 + r % 2][:, 0:D], hT[0:w, r % 2, 128 * n:128 * n + 128], wdn_sb[0:w, n, bass.ds(e * D, D)],
                              start=(n == 0), stop=(n == HC - 1))
                last.then_inc(f_y, 1)

            for r in range(3):
                transpose_tile(0, r)
                if r:
                    up(0, r - 1)

            def body(q):
                for r in range(4):
                    transpose_hidden(q, r)
                    if is_tile(*tile_after(q, r, 3)):
                        transpose_tile(*tile_after(q, r, 3))
                    if is_tile(*tile_after(q, r, 2)):
                        up(*tile_after(q, r, 2))
                    down(q, r)

            body(0)
            with pe.Fori(1, NT // 4 - 1) as q:
                body(q)
            body(NT // 4 - 1)


def lay_out(inp):
    f = np.float32
    half = D // 2
    a = {k: np.asarray(v) for k, v in inp.items()}
    def stacked(w):
        return w.reshape(NI, 2, DK, -1).transpose(1, 2, 0, 3).reshape(NH * DK, -1)
    wq, wk = stacked(a["L0_xattn_Wq_w"]), stacked(a["L0_xattn_Wk_w"])
    wqk = np.stack([wq.T, np.roll(wq, half, axis=1).T, wk.T, np.roll(wk, half, axis=1).T], axis=1)
    bqk = np.concatenate([stacked(a["L0_xattn_Wq_b"]), stacked(a["L0_xattn_Wk_b"])], axis=1)
    pos = np.arange(1, S + 1, dtype=f)[:, None]
    theta = f(10000.0) ** (f(-2.0) * np.arange(half, dtype=f) / f(D))
    angle = pos * theta.astype(f)
    cos = np.repeat(np.cos(angle), 2, axis=1).T.astype(f)
    sin = np.repeat(np.sin(angle), 2, axis=1).T.astype(f)
    sin = np.concatenate([sin[half:], -sin[:half]])
    grid = np.arange(128)
    con = np.concatenate([
        np.eye(128, dtype=f), cos, sin, (grid[:, None] < grid[None, :]).astype(f), np.ones((128, 128), f),
        np.broadcast_to(np.tile(np.arange(E, dtype=f), CH), (128, CH * E)),
        np.broadcast_to(np.tile(np.arange(E, dtype=f) * f(CAP), CH), (128, CH * E)),
        grid[:, None].astype(f), (grid[:, None] * CAP - TRASH).astype(f),
        np.broadcast_to(np.arange(NT, dtype=f), (128, NT)),
        np.broadcast_to(np.arange(NT, dtype=f) * f(128), (128, NT))], axis=1)
    tok = (np.arange(B)[None, :, None] * S + grid[:, None, None]) * 2 + np.arange(2)[None, None, :]
    r = np.broadcast_to
    return dict(
        x=a["x"], ctx_in=a["ctx_1024"],
        gates=r(np.concatenate([a["g_xattn"], a["g_ffn"]])[None, :], (128, 2)), consts=con, wqk=wqk, bqk=bqk,
        wv=a["L0_xattn_Wv_w"].T, bvb=r(a["L0_xattn_Wv_b"][None, :], (128, D)),
        wo=a["L0_xattn_Wo_w"].T, bob=r(a["L0_xattn_Wo_b"][None, :], (128, D)),
        nscale=a["L0_ffn_norm_scale"][:, None], wr=a["L0_ffn_w_router"].T,
        wup=a["L0_ffn_w_up"].transpose(2, 0, 1).reshape(D, E * 2 * H),
        wdn=a["L0_ffn_w_down"].transpose(2, 0, 1).reshape(H, E * D),
        tokrow=tok.astype(np.uint32))


def kernel(**inputs):
    import concourse.bacc as bacc
    from concourse.bass_utils import run_bass_kernel_spmd

    nc = bacc.Bacc("TRN2", target_bir_lowering=False, num_devices=1)
    arrays, args = {}, {}
    for name, value in lay_out(inputs).items():
        value = np.ascontiguousarray(value)
        arrays[f"in_{name}"] = value
        args[name] = nc.dram_tensor(f"in_{name}", value.shape, mybir.dt.from_np(value.dtype), kind="ExternalInput").ap()
    args["out"] = nc.dram_tensor("out_0", (B, S, D), F32, kind="ExternalOutput").ap()
    flamingo(nc, **args)
    r = run_bass_kernel_spmd(nc, [arrays], core_ids=[0])
    return r.results[0]["out_0"]
```

```python
import concourse.bass as bass
import numpy as np
from concourse import mybir
from contextlib import ExitStack

F32 = mybir.dt.float32
BF16 = mybir.dt.bfloat16
U32 = mybir.dt.uint32
I32 = mybir.dt.int32
ALU = mybir.AluOpType
ACT = mybir.ActivationFunctionType
AX = mybir.AxisListType

B, S, D = 32, 128, 128
NH, DK = 16, 8
NI = NH // 2
E, H = 8, 352
CH = 4
NCH = B // CH
CT = CH * S
COMBO_Q = (0, 0, 0, 1, 1, 2)
COMBO_K = (0, 1, 2, 0, 1, 0)
ROWS = len(COMBO_Q) * 2 * DK
NMAX = 2
HC = -(-H // 128)
CAP = B * S + 128
TRASH = E * CAP
NT = -(-(2 * B * S + E * 127) // 128)
NT += -NT % 4
RW = 132
PAD_ROW = 2 * B * S
SCORE_SCALE = float(1.0 / np.sqrt(np.float32(DK)))


def counts(value):
    return not isinstance(value, int) or value > 0


def apart(eng, sem):
    eng.sem_inc(sem, 1)


class Chain:

    def __init__(self, eng, sem, base):
        self.eng, self.sem, self.base, self.n = eng, sem, base, 0

    def link(self, ins):
        self.n += 1
        ins.then_inc(self.sem, 1)
        self.eng.wait_ge(self.sem, self.base + self.n)


def later(j, u, k):
    return j + (u + k) // 8, (u + k) % 8


def inside(j, u):
    return not isinstance(j, int) or 0 <= 8 * j + u < B


def flamingo(nc, x, ctx_in, gates, consts, wqk, bqk, wv, bvb, wo, bob, nscale, wr, wup, wdn, tokrow, out):
    ctx = ExitStack()
    with ctx:
        def sb(name, shape, dt=F32):
            return ctx.enter_context(nc.sbuf_tensor(name, shape, dt))

        def sem(name):
            return ctx.enter_context(nc.semaphore(name))

        slots_dram = nc.dram_tensor("slots_dram", [TRASH + 128, RW], F32, kind="Internal").ap()
        result_dram = nc.dram_tensor("result_dram", [2 * B * S, D], F32, kind="Internal").ap()

        con = sb("con", [128, 5 * 128 + 64 + 2 + 2 * NT + 4 * (DK + 1)])
        ident, cosT, sinT = con[:, 0:128], con[:, 128:256], con[:, 256:384]
        upper, ones = con[:, 384:512], con[:, 512:640]
        iota4 = con[:, 640:672].rearrange("p (k e) -> p k e", k=CH)
        ebase4 = con[:, 672:704].rearrange("p (k e) -> p k e", k=CH)
        exp_no, exp_row = con[0:E, 704:705], con[0:E, 705:706]
        tile_no, tile_row = con[0:E, 706:706 + NT], con[0:E, 706 + NT:706 + 2 * NT]
        pick = con[:, 706 + 2 * NT:706 + 2 * NT + 4 * (DK + 1)]
        conb = sb("conb", [128, 3, 128], BF16)
        identb, upperb, onesb = conb[:, 0, :], conb[:, 1, :], conb[:, 2, :]
        wqk_sb = sb("wqk_sb", [128, 4, 128])
        bqk_sb = sb("bqk_sb", [128, 2])
        wv_sb, bv_sb = sb("wv_sb", [128, 128]), sb("bv_sb", [128, 128])
        wo_sb, bo_sb = sb("wo_sb", [128, 128]), sb("bo_sb", [128, 128])
        gate_sb = sb("gate_sb", [128, 2])
        ns_sb = sb("ns_sb", [128, 1])
        wr_sb = sb("wr_sb", [128, E])
        tok_sb = sb("tok_sb", [128, B, 2], U32)
        tg = sb("tg", [128, 2])
        mhalf = sb("mhalf", [128, CH])

        x_sb = sb("x_sb", [128, B, D])
        ctx_sb = sb("ctx_sb", [128, 2, CH, D])
        xh = sb("xh", [128, CH, D])
        xTs, cTs = sb("xTs", [128, CT]), sb("cTs", [128, CT])
        qa, qb, ka, kb = (sb(n, [128, CT]) for n in ("qa", "qb", "ka", "kb"))
        r1 = sb("r1", [128, 2, CT])
        parts = sb("parts", [128, 2, 3, CT], BF16)
        qz = sb("qz", [128, 2, NI, 2, CT], BF16)
        kp = sb("kp", [128, 2, NI, CT], BF16)
        v9 = sb("v9", [128, 2, CH, NH, DK + 1])
        nmx = sb("nmx", [128, NH])
        mh = sb("mh", [128, 2 * NH], BF16)
        mTs = sb("mTs", [2 * NH, 2, S], BF16)
        pt = sb("pt", [128, NH, S])
        oT = sb("oT", [128, NH // 4, S])
        rc = sb("rc", [128, NH])
        on, onT = sb("on", [128, D]), sb("onT", [128, D])
        st6, mv, ve, rs, nmr = (sb("st6", [128, CH, 6]), sb("mv", [128, CH, 2]), sb("ve", [128, CH]),
                                sb("rs", [128, CH]), sb("nmr", [128, CH]))
        st6b, mv2, ve2, rs2 = (sb("st6b", [128, CH, 6]), sb("mv2", [128, CH, 2]), sb("ve2", [128, CH]),
                               sb("rs2", [128, CH]))
        t1, t2, rr, sc2, nb2 = (sb(n, [128, CH]) for n in ("t1", "t2", "rr", "sc2", "nb2"))
        fscale, fbias = sb("fscale", [128, B]), sb("fbias", [128, B])
        cg = sb("cg", [128, B, 2])
        xr = sb("xr", [128, 2, CH, 2, RW])
        nTs = sb("nTs", [128, CT])
        sc, top = sb("sc", [128, CH, E]), sb("top", [128, CH, E])
        idx = sb("idx", [128, CH, E], U32)
        idxf = sb("idxf", [128, CH, 2])
        sub, ee = sb("sub", [128, CH, E]), sb("ee", [128, CH, E])
        m1, m2, msum = sb("m1", [128, CH, E]), sb("m2", [128, CH, E]), sb("msum", [128, CH, E])
        mb = sb("mb", [128, CH, E], BF16)
        carry = sb("carry", [128, E], BF16)
        cs = sb("cs", [128, E])
        tp, tm1, tm2 = (sb(n, [128, CH, E]) for n in ("tp", "tm1", "tm2"))
        slf = sb("slf", [128, 2, CH])
        slu = sb("slu", [128, 2, CH, 2], U32)
        sume, rsum = sb("sume", [128, CH]), sb("rsum", [128, CH])

        wup_sb = sb("wup_sb", [128, E * 2 * H])
        wdn_sb = sb("wdn_sb", [128, HC, E * D])
        cnt_i, nt_i = sb("cnt_i", [E, 1], I32), sb("nt_i", [E, 1], I32)
        ntf, tsf, tef, tc = (sb(n, [E, 1]) for n in ("ntf", "tsf", "tef", "tc"))
        s1, sel = sb("s1", [E, NT]), sb("sel", [E, NT])
        tabv = sb("tabv", [E, 2, NT])
        tab = sb("tab", [1, 2, NT], I32)
        padrow = sb("padrow", [1, E], I32)
        pad_sb = sb("pad_sb", [128, RW])
        xs = sb("xs", [128, 4, RW])
        xT = sb("xT", [128, 2, 128])
        sg, hh = sb("sg", [128, 2, H]), sb("hh", [128, 2, H])
        hT = sb("hT", [128, 2, HC * 128])
        ys = sb("ys", [128, 4, D])
        yi = sb("yi", [128, 4], U32)
        yl = sb("yl", [128, 2, CH, 2, D])

        bank = [ctx.enter_context(nc.psum_tensor(f"bank{i}", [128, 512], F32)) for i in range(8)]
        SB, STB, PVB, SMALL, PA, PB = bank[0:2], bank[2:4], bank[4], bank[5], bank[6], bank[7]
        heads_ps = SMALL[:, 320:320 + NH * (DK + 1)]
        mT_ps = SMALL[0:2 * NH, 256:320].bitcast(BF16)

        NWL = 10
        w_in, zeroed, cast = sem("w_in"), sem("zeroed"), sem("cast")
        chunk_in = [sem("chunk_in0"), sem("chunk_in1")]
        stack_in = [sem("stack_in0"), sem("stack_in1")]
        m_in = [sem("m_in0"), sem("m_in1")]
        scattered = [sem("scattered0"), sem("scattered1")]
        pe_s, pe_st, pe_pv, pe_mT, pe_aT, pe_o = map(sem, ("pe_s", "pe_st", "pe_pv", "pe_mT", "pe_aT", "pe_o"))
        pe_xT, pe_qk, pe_v, pe_nT, pe_r, pe_pos = map(sem, ("pe_xT", "pe_qk", "pe_v", "pe_nT", "pe_r", "pe_pos"))
        a_tg, a_xh, a_xT, a_hi, a_mid, a_exp, a_aT, a_xn, a_nT, a_e = map(
            sem, ("a_tg", "a_xh", "a_xT", "a_hi", "a_mid", "a_exp", "a_aT", "a_xn", "a_nT", "a_e"))
        d_max, d_mh, d_m, d_mT, d_rc, d_on, d_x1, d_q, d_r1, d_v = map(
            sem, ("d_max", "d_mh", "d_m", "d_mT", "d_rc", "d_on", "d_x1", "d_q", "d_r1", "d_v"))
        d_stat, d_ve, d_rs, d_stat2, d_ve2, d_t2, d_sc2, d_rt, d_top, d_m12, d_slot, d_sl, d_pr = map(
            sem, ("d_stat", "d_ve", "d_rs", "d_stat2", "d_ve2", "d_t2", "d_sc2", "d_rt", "d_top", "d_m12",
                  "d_slot", "d_sl", "d_pr"))
        a_oT, pe_heads, d_bn, d_sc, d_tp = map(sem, ("a_oT", "pe_heads", "d_bn", "d_sc", "d_tp"))
        p_gbo, p_rs, p_k, p_lo, p_xb, p_rs2, p_rr = map(
            sem, ("p_gbo", "p_rs", "p_k", "p_lo", "p_xb", "p_rs2", "p_rr"))
        d_mb, d_cg, d_zero, a_base = map(sem, ('d_mb', 'd_cg', 'd_zero', 'a_base'))
        out_sem, d_apart, p_apart, s_apart = map(sem, ("out_sem", "d_apart", "p_apart", "s_apart"))
        wf_in, padded = sem("wf_in"), sem("padded")
        pe_cnt, pe_ts, pe_tab, d_nt, d_ts, d_tab, d_tc = map(
            sem, ("pe_cnt", "pe_ts", "pe_tab", "d_nt", "d_ts", "d_tab", "d_tc"))
        tile_in = [sem(f"tile_in{r}") for r in range(4)]
        sent = [sem(f"sent{r}") for r in range(4)]
        f_x, f_up, f_hT, f_y = map(sem, ("f_x", "f_up", "f_hT", "f_y"))
        fa_x, fa_g, fa_y, fd_i, fd_h, fd_hT = map(sem, ("fa_x", "fa_g", "fa_y", "fd_i", "fd_h", "fd_hT"))
        back_in = [sem("back_in0"), sem("back_in1")]
        d_o, d_o1 = sem("d_o"), sem("d_o1")

        def tile_after(q, r, k):
            return q + (r + k) // 4, (r + k) % 4

        def is_tile(q, r):
            return not isinstance(q, int) or 4 * q + r < NT

        def blocks(eng, body):
            body(0)
            with eng.Fori(1, B // 8 - 1) as j:
                body(j)
            body(B // 8 - 1)

        block = ctx.enter_context(nc.Block())

        @block.sync
        def _(sp):
            def load(j, cc):
                c = 2 * j + cc
                if counts(2 * c - 2):
                    sp.wait_ge(pe_xT, 2 * c - 2)
                sp.dma_start(x_sb[:, bass.ds(CH * c, CH), :], x[bass.ds(CH * c, CH), :, :].rearrange("b s d -> s b d"))\
                    .then_inc(chunk_in[cc], 16)
                sp.dma_start(ctx_sb[:, cc, :, :], ctx_in[bass.ds(CH * c, CH), :, :].rearrange("b s d -> s b d"))\
                    .then_inc(chunk_in[cc], 16)

            def stack_q(cc, combos):
                for n in combos:
                    for half in range(2):
                        row = n * 2 * DK + half * DK
                        sp.dma_start(qz[row:row + DK, cc, :, half, :],
                                     parts[half * 64:half * 64 + 64, 0, COMBO_Q[n], :]).then_inc(stack_in[cc], 16)

            def stack_k(cc, combos):
                for n in combos:
                    sp.dma_start(kp[n * 2 * DK:(n + 1) * 2 * DK, cc, :, :],
                                 parts[:, 1, COMBO_K[n], :]).then_inc(stack_in[cc], 16)

            def stack_first(j, cc):
                c = 2 * j + cc
                if counts(16 * (c - 1)):
                    sp.wait_ge(pe_st, 16 * (c - 1))
                apart(sp, s_apart)
                sp.wait_ge(a_hi, 2 * c + 1)
                stack_q(cc, (0, 1, 2))

            def stack_second(j, cc):
                c = 2 * j + cc
                sp.wait_ge(a_mid, 2 * c + 1)
                stack_q(cc, (3, 4))

            def stack_third(j, cc):
                c = 2 * j + cc
                sp.wait_ge(p_lo, 2 * c + 1)
                stack_q(cc, (5,))
                sp.wait_ge(a_hi, 2 * c + 2)
                stack_k(cc, (0, 3, 5))

            def stack_fourth(j, cc):
                c = 2 * j + cc
                sp.wait_ge(a_mid, 2 * c + 2)
                stack_k(cc, (1, 4))
                sp.wait_ge(p_lo, 2 * c + 2)
                stack_k(cc, (2,))

            def maxima(j, u):
                sp.wait_ge(d_mT, 8 * j + u + 1)
                t0 = (u % CH) * S
                sp.dma_start(qz[ROWS:ROWS + NMAX, u // CH, :, :, t0:t0 + S].rearrange("r i h t -> r (i h) t"),
                             mTs[:, u % 2, :]).then_inc(m_in[u % 2], 16)

            def store(c):
                sp.wait_ge(d_o, c + 1)
                sp.dma_start(out[CH * c:CH * (c + 1), :, :].rearrange("b s d -> s b d"), x_sb[:, CH * c:CH * (c + 1), :])\
                    .then_inc(out_sem, 16)

            for dst, src in ((con[:, :], consts), (wqk_sb[:, :, :], wqk), (bqk_sb[:, :], bqk), (wv_sb[:, :], wv),
                             (bv_sb[:, :], bvb), (wo_sb[:, :], wo), (bo_sb[:, :], bob), (gate_sb[:, :], gates),
                             (ns_sb[:, :], nscale), (wr_sb[:, :], wr)):
                sp.dma_start(dst, src).then_inc(w_in, 16)
            load(0, 0)
            load(0, 1)
            sp.wait_ge(d_zero, 4)
            sp.wait_ge(zeroed, 3)
            stack_first(0, 0)
            stack_second(0, 0)
            stack_third(0, 0)
            stack_fourth(0, 0)
            maxima(0, 0)

            sp.dma_start(wup_sb[:, :], wup).then_inc(wf_in, 16)
            for n in range(HC):
                rows_n = min(128, H - 128 * n)
                sp.dma_start(wdn_sb[0:rows_n, n, :], wdn[128 * n:128 * n + rows_n, :]).then_inc(wf_in, 16)

            def body(j):
                for u in range(8):
                    uu, cc = u % CH, u // CH
                    nj, ncc = (j, 1) if cc == 0 else (j + 1, 0)
                    if uu == 0 and inside(j + 1, 4 * cc):
                        load(j + 1, cc)
                    if uu == 0 and inside(nj, 4 * ncc):
                        stack_first(nj, ncc)
                    if uu == 1 and inside(nj, 4 * ncc):
                        stack_third(nj, ncc)
                    if inside(*later(j, u, 1)):
                        maxima(*later(j, u, 1))
                    if uu == 0 and inside(nj, 4 * ncc):
                        stack_second(nj, ncc)
                    if uu == 1 and inside(nj, 4 * ncc):
                        stack_fourth(nj, ncc)

            blocks(sp, body)
            sp.wait_ge(d_nt, 1)
            sp.wait_ge(zeroed, 5)
            for e in range(E):
                row = sp.value_load(padrow[0:1, e:e + 1], min_val=0, max_val=TRASH - 128)
                sp.dma_start(slots_dram[bass.ds(row, 128), :], pad_sb[:, :]).then_inc(padded, 16)
            sp.wait_ge(padded, 16 * E)
            sp.wait_ge(scattered[0], 16 + 128 * (B // 8))
            sp.wait_ge(scattered[1], 16 + 128 * (B // 8))
            sp.wait_ge(d_tab, 1)

            def body(q):
                for r in range(4):
                    t = 4 * q + r
                    row = sp.value_load(tab[0:1, 0, bass.ds(t, 1)], min_val=0, max_val=TRASH)
                    if counts(t - 3):
                        sp.wait_ge(f_x, t - 3)
                    if counts(t - 3):
                        sp.wait_ge(fd_i, t - 3)
                    sp.dma_start(xs[:, r, :], slots_dram[bass.ds(row, 128), :]).then_inc(tile_in[r], 16)

            body(0)
            with sp.Fori(1, NT // 4) as q:
                body(q)
            for r in range(4):
                sp.wait_ge(sent[r], 16 * (NT // 4))
            for c in range(NCH):
                if counts(c - 1):
                    sp.wait_ge(d_o, c - 1)
                sp.dma_start(yl[:, c % 2, :, :, :], result_dram[c * 2 * CT:(c + 1) * 2 * CT, :]
                             .rearrange("(b s k) d -> s b k d", s=S, k=2)).then_inc(back_in[c % 2], 16)
                if c > 0:
                    store(c - 1)
            store(NCH - 1)
            sp.wait_ge(out_sem, 16 * NCH)

        @block.gpsimd
        def _(pool):
            def power(j, cc):
                c = 2 * j + cc
                pool.wait_ge(d_ve, c + 1)
                if counts(c):
                    pool.wait_ge(a_xh, c)
                nc.gpsimd.tensor_tensor(rs[:, :], ve[:, :], mhalf[:, :], ALU.pow).then_inc(p_rs, 1)

            def rotate_k(j, cc):
                c = 2 * j + cc
                pool.wait_ge(a_xT, 2 * c + 2)
                if counts(2 * c):
                    pool.wait_ge(pe_qk, 2 * c)
                for dst, tab in ((ka, cosT), (kb, sinT)):
                    last = nc.gpsimd.tensor_tensor(dst[:, :].rearrange("p (k s) -> p k s", k=CH),
                                                   cTs[:, :].rearrange("p (k s) -> p k s", k=CH),
                                                   tab.unsqueeze(1).to_broadcast([128, CH, S]), ALU.mult)
                last.then_inc(p_k, 1)

            def low(j, cc, t):
                c = 2 * j + cc
                pool.wait_ge(a_mid, 2 * c + t + 1)
                nc.gpsimd.tensor_tensor(parts[:, t, 2, :], r1[:, t, :], parts[:, t, 1, :], ALU.subtract)\
                    .then_inc(p_lo, 1)

            def add_bias(j, cc):
                c = 2 * j + cc
                pool.wait_ge(a_xh, c + 1)
                nc.gpsimd.tensor_tensor(x_sb[:, bass.ds(CH * c, CH), :], x_sb[:, bass.ds(CH * c, CH), :],
                                        bo_sb[:, :].unsqueeze(1).to_broadcast([128, CH, D]), ALU.add).then_inc(p_xb, 1)

            def power2a(j, cc):
                c = 2 * j + cc
                pool.wait_ge(d_ve2, c + 1)
                nc.gpsimd.tensor_tensor(rs2[:, :], ve2[:, :], mhalf[:, :], ALU.pow).then_inc(p_rs2, 1)

            def power2b(j, cc):
                c = 2 * j + cc
                pool.wait_ge(d_t2, c + 1)
                nc.gpsimd.tensor_tensor(rr[:, :], t2[:, :], mhalf[:, :], ALU.pow).then_inc(p_rr, 1)

            def scatter(j, cc, batches):
                c = 2 * j + cc
                pool.wait_ge(d_slot, c + 1)
                pool.wait_ge(a_xn, c + 1)
                apart(pool, p_apart)
                for k in batches:
                    for kk in range(2):
                        nc.gpsimd.indirect_dma_start(
                            out=slots_dram, out_offset=bass.IndirectOffsetOnAxis(ap=slu[:, cc, k, kk:kk + 1], axis=0),
                            in_=xr[:, cc, k, kk, :], in_offset=None).then_inc(scattered[cc], 16)

            nc.gpsimd.memset(kp[96:128, :, :, :], 1.0).then_inc(zeroed, 1)
            pool.wait_ge(zeroed, 1)
            nc.gpsimd.memset(xr[:, :, :, :, :], 0.0).then_inc(zeroed, 1)
            nc.gpsimd.memset(mhalf[:, :], -0.5).then_inc(zeroed, 1)
            nc.gpsimd.memset(pad_sb[:, :], 0.0).then_inc(zeroed, 1)
            pool.wait_ge(zeroed, 4)
            nc.gpsimd.memset(pad_sb[:, D:D + 1].bitcast(U32), PAD_ROW).then_inc(zeroed, 1)
            pool.wait_ge(zeroed, 5)
            pool.dma_start(slots_dram[TRASH:TRASH + 128, :], pad_sb[:, :]).then_inc(scattered[0], 16)
            pool.dma_start(tok_sb[:, :, :], tokrow).then_inc(scattered[1], 16)
            pool.wait_ge(w_in, 16 * NWL)
            pool.wait_ge(a_tg, 1)
            nc.gpsimd.tensor_scalar(bo_sb[:, :], bo_sb[:, :], tg[:, 0:1], None, ALU.mult).then_inc(p_gbo, 1)
            pool.wait_ge(p_gbo, 1)
            pool.wait_ge(zeroed, 3)
            power(0, 0)
            rotate_k(0, 0)
            power(0, 1)
            low(0, 0, 0)
            low(0, 0, 1)
            rotate_k(0, 1)
            add_bias(0, 0)
            add_bias(0, 1)

            def body(j):
                for u in range(8):
                    uu, cc = u % CH, u // CH
                    nj, ncc = (j, 1) if cc == 0 else (j + 1, 0)
                    pj, pcc = (j - 1, 1) if cc == 0 else (j, 0)
                    has_next, has_after = inside(nj, 4 * ncc), inside(j + 1, 4 * cc)
                    has_last, has_before = inside(pj, 4 * pcc), inside(j - 1, 4 * cc)
                    if uu == 0:
                        if has_next:
                            low(nj, ncc, 0)
                        if has_last:
                            power2a(pj, pcc)
                    if uu == 1:
                        if has_before:
                            scatter(j - 1, cc, (0, 1))
                        if has_next:
                            low(nj, ncc, 1)
                        if has_last:
                            power2b(pj, pcc)
                    if uu == 2:
                        if has_before:
                            scatter(j - 1, cc, (2, 3))
                        if has_after:
                            power(j + 1, cc)
                    if uu == 3 and has_after:
                        add_bias(j + 1, cc)
                        rotate_k(j + 1, cc)

            blocks(pool, body)
            J = B // 8 - 1
            power2a(J, 1)
            power2b(J, 1)
            scatter(J, 0, range(CH))
            scatter(J, 1, range(CH))

            def send(q):
                for r in range(4):
                    pool.wait_ge(fa_y, 4 * q + r + 1)
                    apart(pool, p_apart)
                    nc.gpsimd.indirect_dma_start(
                        out=result_dram, out_offset=bass.IndirectOffsetOnAxis(ap=yi[:, r:r + 1], axis=0),
                        in_=ys[:, r, :], in_offset=None, bounds_check=PAD_ROW - 1, oob_is_err=False)\
                        .then_inc(sent[r], 16)

            with pool.Fori(0, NT // 4) as q:
                send(q)

        @block.scalar
        def _(act):
            def normalise(j, cc):
                c = 2 * j + cc
                act.wait_ge(d_rs, c + 1)
                if counts(2 * c - 1):
                    act.wait_ge(pe_xT, 2 * c - 1)
                for k in range(CH):
                    last = nc.scalar.activation(xh[:, k, :], x_sb[:, bass.ds(CH * c + k, 1), :], ACT.Identity,
                                                bias=nmr[:, k:k + 1], scale=rs[:, k:k + 1])
                last.then_inc(a_xh, 1)

            def transposed(j, cc):
                c = 2 * j + cc
                act.wait_ge(pe_xT, 2 * c + 1)
                if counts(c):
                    act.wait_ge(d_q, c)
                nc.scalar.activation(xTs[:, :], PA[:, :], ACT.Copy).then_inc(a_xT, 1)
                act.wait_ge(pe_xT, 2 * c + 2)
                if counts(c):
                    act.wait_ge(p_k, c)
                if counts(c):
                    act.wait_ge(pe_v, c)
                nc.scalar.activation(cTs[:, :], PB[:, :], ACT.Copy).then_inc(a_xT, 1)

            def high(j, cc, t):
                c = 2 * j + cc
                if t == 0:
                    if counts(288 * (j + cc)):
                        act.wait_ge(stack_in[1 - cc], 288 * (j + cc))
                act.wait_ge(pe_qk, 2 * c + t + 1)
                nc.scalar.activation(parts[:, t, 0, :], (PA, PB)[t][:, :], ACT.Identity, bias=bqk_sb[:, t:t + 1])\
                    .then_inc(a_hi, 1)

            def middle(j, cc, t):
                c = 2 * j + cc
                act.wait_ge(d_r1, 2 * c + t + 1)
                nc.scalar.activation(parts[:, t, 1, :], r1[:, t, :], ACT.Copy).then_inc(a_mid, 1)

            def exponent(j, u, g):
                b = 8 * j + u
                act.wait_ge(pe_st, 4 * b + g + 1)
                if counts(4 * (b - 1) + g + 1):
                    act.wait_ge(pe_pv, 4 * (b - 1) + g + 1)
                nc.scalar.activation(pt[:, 4 * g:4 * g + 4, :], STB[g % 2][:, :].rearrange("p (h s) -> p h s", h=4),
                                     ACT.Exp, scale=SCORE_SCALE).then_inc(a_exp, 1)

            def heads_out(j, u):
                b = 8 * j + u
                act.wait_ge(pe_pv, 4 * b + 4)
                if counts(b):
                    act.wait_ge(pe_heads, b)
                nc.scalar.activation(oT[:, :, :].rearrange("p g s -> p (g s)"), PVB[:, :], ACT.Copy).then_inc(a_oT, 1)

            def attended(j, u):
                b = 8 * j + u
                act.wait_ge(pe_aT, b + 1)
                if counts(b):
                    act.wait_ge(pe_o, b)
                nc.scalar.activation(onT[:, :], SMALL[:, 0:D], ACT.Copy).then_inc(a_aT, 1)

            def rows(j, cc):
                c = 2 * j + cc
                act.wait_ge(d_sc2, c + 1)
                act.wait_ge(scattered[cc], 16 + 128 * j)
                for k in range(CH):
                    last = nc.scalar.activation(xr[:, cc, k, :, 0:D], x_sb[:, bass.ds(CH * c + k, 1), :].to_broadcast([128, 2, D]),
                                                ACT.Identity, bias=nb2[:, k:k + 1], scale=sc2[:, k:k + 1])
                last.then_inc(a_xn, 1)

            def rows_transposed(j, cc):
                c = 2 * j + cc
                act.wait_ge(pe_nT, c + 1)
                if counts(c):
                    act.wait_ge(pe_r, c)
                nc.scalar.activation(nTs[:, :], PA[:, :], ACT.Identity, scale=ns_sb[:, 0:1]).then_inc(a_nT, 1)

            def expert_exp(j, cc):
                act.wait_ge(d_top, 2 * j + cc + 1)
                nc.scalar.activation(ee[:, :, :], sub[:, :, :], ACT.Exp).then_inc(a_e, 1)

            act.wait_ge(w_in, 16 * NWL)
            act.wait_ge(zeroed, 3)
            nc.scalar.activation(tg[:, :], gate_sb[:, :], ACT.Tanh).then_inc(a_tg, 1)
            normalise(0, 0)
            transposed(0, 0)
            high(0, 0, 0)
            high(0, 0, 1)
            middle(0, 0, 0)
            middle(0, 0, 1)
            normalise(0, 1)
            transposed(0, 1)

            def body(j):
                for u in range(8):
                    uu, cc = u % CH, u // CH
                    nj, ncc = (j, 1) if cc == 0 else (j + 1, 0)
                    pj, pcc = (j - 1, 1) if cc == 0 else (j, 0)
                    has_next, has_after = inside(nj, 4 * ncc), inside(j + 1, 4 * cc)
                    has_last, has_before = inside(pj, 4 * pcc), inside(j - 1, 4 * cc)
                    prv = later(j, u, -1)
                    if uu == 1 and has_next:
                        high(nj, ncc, 1)
                    if inside(*prv):
                        heads_out(*prv)
                    if uu == 0 and has_before:
                        expert_exp(j - 1, cc)
                    if uu == 0 and has_next:
                        high(nj, ncc, 0)
                    if uu == 2 and has_last:
                        rows(pj, pcc)
                    if uu == 3 and has_after:
                        normalise(j + 1, cc)
                    exponent(j, u, 0)
                    if inside(*prv):
                        attended(*prv)
                    exponent(j, u, 1)
                    if uu == 1 and has_next:
                        middle(nj, ncc, 1)
                    if uu == 2 and has_last:
                        rows_transposed(pj, pcc)
                    if uu == 3 and has_after:
                        transposed(j + 1, cc)
                    exponent(j, u, 2)
                    exponent(j, u, 3)
                    if uu == 0 and has_next:
                        middle(nj, ncc, 0)

            blocks(act, body)
            J = B // 8 - 1
            heads_out(J, 7)
            attended(J, 7)
            expert_exp(J, 0)
            rows(J, 1)
            rows_transposed(J, 1)
            expert_exp(J, 1)

            def base(b):
                nc.scalar.activation(x_sb[:, bass.ds(b, 1), :], x_sb[:, bass.ds(b, 1), :], ACT.Identity,
                                     bias=fbias[:, bass.ds(b, 1)], scale=fscale[:, bass.ds(b, 1)]).then_inc(a_base, 1)

            def rows_up(q, r):
                t = 4 * q + r
                act.wait_ge(f_x, t + 1)
                if counts(2 * (t - 1)):
                    act.wait_ge(f_up, 2 * (t - 1))
                nc.scalar.activation(xT[:, r % 2, :], bank[4][:, 0:128], ACT.Identity, scale=ns_sb[:, 0:1])\
                    .then_inc(fa_x, 1)

            def gate(q, r):
                t = 4 * q + r
                act.wait_ge(f_up, 2 * t + 1)
                if counts(t - 1):
                    act.wait_ge(fd_h, t - 1)
                nc.scalar.activation(sg[:, r % 2, :], bank[2 * (r % 2)][:, 0:H], ACT.Silu).then_inc(fa_g, 1)

            def result(q, r):
                t = 4 * q + r
                act.wait_ge(f_y, t + 1)
                if counts(16 * q):
                    act.wait_ge(sent[r], 16 * q)
                nc.scalar.activation(ys[:, r, :], bank[6 + r % 2][:, 0:D], ACT.Copy).then_inc(fa_y, 1)

            for r in range(3):
                rows_up(0, r)
                if r:
                    gate(0, r - 1)

            def body(q):
                for r in range(4):
                    if is_tile(*tile_after(q, r, 3)):
                        rows_up(*tile_after(q, r, 3))
                    if is_tile(*tile_after(q, r, 2)):
                        gate(*tile_after(q, r, 2))
                    result(q, r)

            body(0)
            with act.Fori(1, NT // 4 - 1) as q:
                body(q)
                base(2 * q - 2)
                base(2 * q - 1)
            body(NT // 4 - 1)

        @block.vector
        def _(dve):
            def statistics(j, cc):
                c = 2 * j + cc
                dve.wait_ge(chunk_in[cc], 32 * (j + 1))
                ch = Chain(dve, d_stat, 2 * c)
                for k in range(CH):
                    last = nc.vector.bn_stats(st6[:, k, :], x_sb[:, bass.ds(CH * c + k, 1), :])
                ch.link(last)
                if counts(c):
                    dve.wait_ge(a_xh, c)
                apart(dve, d_apart)
                for k in range(CH):
                    last = nc.vector.bn_aggr(mv[:, k, :], st6[:, k, :])
                ch.link(last)
                nc.vector.tensor_scalar(ve[:, :], mv[:, :, 1], 1e-5, None, ALU.add).then_inc(d_ve, 1)

            def shift(j, cc):
                c = 2 * j + cc
                dve.wait_ge(p_rs, c + 1)
                nc.vector.scalar_tensor_tensor(nmr[:, :], mv[:, :, 0], -1.0, rs[:, :], ALU.mult, ALU.mult)\
                    .then_inc(d_rs, 1)

            def rotate_q(j, cc):
                c = 2 * j + cc
                dve.wait_ge(a_xT, 2 * c + 1)
                if counts(2 * c - 1):
                    dve.wait_ge(pe_qk, 2 * c - 1)
                for dst, tab in ((qa, cosT), (qb, sinT)):
                    last = nc.vector.tensor_tensor(dst[:, :].rearrange("p (k s) -> p k s", k=CH),
                                                   xTs[:, :].rearrange("p (k s) -> p k s", k=CH),
                                                   tab.unsqueeze(1).to_broadcast([128, CH, S]), ALU.mult)
                last.then_inc(d_q, 1)

            def remainder(j, cc, t):
                c = 2 * j + cc
                dve.wait_ge(a_hi, 2 * c + t + 1)
                if counts(2 * c - 1 + t):
                    dve.wait_ge(p_lo, 2 * c - 1 + t)
                nc.vector.scalar_tensor_tensor(r1[:, t, :], (PA, PB)[t][:, :], bqk_sb[:, t:t + 1], parts[:, t, 0, :],
                                               ALU.add, ALU.subtract).then_inc(d_r1, 1)

            def values(j, cc):
                c = 2 * j + cc
                dve.wait_ge(pe_v, c + 1)
                if counts(16 * (c - 1)):
                    dve.wait_ge(pe_pv, 16 * (c - 1))
                nc.vector.tensor_tensor(v9[:, cc, :, :, 0:DK],
                                        PA[:, :].rearrange("p (k h d) -> p k h d", k=CH, h=NH),
                                        bv_sb[:, :].rearrange("p (h d) -> p h d", h=NH).unsqueeze(1)
                                        .to_broadcast([128, CH, NH, DK]), ALU.add).then_inc(d_v, 1)

            def maximum(j, u, g):
                b = 8 * j + u
                dve.wait_ge(pe_s, 4 * b + g + 1)
                if g == 0:
                    if counts(b):
                        dve.wait_ge(d_m, b)
                nc.vector.tensor_reduce(nmx[:, 4 * g:4 * g + 4], SB[g % 2][:, :].rearrange("p (h s) -> p h s", h=4),
                                        AX.X, ALU.max, negate=True).then_inc(d_max, 1)

            def split_maximum(j, u):
                b = 8 * j + u
                dve.wait_ge(d_max, 4 * b + 4)
                if counts(b):
                    dve.wait_ge(pe_mT, b)
                nc.vector.tensor_copy(mh[:, 0:NH], nmx[:, :]).then_inc(d_mh, 1)
                dve.wait_ge(d_mh, b + 1)
                nc.vector.tensor_tensor(mh[:, NH:2 * NH], nmx[:, :], mh[:, 0:NH], ALU.subtract).then_inc(d_m, 1)

            def maximum_transposed(j, u):
                b = 8 * j + u
                dve.wait_ge(pe_mT, b + 1)
                if counts(16 * (4 * j + u // 2)):
                    dve.wait_ge(m_in[u % 2], 16 * (4 * j + u // 2))
                nc.vector.tensor_copy(mTs[:, u % 2, :], mT_ps).then_inc(d_mT, 1)

            def divide(j, u):
                b = 8 * j + u
                dve.wait_ge(pe_heads, b + 1)
                pv = heads_ps.rearrange("p (h d) -> p h d", h=NH)
                nc.vector.reciprocal(rc[:, :], pv[:, :, DK]).then_inc(d_rc, 1)
                dve.wait_ge(d_rc, b + 1)
                if counts(b):
                    dve.wait_ge(pe_aT, b)
                nc.vector.tensor_tensor(on[:, :].rearrange("p (h d) -> p h d", h=NH), pv[:, :, 0:DK],
                                        rc[:, :].unsqueeze(2).to_broadcast([128, NH, DK]), ALU.mult).then_inc(d_on, 1)

            def add_attention(j, u):
                b = 8 * j + u
                dve.wait_ge(pe_o, b + 1)
                dve.wait_ge(p_xb, 2 * j + u // CH + 1)
                nc.vector.scalar_tensor_tensor(x_sb[:, bass.ds(b, 1), :].rearrange("p b d -> p (b d)"), SMALL[:, D:2 * D], tg[:, 0:1], x_sb[:, bass.ds(b, 1), :].rearrange("p b d -> p (b d)"),
                                               ALU.mult, ALU.add).then_inc(d_x1, 1)

            def statistics1(j, u):
                b = 8 * j + u
                dve.wait_ge(d_x1, b + 1)
                apart(dve, d_apart)
                nc.vector.bn_stats(st6b[:, u % CH, :], x_sb[:, bass.ds(b, 1), :]).then_inc(d_bn, 1)

            def statistics2(j, cc):
                c = 2 * j + cc
                dve.wait_ge(d_bn, CH * (c + 1))
                apart(dve, d_apart)
                for k in range(CH):
                    last = nc.vector.bn_aggr(mv2[:, k, :], st6b[:, k, :])
                last.then_inc(d_stat2, 1)
                dve.wait_ge(d_stat2, c + 1)
                nc.vector.tensor_scalar(ve2[:, :], mv2[:, :, 1], 1e-5, None, ALU.add).then_inc(d_ve2, 1)

            def scales2(j, cc):
                c = 2 * j + cc
                ch = Chain(dve, d_rt, 6 * c)
                if counts(c):
                    dve.wait_ge(a_xn, c)
                apart(dve, d_apart)
                dve.wait_ge(p_rs2, c + 1)
                ch.link(nc.vector.tensor_tensor(t1[:, :], mv2[:, :, 1], rs2[:, :], ALU.mult))
                ch.link(nc.vector.tensor_tensor(t1[:, :], t1[:, :], rs2[:, :], ALU.mult))
                nc.vector.tensor_scalar(t2[:, :], t1[:, :], 1e-6, None, ALU.add).then_inc(d_t2, 1)
                fs, fb = fscale[:, bass.ds(CH * c, CH)], fbias[:, bass.ds(CH * c, CH)]
                nc.vector.tensor_scalar(fs, rs2[:, :], tg[:, 1:2], 1.0, ALU.mult, ALU.add)
                ch.link(nc.vector.scalar_tensor_tensor(nb2[:, :], mv2[:, :, 0], -1.0, rs2[:, :], ALU.mult, ALU.mult))
                ch.link(nc.vector.tensor_scalar(fb, nb2[:, :], tg[:, 1:2], None, ALU.mult))
                dve.wait_ge(p_rr, c + 1)
                ch.link(nc.vector.tensor_tensor(nb2[:, :], nb2[:, :], rr[:, :], ALU.mult))
                ch.link(nc.vector.tensor_tensor(sc2[:, :], rs2[:, :], rr[:, :], ALU.mult))
                nc.vector.tensor_copy(t1[:, 0:1], sc2[:, 0:1]).then_inc(d_sc2, 1)

            def take_scores(j, cc):
                c = 2 * j + cc
                dve.wait_ge(pe_r, c + 1)
                if counts(c):
                    dve.wait_ge(a_e, c)
                nc.vector.tensor_copy(sc[:, :, :], SB[1][:, 0:CH * E].rearrange("p (k e) -> p k e", k=CH)).then_inc(d_sc, 1)

            def choose(j, cc):
                c = 2 * j + cc
                ch = Chain(dve, d_m12, 4 * c)
                if counts(c):
                    dve.wait_ge(pe_pos, c)
                apart(dve, d_apart)
                dve.wait_ge(d_sc, c + 1)
                apart(dve, d_apart)
                for k in range(CH):
                    last = nc.vector.max(top[:, k, :], sc[:, k, :])
                ch.link(last)
                apart(dve, d_apart)
                for k in range(CH):
                    last = nc.vector.max_index(idx[:, k, :], top[:, k, :], sc[:, k, :])
                nc.vector.tensor_tensor(sub[:, :, :], top[:, :, :], top[:, :, 0:1].to_broadcast([128, CH, E]),
                                        ALU.subtract).then_inc(d_top, 1)
                dve.wait_ge(d_top, c + 1)
                ch.link(nc.vector.tensor_copy(idxf[:, :, :], idx[:, :, 0:2]))
                nc.vector.tensor_tensor(m1[:, :, :], iota4, idxf[:, :, 0:1].to_broadcast([128, CH, E]), ALU.is_equal)
                ch.link(nc.vector.tensor_tensor(m2[:, :, :], iota4, idxf[:, :, 1:2].to_broadcast([128, CH, E]), ALU.is_equal))
                ch.link(nc.vector.tensor_tensor(msum[:, :, :], m1[:, :, :], m2[:, :, :], ALU.add))
                nc.vector.tensor_copy(mb[:, :, :], msum[:, :, :]).then_inc(d_mb, 1)

            def take_positions(j, cc):
                c = 2 * j + cc
                dve.wait_ge(pe_pos, c + 1)
                nc.vector.tensor_tensor(tp[:, :, :], SB[1][:, 64:64 + CH * E].rearrange("p (k e) -> p k e", k=CH), ebase4,
                                        ALU.add).then_inc(d_tp, 1)

            def place(j, cc):
                c = 2 * j + cc
                ch = Chain(dve, d_sl, 5 * c)
                dve.wait_ge(d_tp, c + 1)
                nc.vector.tensor_tensor(tm1[:, :, :], tp[:, :, :], m1[:, :, :], ALU.mult)
                ch.link(nc.vector.tensor_tensor(tm2[:, :, :], tp[:, :, :], m2[:, :, :], ALU.mult))
                nc.vector.tensor_reduce(slf[:, 0, :], tm1[:, :, :], AX.X, ALU.add)
                ch.link(nc.vector.tensor_reduce(slf[:, 1, :], tm2[:, :, :], AX.X, ALU.add))
                dve.wait_ge(scattered[cc], 16 + 128 * j)
                nc.vector.tensor_copy(xr[:, cc, :, :, D:D + 1].bitcast(U32), tok_sb[:, bass.ds(CH * c, CH), :].unsqueeze(3))
                ch.link(nc.vector.tensor_copy(slu[:, cc, :, :], slf[:, :, :].rearrange("p a k -> p k a")))
                ch.link(nc.vector.tensor_reduce(cs[:, :], msum[:, :, :].rearrange("p k e -> p e k"), AX.X, ALU.add))
                ch.link(nc.vector.tensor_tensor(carry[:, :], carry[:, :], cs[:, :], ALU.add))
                nc.vector.tensor_copy(cs[:, 0:1], carry[:, 0:1]).then_inc(d_slot, 1)

            def probabilities(j, cc):
                c = 2 * j + cc
                ch = Chain(dve, d_pr, 2 * c)
                dve.wait_ge(a_e, c + 1)
                ch.link(nc.vector.tensor_reduce(sume[:, :], ee[:, :, :], AX.X, ALU.add))
                ch.link(nc.vector.reciprocal(rsum[:, :], sume[:, :]))
                nc.vector.scalar_tensor_tensor(cg[:, bass.ds(CH * c, CH), :], ee[:, :, 0:2], tg[:, 1:2],
                                               rsum[:, :].unsqueeze(2).to_broadcast([128, CH, 2]), ALU.mult, ALU.mult).then_inc(d_cg, 1)

            nc.vector.memset(qz[:, :, :, :, :].bitcast(U32), 0).then_inc(d_zero, 1)
            nc.vector.memset(v9[:, :, :, :, :], 1.0).then_inc(d_zero, 1)
            nc.vector.memset(carry[:, :], 0.0).then_inc(d_zero, 1)
            nc.vector.memset(PVB[:, :], 0.0).then_inc(d_zero, 1)
            dve.wait_ge(scattered[1], 16)
            dve.wait_ge(w_in, 16 * NWL)
            nc.vector.tensor_copy(identb, ident)
            nc.vector.tensor_copy(upperb, upper)
            nc.vector.tensor_copy(onesb, ones).then_inc(cast, 1)
            dve.wait_ge(d_zero, 4)
            dve.wait_ge(a_tg, 1)
            statistics(0, 0)
            shift(0, 0)
            rotate_q(0, 0)
            statistics(0, 1)
            remainder(0, 0, 0)
            remainder(0, 0, 1)
            shift(0, 1)
            values(0, 0)
            rotate_q(0, 1)
            for g in range(4):
                maximum(0, 0, g)
            split_maximum(0, 0)
            maximum_transposed(0, 0)

            def body(j):
                for u in range(8):
                    uu, cc = u % CH, u // CH
                    nj, ncc = (j, 1) if cc == 0 else (j + 1, 0)
                    pj, pcc = (j - 1, 1) if cc == 0 else (j, 0)
                    has_next, has_after = inside(nj, 4 * ncc), inside(j + 1, 4 * cc)
                    has_last, has_before = inside(pj, 4 * pcc), inside(j - 1, 4 * cc)
                    nxt, prv = later(j, u, 1), later(j, u, -1)
                    if uu == 0 and has_before:
                        take_positions(j - 1, cc)
                    if uu == 3 and has_last:
                        take_scores(pj, pcc)
                    if inside(*nxt):
                        maximum(*nxt, 0)
                        maximum(*nxt, 1)
                    if inside(*prv):
                        divide(*prv)
                    if uu == 1 and has_next:
                        remainder(nj, ncc, 1)
                    if inside(*nxt):
                        maximum(*nxt, 2)
                        maximum(*nxt, 3)
                        split_maximum(*nxt)
                    if inside(*prv):
                        add_attention(*prv)
                    if inside(*nxt):
                        maximum_transposed(*nxt)
                    if inside(*prv):
                        statistics1(*prv)
                    if uu == 0:
                        if has_next:
                            remainder(nj, ncc, 0)
                        if has_before:
                            place(j - 1, cc)
                        if has_last:
                            statistics2(pj, pcc)
                    if uu == 1:
                        if has_last:
                            scales2(pj, pcc)
                        if has_next:
                            values(nj, ncc)
                    if uu == 2:
                        if has_after:
                            statistics(j + 1, cc)
                        if has_before:
                            probabilities(j - 1, cc)
                        if has_after:
                            shift(j + 1, cc)
                    if uu == 3:
                        if has_last:
                            choose(pj, pcc)
                        if has_after:
                            rotate_q(j + 1, cc)

            blocks(dve, body)
            J = B // 8 - 1
            take_positions(J, 0)
            divide(J, 7)
            place(J, 0)
            probabilities(J, 0)
            add_attention(J, 7)
            statistics1(J, 7)
            statistics2(J, 1)
            scales2(J, 1)
            take_scores(J, 1)
            choose(J, 1)
            take_positions(J, 1)
            place(J, 1)

            ch = Chain(dve, d_tc, 0)
            dve.wait_ge(pe_cnt, 1)
            ch.link(nc.vector.tensor_scalar(cnt_i[:, :], PB[0:E, 0:1], 127.0, None, ALU.add))
            ch.link(nc.vector.tensor_scalar(nt_i[:, :], cnt_i[:, :], 7, None, ALU.arith_shift_right))
            nc.vector.tensor_tensor(padrow[:, :], PB[0:1, 8:8 + E], ebase4[0:1, 0, :], ALU.add)
            nc.vector.tensor_copy(ntf[:, :], nt_i[:, :]).then_inc(d_nt, 1)
            dve.wait_ge(pe_ts, 1)
            ch.link(nc.vector.tensor_copy(tsf[:, :], PB[0:E, 16:17]))
            nc.vector.scalar_tensor_tensor(tc[:, :], tsf[:, :], -128.0, exp_row, ALU.mult, ALU.add)
            ch.link(nc.vector.tensor_tensor(tef[:, :], tsf[:, :], ntf[:, :], ALU.add))
            ch.link(nc.vector.tensor_scalar(s1[:, :], tile_no, tsf[:, 0:1], None, ALU.is_ge))
            ch.link(nc.vector.scalar_tensor_tensor(sel[:, :], tile_no, tef[:, 0:1], s1[:, :], ALU.is_lt, ALU.mult))
            nc.vector.scalar_tensor_tensor(tabv[:, 0, :], tile_row, tc[:, 0:1], sel[:, :], ALU.add, ALU.mult)
            nc.vector.tensor_scalar(tabv[:, 1, :], sel[:, :], exp_no, None, ALU.mult).then_inc(d_ts, 1)
            dve.wait_ge(pe_tab, 1)
            nc.vector.tensor_scalar(tab[:, 0, :], PB[0:1, 32:32 + NT], float(TRASH), None, ALU.add)
            nc.vector.tensor_copy(tab[:, 1, :], PB[0:1, 32 + NT:32 + 2 * NT]).then_inc(d_tab, 1)
            probabilities(J, 1)

            def result_rows(q, r):
                t = 4 * q + r
                dve.wait_ge(tile_in[r], 16 * (q + 1))
                if counts(16 * q):
                    dve.wait_ge(sent[r], 16 * q)
                nc.vector.tensor_copy(yi[:, r:r + 1], xs[:, r, D:D + 1].bitcast(U32)).then_inc(fd_i, 1)

            def hidden(q, r):
                t = 4 * q + r
                dve.wait_ge(fa_g, t + 1)
                dve.wait_ge(f_up, 2 * t + 2)
                if counts(t - 1):
                    dve.wait_ge(f_hT, t - 1)
                nc.vector.tensor_tensor(hh[:, r % 2, :], sg[:, r % 2, :], bank[2 * (r % 2) + 1][:, 0:H], ALU.mult)\
                    .then_inc(fd_h, 1)

            def hidden_down(q, r):
                t = 4 * q + r
                dve.wait_ge(f_hT, t + 1)
                if counts(t - 1):
                    dve.wait_ge(f_y, t - 1)
                nfull = H // 128 * 128
                nc.vector.tensor_copy(hT[:, r % 2, 0:nfull], bank[5][:, 0:nfull])
                nc.vector.tensor_copy(hT[0:H - nfull, r % 2, nfull:nfull + 128], bank[5][0:H - nfull, nfull:nfull + 128])\
                    .then_inc(fd_hT, 1)

            for r in range(3):
                result_rows(0, r)
            for r in range(2):
                hidden(0, r)

            def body(q):
                for r in range(4):
                    hidden_down(q, r)
                    if is_tile(*tile_after(q, r, 3)):
                        result_rows(*tile_after(q, r, 3))
                    if is_tile(*tile_after(q, r, 2)):
                        hidden(*tile_after(q, r, 2))

            body(0)
            with dve.Fori(1, NT // 4 - 1) as q:
                body(q)
            body(NT // 4 - 1)

            dve.wait_ge(a_base, B)
            for c in range(NCH):
                dve.wait_ge(back_in[c % 2], 16 * (c // 2 + 1))
                for k in range(CH):
                    b = CH * c + k
                    last = nc.vector.scalar_tensor_tensor(x_sb[:, b, :], yl[:, c % 2, k, 0, :], cg[:, b, 0:1], x_sb[:, b, :],
                                                          ALU.mult, ALU.add)
                last.then_inc(d_o1, 1)
                dve.wait_ge(d_o1, c + 1)
                for k in range(CH):
                    b = CH * c + k
                    last = nc.vector.scalar_tensor_tensor(x_sb[:, b, :], yl[:, c % 2, k, 1, :], cg[:, b, 1:2], x_sb[:, b, :],
                                                          ALU.mult, ALU.add)
                last.then_inc(d_o, 1)

        @block.tensor
        def _(pe):
            mm = nc.tensor.matmul

            def transposes(j, cc):
                c = 2 * j + cc
                pe.wait_ge(a_xh, c + 1)
                if counts(c - 2):
                    pe.wait_ge(a_nT, c - 2)
                if counts(c):
                    pe.wait_ge(d_v, c)
                for k in range(CH):
                    last = nc.tensor.transpose(PA[:, k * S:(k + 1) * S], xh[:, k, :], ident)
                last.then_inc(pe_xT, 1)
                pe.wait_ge(chunk_in[cc], 32 * (j + 1))
                if counts(2 * c):
                    pe.wait_ge(d_r1, 2 * c)
                for k in range(CH):
                    last = nc.tensor.transpose(PB[:, k * S:(k + 1) * S], ctx_sb[:, cc, k, :], ident)
                last.then_inc(pe_xT, 1)

            def project(j, cc, t):
                c = 2 * j + cc
                ps, a, b_, ready = ((PA, qa, qb, d_q), (PB, ka, kb, p_k))[t]
                pe.wait_ge(ready, c + 1)
                mm(ps[:, :], wqk_sb[:, 2 * t, :], a[:, :], start=True, stop=False)
                mm(ps[:, :], wqk_sb[:, 2 * t + 1, :], b_[:, :], start=False, stop=True).then_inc(pe_qk, 1)

            def project_v(j, cc):
                c = 2 * j + cc
                pe.wait_ge(d_r1, 2 * c + 1)
                for k in range(CH):
                    last = mm(PA[:, k * D:(k + 1) * D], cTs[:, k * S:(k + 1) * S], wv_sb[:, :], start=True, stop=True)
                last.then_inc(pe_v, 1)

            def scores(j, u, g):
                b, cc, t0 = 8 * j + u, u // CH, (u % CH) * S
                if g == 0 and u % CH == 0:
                    pe.wait_ge(stack_in[cc], 288 * (j + 1))
                if counts(4 * b + g - 1):
                    pe.wait_ge(d_max, 4 * b + g - 1)
                for k in range(4):
                    i, half = 2 * g + k // 2, k % 2
                    last = mm(SB[g % 2][:, k * S:(k + 1) * S], qz[0:ROWS, cc, i, half, t0:t0 + S],
                              kp[0:ROWS, cc, i, t0:t0 + S], start=True, stop=True)
                last.then_inc(pe_s, 1)

            def scores_by_key(j, u, g):
                b, cc, t0 = 8 * j + u, u // CH, (u % CH) * S
                if g == 0:
                    pe.wait_ge(m_in[u % 2], 16 * (4 * j + u // 2 + 1))
                if counts(4 * b + g - 1):
                    pe.wait_ge(a_exp, 4 * b + g - 1)
                for k in range(2):
                    i = 2 * g + k
                    last = mm(STB[g % 2][:, k * 2 * S:(k + 1) * 2 * S].rearrange("p (h s) -> p h s", h=2),
                              kp[0:ROWS + NMAX, cc, i, t0:t0 + S],
                              qz[0:ROWS + NMAX, cc, i, :, t0:t0 + S], start=True, stop=True)
                last.then_inc(pe_st, 1)

            def weighted_values(j, u, g):
                b = 8 * j + u
                pe.wait_ge(a_exp, 4 * b + g + 1)
                if g == 0:
                    pe.wait_ge(d_v, 2 * j + u // CH + 1)
                    if counts(b):
                        pe.wait_ge(a_oT, b)
                for k in range(4):
                    last = mm(PVB[32 * k:32 * k + DK + 1, g * S:(g + 1) * S], v9[:, u // CH, u % CH, 4 * g + k, :],
                              pt[:, 4 * g + k, :], start=True, stop=True)
                last.then_inc(pe_pv, 1)

            def heads_by_query(j, u):
                b = 8 * j + u
                w = 4 * (DK + 1)
                pe.wait_ge(a_oT, b + 1)
                pe.wait_ge(d_mT, min(b + 2, B) if isinstance(b, int) else b + 2)
                for g in range(NH // 4):
                    last = mm(heads_ps[:, g * w:(g + 1) * w], oT[:, g, :], pick, start=True, stop=True)
                last.then_inc(pe_heads, 1)

            def transpose_maximum(j, u):
                b = 8 * j + u
                pe.wait_ge(d_m, b + 1)
                if counts(b - 1):
                    pe.wait_ge(d_x1, b - 1)
                nc.tensor.transpose(mT_ps, mh[:, :], identb).then_inc(pe_mT, 1)

            def transpose_attended(j, u):
                b = 8 * j + u
                pe.wait_ge(d_on, b + 1)
                nc.tensor.transpose(SMALL[:, 0:D], on[:, :], ident).then_inc(pe_aT, 1)

            def project_out(j, u):
                b = 8 * j + u
                pe.wait_ge(a_aT, b + 1)
                mm(SMALL[:, D:2 * D], onT[:, :], wo_sb[:, :], start=True, stop=True).then_inc(pe_o, 1)

            def transpose_rows(j, cc):
                c = 2 * j + cc
                pe.wait_ge(a_xn, c + 1)
                pe.wait_ge(d_v, min(c + 3, NCH) if isinstance(c, int) else c + 3)
                for k in range(CH):
                    last = nc.tensor.transpose(PA[:, k * S:(k + 1) * S], xr[:, cc, k, 0, 0:D], ident)
                last.then_inc(pe_nT, 1)

            def router(j, cc, b):
                c = 2 * j + cc
                pe.wait_ge(a_nT, c + 1)
                pe.wait_ge(d_max, min(4 * (b + 1), 4 * B) if isinstance(b, int) else 4 * (b + 1))
                for k in range(CH):
                    last = mm(SB[1][:, k * E:(k + 1) * E], nTs[:, k * S:(k + 1) * S], wr_sb[:, :], start=True, stop=True)
                last.then_inc(pe_r, 1)

            def positions(j, cc, b):
                c = 2 * j + cc
                pe.wait_ge(d_mb, c + 1)
                pe.wait_ge(d_max, min(4 * (b + 1), 4 * B) if isinstance(b, int) else 4 * (b + 1))
                for k in range(CH):
                    dst = SB[1][:, 64 + k * E:64 + (k + 1) * E]
                    mm(dst, upperb, mb[:, k, :], start=True, stop=False)
                    for kk in range(k):
                        mm(dst, onesb, mb[:, kk, :], start=False, stop=False)
                    last = mm(dst, onesb, carry[:, :], start=False, stop=True)
                last.then_inc(pe_pos, 1)

            pe.wait_ge(w_in, 16 * NWL)
            pe.wait_ge(cast, 1)
            pe.wait_ge(d_zero, 4)
            pe.wait_ge(zeroed, 3)
            transposes(0, 0)
            project(0, 0, 0)
            project(0, 0, 1)
            project_v(0, 0)
            transposes(0, 1)
            for g in range(4):
                scores(0, 0, g)
            transpose_maximum(0, 0)

            def body(j):
                for u in range(8):
                    uu, cc = u % CH, u // CH
                    nj, ncc = (j, 1) if cc == 0 else (j + 1, 0)
                    pj, pcc = (j - 1, 1) if cc == 0 else (j, 0)
                    has_next, has_after = inside(nj, 4 * ncc), inside(j + 1, 4 * cc)
                    has_last, has_before = inside(pj, 4 * pcc), inside(j - 1, 4 * cc)
                    nxt, prv = later(j, u, 1), later(j, u, -1)
                    if uu == 0 and has_before:
                        positions(j - 1, cc, 8 * j + u)
                    if uu == 3 and has_last:
                        router(pj, pcc, 8 * j + u)
                    if inside(*nxt):
                        scores(*nxt, 0)
                    if inside(*prv):
                        weighted_values(*prv, 3)
                    if uu == 0 and has_before:
                        pe.wait_ge(d_tp, 2 * (j - 1) + cc + 1)
                    if uu == 3 and has_last:
                        pe.wait_ge(d_sc, 2 * pj + pcc + 1)
                    if inside(*nxt):
                        scores(*nxt, 1)
                    if uu == 0 and has_next:
                        project(nj, ncc, 0)
                    if uu == 1 and has_next:
                        project_v(nj, ncc)
                    if inside(*prv):
                        heads_by_query(*prv)
                    if inside(*nxt):
                        scores(*nxt, 2)
                    scores_by_key(j, u, 0)
                    if inside(*nxt):
                        scores(*nxt, 3)
                    scores_by_key(j, u, 1)
                    if inside(*prv):
                        transpose_attended(*prv)
                    if uu == 2 and has_last:
                        transpose_rows(pj, pcc)
                    if uu == 3 and has_after:
                        transposes(j + 1, cc)
                    weighted_values(j, u, 0)
                    scores_by_key(j, u, 2)
                    if inside(*prv):
                        project_out(*prv)
                    weighted_values(j, u, 1)
                    scores_by_key(j, u, 3)
                    if inside(*nxt):
                        transpose_maximum(*nxt)
                    weighted_values(j, u, 2)
                    if uu == 0 and has_next:
                        project(nj, ncc, 1)

            blocks(pe, body)
            J = B // 8 - 1
            weighted_values(J, 7, 3)
            positions(J, 0, B)
            heads_by_query(J, 7)
            transpose_attended(J, 7)
            project_out(J, 7)
            transpose_rows(J, 1)
            router(J, 1, B)
            positions(J, 1, B)

            pe.wait_ge(d_slot, NCH)
            mm(PB[0:E, 0:1], carry[:, :], onesb[:, 0:1], start=True, stop=True)
            mm(PB[0:1, 8:8 + E], onesb[:, 0:1], carry[:, :], start=True, stop=True).then_inc(pe_cnt, 1)
            pe.wait_ge(d_nt, 1)
            mm(PB[0:E, 16:17], upper[0:E, 0:E], ntf[:, :], start=True, stop=True).then_inc(pe_ts, 1)
            pe.wait_ge(d_ts, 1)
            mm(PB[0:1, 32:32 + 2 * NT], ones[0:E, 0:1], tabv[:, :, :].rearrange("p a t -> p (a t)"), start=True, stop=True)\
                .then_inc(pe_tab, 1)
            pe.wait_ge(d_tab, 1)
            pe.wait_ge(wf_in, 16 * (1 + HC))

            def expert_of(q, r):
                return pe.value_load(tab[0:1, 1, bass.ds(4 * q + r, 1)], min_val=0, max_val=E - 1)

            def transpose_tile(q, r):
                t = 4 * q + r
                pe.wait_ge(tile_in[r], 16 * (q + 1))
                if counts(t):
                    pe.wait_ge(fa_x, t)
                nc.tensor.transpose(bank[4][:, 0:128], xs[:, r, 0:D], ident).then_inc(f_x, 1)

            def up(q, r):
                t = 4 * q + r
                e = expert_of(q, r)
                pe.wait_ge(fa_x, t + 1)
                if counts(t - 1):
                    pe.wait_ge(fd_h, t - 1)
                mm(bank[2 * (r % 2)][:, 0:H], xT[:, r % 2, :], wup_sb[:, bass.ds(e * (2 * H) + H, H)], start=True, stop=True)\
                    .then_inc(f_up, 1)
                mm(bank[2 * (r % 2) + 1][:, 0:H], xT[:, r % 2, :], wup_sb[:, bass.ds(e * (2 * H), H)], start=True, stop=True)\
                    .then_inc(f_up, 1)

            def transpose_hidden(q, r):
                t = 4 * q + r
                pe.wait_ge(fd_h, t + 1)
                if counts(t):
                    pe.wait_ge(fd_hT, t)
                for n in range(HC):
                    w = min(128, H - 128 * n)
                    last = nc.tensor.transpose(bank[5][0:w, 128 * n:128 * n + 128], hh[:, r % 2, 128 * n:128 * n + w], ident)
                last.then_inc(f_hT, 1)

            def down(q, r):
                t = 4 * q + r
                e = expert_of(q, r)
                pe.wait_ge(fd_hT, t + 1)
                if counts(t - 1):
                    pe.wait_ge(fa_y, t - 1)
                for n in range(HC):
                    w = min(128, H - 128 * n)
                    last = mm(bank[6 + r % 2][:, 0:D], hT[0:w, r % 2, 128 * n:128 * n + 128], wdn_sb[0:w, n, bass.ds(e * D, D)],
                              start=(n == 0), stop=(n == HC - 1))
                last.then_inc(f_y, 1)

            for r in range(3):
                transpose_tile(0, r)
                if r:
                    up(0, r - 1)

            def body(q):
                for r in range(4):
                    transpose_hidden(q, r)
                    if is_tile(*tile_after(q, r, 3)):
                        transpose_tile(*tile_after(q, r, 3))
                    if is_tile(*tile_after(q, r, 2)):
                        up(*tile_after(q, r, 2))
                    down(q, r)

            body(0)
            with pe.Fori(1, NT // 4 - 1) as q:
                body(q)
            body(NT // 4 - 1)


def lay_out(inp):
    f = np.float32
    half = D // 2
    a = {k: np.asarray(v) for k, v in inp.items()}
    def stacked(w):
        return w.reshape(NI, 2, DK, -1).transpose(1, 2, 0, 3).reshape(NH * DK, -1)
    wq, wk = stacked(a["L0_xattn_Wq_w"]), stacked(a["L0_xattn_Wk_w"])
    wqk = np.stack([wq.T, np.roll(wq, half, axis=1).T, wk.T, np.roll(wk, half, axis=1).T], axis=1)
    bqk = np.concatenate([stacked(a["L0_xattn_Wq_b"]), stacked(a["L0_xattn_Wk_b"])], axis=1)
    pos = np.arange(1, S + 1, dtype=f)[:, None]
    theta = f(10000.0) ** (f(-2.0) * np.arange(half, dtype=f) / f(D))
    angle = pos * theta.astype(f)
    cos = np.repeat(np.cos(angle), 2, axis=1).T.astype(f)
    sin = np.repeat(np.sin(angle), 2, axis=1).T.astype(f)
    sin = np.concatenate([sin[half:], -sin[:half]])
    grid = np.arange(128)
    pick = np.zeros((128, 4 * (DK + 1)), f)
    for k in range(4):
        pick[32 * k + np.arange(DK + 1), (DK + 1) * k + np.arange(DK + 1)] = 1
    con = np.concatenate([
        np.eye(128, dtype=f), cos, sin, (grid[:, None] < grid[None, :]).astype(f), np.ones((128, 128), f),
        np.broadcast_to(np.tile(np.arange(E, dtype=f), CH), (128, CH * E)),
        np.broadcast_to(np.tile(np.arange(E, dtype=f) * f(CAP), CH), (128, CH * E)),
        grid[:, None].astype(f), (grid[:, None] * CAP - TRASH).astype(f),
        np.broadcast_to(np.arange(NT, dtype=f), (128, NT)),
        np.broadcast_to(np.arange(NT, dtype=f) * f(128), (128, NT)), pick], axis=1)
    tok = (np.arange(B)[None, :, None] * S + grid[:, None, None]) * 2 + np.arange(2)[None, None, :]
    r = np.broadcast_to
    return dict(
        x=a["x"], ctx_in=a["ctx_1024"],
        gates=r(np.concatenate([a["g_xattn"], a["g_ffn"]])[None, :], (128, 2)), consts=con, wqk=wqk, bqk=bqk,
        wv=a["L0_xattn_Wv_w"].T, bvb=r(a["L0_xattn_Wv_b"][None, :], (128, D)),
        wo=a["L0_xattn_Wo_w"].T, bob=r(a["L0_xattn_Wo_b"][None, :], (128, D)),
        nscale=a["L0_ffn_norm_scale"][:, None], wr=a["L0_ffn_w_router"].T,
        wup=a["L0_ffn_w_up"].transpose(2, 0, 1).reshape(D, E * 2 * H),
        wdn=a["L0_ffn_w_down"].transpose(2, 0, 1).reshape(H, E * D),
        tokrow=tok.astype(np.uint32))


def kernel(**inputs):
    import concourse.bacc as bacc
    from concourse.bass_utils import run_bass_kernel_spmd

    nc = bacc.Bacc("TRN2", target_bir_lowering=False, num_devices=1)
    arrays, args = {}, {}
    for name, value in lay_out(inputs).items():
        value = np.ascontiguousarray(value)
        arrays[f"in_{name}"] = value
        args[name] = nc.dram_tensor(f"in_{name}", value.shape, mybir.dt.from_np(value.dtype), kind="ExternalInput").ap()
    args["out"] = nc.dram_tensor("out_0", (B, S, D), F32, kind="ExternalOutput").ap()
    flamingo(nc, **args)
    r = run_bass_kernel_spmd(nc, [arrays], core_ids=[0])
    return r.results[0]["out_0"]
```

```python
import concourse.bass as bass
import numpy as np
from concourse import mybir
from contextlib import ExitStack

F32 = mybir.dt.float32
BF16 = mybir.dt.bfloat16
U32 = mybir.dt.uint32
I32 = mybir.dt.int32
ALU = mybir.AluOpType
ACT = mybir.ActivationFunctionType
AX = mybir.AxisListType

B, S, D = 32, 128, 128
NH, DK = 16, 8
NI = NH // 2
E, H = 8, 352
CH = 4
NCH = B // CH
CT = CH * S
COMBO_Q = (0, 0, 0, 1, 1, 2)
COMBO_K = (0, 1, 2, 0, 1, 0)
ROWS = len(COMBO_Q) * 2 * DK
NMAX = 2
HC = -(-H // 128)
EW = 2 * H + HC * D
CAP = B * S + 128
TRASH = E * CAP
TILE_BITS = (TRASH // 128).bit_length()
SLOTS = 128 * 2 ** TILE_BITS
YR = 4
R = 8
NT = -(-(2 * B * S + E * 127) // 128)
NT += -NT % R
RW = 132
PAD_ROW = 2 * B * S
SCORE_SCALE = float(1.0 / np.sqrt(np.float32(DK)))


def counts(value):
    return not isinstance(value, int) or value > 0


def apart(eng, sem):
    eng.sem_inc(sem, 1)


class Chain:

    def __init__(self, eng, sem, base):
        self.eng, self.sem, self.base, self.n = eng, sem, base, 0

    def link(self, ins):
        self.n += 1
        ins.then_inc(self.sem, 1)
        self.eng.wait_ge(self.sem, self.base + self.n)


def later(j, u, k):
    return j + (u + k) // 8, (u + k) % 8


def inside(j, u):
    return not isinstance(j, int) or 0 <= 8 * j + u < B


def flamingo(nc, x, ctx_in, gates, consts, wqk, bqk, wv, bvb, wo, bob, nscale, wr, wup, wdn, tokrow, out):
    ctx = ExitStack()
    with ctx:
        def sb(name, shape, dt=F32):
            return ctx.enter_context(nc.sbuf_tensor(name, shape, dt))

        def sem(name):
            return ctx.enter_context(nc.semaphore(name))

        slots_dram = nc.dram_tensor("slots_dram", [SLOTS, RW], F32, kind="Internal").ap()
        result_dram = nc.dram_tensor("result_dram", [2 * B * S, D], F32, kind="Internal").ap()

        con = sb("con", [128, 5 * 128 + 64 + 2 + 2 * NT])
        ident, cosT, sinT = con[:, 0:128], con[:, 128:256], con[:, 256:384]
        upper, ones = con[:, 384:512], con[:, 512:640]
        iota4 = con[:, 640:672].rearrange("p (k e) -> p k e", k=CH)
        ebase4 = con[:, 672:704].rearrange("p (k e) -> p k e", k=CH)
        exp_no, exp_tile = con[0:E, 704:705], con[0:E, 705:706]
        tile_no, place8 = con[0:E, 706:706 + NT], con[0:1, 706 + NT:706 + 2 * NT]
        conb = sb("conb", [128, 3, 128], BF16)
        identb, upperb, onesb = conb[:, 0, :], conb[:, 1, :], conb[:, 2, :]
        wqk_sb = sb("wqk_sb", [128, 4, 128])
        bqk_sb = sb("bqk_sb", [128, 2])
        wv_sb, bv_sb = sb("wv_sb", [128, 128]), sb("bv_sb", [128, 128])
        wo_sb, bo_sb = sb("wo_sb", [128, 128]), sb("bo_sb", [128, 128])
        gate_sb = sb("gate_sb", [128, 2])
        ns_sb = sb("ns_sb", [128, 1])
        wr_sb = sb("wr_sb", [128, E])
        tok_sb = sb("tok_sb", [128, B, 2], U32)
        tg, silu_table = sb("tg", [128, 2]), sb("silu_table", [128, 1])
        mhalf = sb("mhalf", [128, 2, CH])

        x_sb = sb("x_sb", [128, B, D])
        ctx_sb = sb("ctx_sb", [128, 2, CH, D])
        xh = sb("xh", [128, CH, D])
        xTs, cTs = sb("xTs", [128, CT]), sb("cTs", [128, CT])
        qa, qb, ka, kb = (sb(n, [128, CT]) for n in ("qa", "qb", "ka", "kb"))
        r1 = sb("r1", [128, 2, CT])
        parts = sb("parts", [128, 2, 3, CT], BF16)
        qz = sb("qz", [128, 2, NI, 2, CT], BF16)
        kp = sb("kp", [128, 2, NI, CT], BF16)
        v9 = sb("v9", [128, 2, CH, NH, DK + 1])
        nmx = sb("nmx", [128, NH])
        mh = sb("mh", [128, 2 * NH], BF16)
        mTs = sb("mTs", [2 * NH, 2, S], BF16)
        pt = sb("pt", [128, NH, S])
        oT = sb("oT", [128, NH // 4, S])
        rc = sb("rc", [128, NH])
        on, onT = sb("on", [128, D]), sb("onT", [128, D])
        st6, mv, ve, rs, nmr = (sb("st6", [128, CH, 6]), sb("mv", [128, CH, 2]), sb("ve", [128, CH]),
                                sb("rs", [128, CH]), sb("nmr", [128, CH]))
        st6b, mv2, ve2, rs2 = (sb("st6b", [128, CH, 6]), sb("mv2", [128, CH, 2]), sb("ve2", [128, 2, CH]),
                               sb("rs2", [128, 2, 2, CH]))
        nb2, ntg = sb("nb2", [128, CH]), sb("ntg", [128, 1])
        fscale, fbias = sb("fscale", [128, B]), sb("fbias", [128, B])
        xr = sb("xr", [128, 2, CH, 2, RW])
        nTs = sb("nTs", [128, CT])
        sc, top = sb("sc", [128, CH, E]), sb("top", [128, CH, E])
        idx = sb("idx", [128, CH, E], U32)
        sub, ee = sb("sub", [128, CH, E]), sb("ee", [128, CH, E])
        m12 = sb("m12", [128, 2, CH, E])
        mb = sb("mb", [128, CH, E], BF16)
        carry = sb("carry", [128, E], BF16)
        cs = sb("cs", [128, E])
        tp, tm = sb("tp", [128, CH, E]), sb("tm", [128, 2, CH, E])
        slf = sb("slf", [128, 2, CH])
        slu = sb("slu", [128, 2, CH, 2], U32)
        sume, rsum = sb("sume", [128, CH]), sb("rsum", [128, CH])

        wf_sb = sb("wf_sb", [128, E * EW])
        cnt_i, nt_i = sb("cnt_i", [E, 1], I32), sb("nt_i", [E, 1], I32)
        ntf, tsf, tef, tc = (sb(n, [E, 1]) for n in ("ntf", "tsf", "tef", "tc"))
        s1, sel = sb("s1", [E, NT]), sb("sel", [E, NT])
        tabv = sb("tabv", [E, 2, NT])
        rows2 = sb("rows2", [1, NT // 2], I32)
        word = sb("word", [1, NT // 4], I32)
        shifted, odd = sb("shifted", [1, NT // 4 + 1, 4]), sb("odd", [1, NT // 2])
        w4, w3 = sb("w4", [1, NT // 4]), sb("w3", [1, NT // 4])
        padrow = sb("padrow", [1, E], I32)
        pad_sb = sb("pad_sb", [128, RW])
        xs = sb("xs", [128, R, RW])
        xT = sb("xT", [128, 2, 128])
        sg, hh = sb("sg", [128, 2, H]), sb("hh", [128, 2, H])
        hT = sb("hT", [128, 2, HC * 128])
        ys = sb("ys", [128, R, D])
        yi, yc = sb("yi", [128, R], U32), sb("yc", [128, R])
        yl = sb("yl", [128, YR, CH, 2, D])

        bank = [ctx.enter_context(nc.psum_tensor(f"bank{i}", [128, 512], F32)) for i in range(8)]
        SB, STB, PVB, SMALL, PA, PB = bank[0:2], bank[2:4], bank[4], bank[5], bank[6], bank[7]
        heads_ps = PVB[:, :].rearrange("p (h d) -> p h d", h=NH)
        mT_ps = SMALL[0:2 * NH, 256:320].bitcast(BF16)

        NW1, NW2 = 5, 5
        w_in, w2_in, zeroed, cast = sem("w_in"), sem("w2_in"), sem("zeroed"), sem("cast")
        chunk_in = [sem("chunk_in0"), sem("chunk_in1")]
        stack_in = [sem("stack_in0"), sem("stack_in1")]
        m_in = [sem("m_in0"), sem("m_in1")]
        scattered = [sem("scattered0"), sem("scattered1")]
        pe_s, pe_st, pe_pv, pe_mT, pe_aT, pe_o = map(sem, ("pe_s", "pe_st", "pe_pv", "pe_mT", "pe_aT", "pe_o"))
        pe_xT, pe_qk, pe_v, pe_nT, pe_r, pe_pos = map(sem, ("pe_xT", "pe_qk", "pe_v", "pe_nT", "pe_r", "pe_pos"))
        a_tg, a_xh, a_xT, a_hi, a_mid, a_exp, a_aT, a_xn, a_nT, a_e = map(
            sem, ("a_tg", "a_xh", "a_xT", "a_hi", "a_mid", "a_exp", "a_aT", "a_xn", "a_nT", "a_e"))
        d_max, d_mh, d_m, d_mT, d_rc, d_on, d_x1, d_q, d_r1, d_v = map(
            sem, ("d_max", "d_mh", "d_m", "d_mT", "d_rc", "d_on", "d_x1", "d_q", "d_r1", "d_v"))
        d_stat, d_ve, d_rs, d_stat2, d_ve2, d_t2, d_sc2, d_rt, d_top, d_m12, d_slot, d_sl, d_pr = map(
            sem, ("d_stat", "d_ve", "d_rs", "d_stat2", "d_ve2", "d_t2", "d_sc2", "d_rt", "d_top", "d_m12",
                  "d_slot", "d_sl", "d_pr"))
        a_oT, pe_heads, d_bn, d_sc, d_tp, d_fs, d_ntg = map(
            sem, ("a_oT", "pe_heads", "d_bn", "d_sc", "d_tp", "d_fs", "d_ntg"))
        d_mx, d_slf = sem("d_mx"), sem("d_slf")
        p_gbo, p_rs, p_k, p_lo, p_xb, p_rs2, p_rr = map(
            sem, ("p_gbo", "p_rs", "p_k", "p_lo", "p_xb", "p_rs2", "p_rr"))
        d_mb, d_cg, d_zero, a_base = map(sem, ('d_mb', 'd_cg', 'd_zero', 'a_base'))
        out_sem, d_apart, p_apart, s_apart = map(sem, ("out_sem", "d_apart", "p_apart", "s_apart"))
        wf_in, padded = sem("wf_in"), [sem(f"padded{i}") for i in range(2)]
        pe_cnt, pe_ts, pe_tab, d_nt, d_ts, d_tab, d_tc = map(
            sem, ("pe_cnt", "pe_ts", "pe_tab", "d_nt", "d_ts", "d_tab", "d_tc"))
        tile_in = [sem(f"tile_in{r}") for r in range(R)]
        sent = [sem(f"sent{r}") for r in range(R)]
        f_x, f_up, f_hT, f_y = map(sem, ("f_x", "f_up", "f_hT", "f_y"))
        fa_x, fa_g, fa_y, fd_i, fd_h, fd_hT = map(sem, ("fa_x", "fa_g", "fa_y", "fd_i", "fd_h", "fd_hT"))
        back_in = [sem(f"back_in{r}") for r in range(YR)]
        d_o, d_o1 = sem("d_o"), sem("d_o1")
        d_rows = sem("d_rows")

        def tile_after(q, r, k):
            return q + (r + k) // R, (r + k) % R

        def is_tile(q, r):
            return not isinstance(q, int) or R * q + r < NT

        def blocks(eng, body):
            body(0)
            with eng.Fori(1, B // 8 - 1) as j:
                body(j)
            body(B // 8 - 1)

        block = ctx.enter_context(nc.Block())

        @block.sync
        def _(sp):
            def load(j, cc):
                c = 2 * j + cc
                if counts(2 * c - 2):
                    sp.wait_ge(pe_xT, 2 * c - 2)
                sp.dma_start(x_sb[:, bass.ds(CH * c, CH), :], x[bass.ds(CH * c, CH), :, :].rearrange("b s d -> s b d"))\
                    .then_inc(chunk_in[cc], 16)
                sp.dma_start(ctx_sb[:, cc, :, :], ctx_in[bass.ds(CH * c, CH), :, :].rearrange("b s d -> s b d"))\
                    .then_inc(chunk_in[cc], 16)

            def stack_q(cc, combos):
                for n in combos:
                    for half in range(2):
                        row = n * 2 * DK + half * DK
                        sp.dma_start(qz[row:row + DK, cc, :, half, :],
                                     parts[half * 64:half * 64 + 64, 0, COMBO_Q[n], :]).then_inc(stack_in[cc], 16)

            def stack_k(cc, combos):
                for n in combos:
                    sp.dma_start(kp[n * 2 * DK:(n + 1) * 2 * DK, cc, :, :],
                                 parts[:, 1, COMBO_K[n], :]).then_inc(stack_in[cc], 16)

            def stack_first(j, cc):
                c = 2 * j + cc
                if counts(16 * (c - 1)):
                    sp.wait_ge(pe_st, 16 * (c - 1))
                apart(sp, s_apart)
                sp.wait_ge(a_hi, 2 * c + 1)
                stack_q(cc, (0, 1, 2))

            def stack_second(j, cc):
                c = 2 * j + cc
                sp.wait_ge(a_mid, 2 * c + 1)
                stack_q(cc, (3, 4))

            def stack_third(j, cc):
                c = 2 * j + cc
                sp.wait_ge(p_lo, 2 * c + 1)
                stack_q(cc, (5,))
                sp.wait_ge(a_hi, 2 * c + 2)
                stack_k(cc, (0, 3, 5))

            def stack_fourth(j, cc):
                c = 2 * j + cc
                sp.wait_ge(a_mid, 2 * c + 2)
                stack_k(cc, (1, 4))
                sp.wait_ge(p_lo, 2 * c + 2)
                stack_k(cc, (2,))

            def maxima(j, u):
                sp.wait_ge(d_mT, 8 * j + u + 1)
                t0 = (u % CH) * S
                sp.dma_start(qz[ROWS:ROWS + NMAX, u // CH, :, :, t0:t0 + S].rearrange("r i h t -> r (i h) t"),
                             mTs[:, u % 2, :]).then_inc(m_in[u % 2], 16)

            def store(c):
                sp.wait_ge(d_o, c + 1)
                sp.dma_start(out[CH * c:CH * (c + 1), :, :].rearrange("b s d -> s b d"), x_sb[:, CH * c:CH * (c + 1), :])\
                    .then_inc(out_sem, 16)

            load(0, 0)
            for dst, src in ((gate_sb[:, :], gates), (con[:, :], consts), (wqk_sb[:, :, :], wqk), (bqk_sb[:, :], bqk),
                             (bo_sb[:, :], bob)):
                sp.dma_start(dst, src).then_inc(w_in, 16)
            load(0, 1)
            for dst, src in ((wv_sb[:, :], wv), (bv_sb[:, :], bvb), (wo_sb[:, :], wo), (ns_sb[:, :], nscale),
                             (wr_sb[:, :], wr)):
                sp.dma_start(dst, src).then_inc(w2_in, 16)
            sp.wait_ge(d_zero, 1)
            sp.wait_ge(zeroed, 1)
            stack_first(0, 0)
            stack_second(0, 0)
            stack_third(0, 0)
            stack_fourth(0, 0)
            maxima(0, 0)
            sp.wait_ge(zeroed, 5)

            wf = wf_sb[:, :].rearrange("p (e w) -> p e w", e=E)

            def ffn_weights(u):
                sp.dma_start(wf[:, u, 0:2 * H], wup[:, u * 2 * H:(u + 1) * 2 * H]).then_inc(wf_in, 16)
                n = u - (E - HC)
                if n >= 0:
                    rows_n = min(128, H - 128 * n)
                    sp.dma_start(wf[0:rows_n, :, 2 * H + n * D:2 * H + (n + 1) * D],
                                 wdn[128 * n:128 * n + rows_n, :].rearrange("p (e w) -> p e w", e=E)).then_inc(wf_in, 16)

            def body(j):
                for u in range(8):
                    uu, cc = u % CH, u // CH
                    nj, ncc = (j, 1) if cc == 0 else (j + 1, 0)
                    if uu == 0 and inside(j + 1, 4 * cc):
                        load(j + 1, cc)
                    if uu == 0 and inside(nj, 4 * ncc):
                        stack_first(nj, ncc)
                    if uu == 1 and inside(nj, 4 * ncc):
                        stack_third(nj, ncc)
                    if inside(*later(j, u, 1)):
                        maxima(*later(j, u, 1))
                    if uu == 0 and inside(nj, 4 * ncc):
                        stack_second(nj, ncc)
                    if uu == 1 and inside(nj, 4 * ncc):
                        stack_fourth(nj, ncc)
                    if isinstance(j, int) and j == 0:
                        ffn_weights(u)

            blocks(sp, body)
            sp.wait_ge(d_nt, 1)
            for e in range(E // 2):
                row = sp.value_load(padrow[0:1, e:e + 1], min_val=0, max_val=TRASH - 128)
                sp.dma_start(slots_dram[bass.ds(row, 128), :], pad_sb[:, :]).then_inc(padded[0], 16)
            sp.wait_ge(d_tab, 1)

            def body(q):
                for r in range(R):
                    t = R * q + r
                    if r % 2 == 0:
                        pair = sp.value_load(rows2[0:1, bass.ds(R // 2 * q + r // 2, 1)], min_val=0, max_val=4 ** TILE_BITS - 1)
                    if isinstance(q, int) and q == 0 and r == 0:
                        sp.wait_ge(padded[0], 16 * (E // 2))
                        sp.wait_ge(padded[1], 16 * (E - E // 2))
                        sp.wait_ge(scattered[0], 16 + 128 * (B // 8))
                        sp.wait_ge(scattered[1], 16 + 128 * (B // 8))
                    row = ((pair >> (TILE_BITS * (r % 2))) & (2 ** TILE_BITS - 1)) * 128
                    if counts(t - R + 1):
                        sp.wait_ge(f_x, t - R + 1)
                    if counts(t - R + 1):
                        sp.wait_ge(fd_i, t - R + 1)
                    apart(sp, s_apart)
                    sp.dma_start(xs[:, r, :], slots_dram[bass.ds(row, 128), :]).then_inc(tile_in[r], 16)

            body(0)
            with sp.Fori(1, NT // R) as q:
                body(q)
            for r in range(R):
                sp.wait_ge(sent[r], 16 * (NT // R))
            def fetch(c):
                if counts(c - YR + 1):
                    sp.wait_ge(d_o, c - YR + 1)
                sp.dma_start(yl[:, c % YR, :, :, :], result_dram[c * 2 * CT:(c + 1) * 2 * CT, :]
                             .rearrange("(b s k) d -> s b k d", s=S, k=2)).then_inc(back_in[c % YR], 16)

            for c in range(YR):
                fetch(c)
            for c in range(NCH - 1):
                store(c)
                if c + YR < NCH:
                    fetch(c + YR)
            store(NCH - 1)
            sp.wait_ge(out_sem, 16 * NCH)

        @block.gpsimd
        def _(pool):
            def power(j, cc):
                c = 2 * j + cc
                pool.wait_ge(d_ve, c + 1)
                if counts(c):
                    pool.wait_ge(a_xh, c)
                nc.gpsimd.tensor_tensor(rs[:, :], ve[:, :], mhalf[:, 0, :], ALU.pow).then_inc(p_rs, 1)

            def rotate_k(j, cc):
                c = 2 * j + cc
                pool.wait_ge(a_xT, 2 * c + 2)
                if counts(2 * c):
                    pool.wait_ge(pe_qk, 2 * c)
                for dst, tab in ((ka, cosT), (kb, sinT)):
                    last = nc.gpsimd.tensor_tensor(dst[:, :].rearrange("p (k s) -> p k s", k=CH),
                                                   cTs[:, :].rearrange("p (k s) -> p k s", k=CH),
                                                   tab.unsqueeze(1).to_broadcast([128, CH, S]), ALU.mult)
                last.then_inc(p_k, 1)

            def low(j, cc, t):
                c = 2 * j + cc
                pool.wait_ge(a_mid, 2 * c + t + 1)
                nc.gpsimd.tensor_tensor(parts[:, t, 2, :], r1[:, t, :], parts[:, t, 1, :], ALU.subtract)\
                    .then_inc(p_lo, 1)

            def add_bias(j, cc):
                c = 2 * j + cc
                pool.wait_ge(a_xh, c + 1)
                nc.gpsimd.tensor_tensor(x_sb[:, bass.ds(CH * c, CH), :], x_sb[:, bass.ds(CH * c, CH), :],
                                        bo_sb[:, :].unsqueeze(1).to_broadcast([128, CH, D]), ALU.add).then_inc(p_xb, 1)

            def power2(j, cc):
                c = 2 * j + cc
                pool.wait_ge(d_ve2, c + 1)
                nc.gpsimd.tensor_tensor(rs2[:, cc, :, :], ve2[:, :, :], mhalf[:, :, :], ALU.pow).then_inc(p_rs2, 1)

            def scatter(j, cc, batches):
                c = 2 * j + cc
                pool.wait_ge(d_slot, c + 1)
                pool.wait_ge(a_xn, c + 1)
                if isinstance(c, int) and c == NCH - 1:
                    pool.wait_ge(d_rows, 1)
                pool.wait_ge(d_cg, c + 1)
                apart(pool, p_apart)
                for k in batches:
                    for kk in range(2):
                        nc.gpsimd.indirect_dma_start(
                            out=slots_dram, out_offset=bass.IndirectOffsetOnAxis(ap=slu[:, cc, k, kk:kk + 1], axis=0),
                            in_=xr[:, cc, k, kk, :], in_offset=None).then_inc(scattered[cc], 16)

            nc.gpsimd.memset(kp[ROWS:ROWS + NMAX, :, :, :].bitcast(U32), 0x3F803F80).then_inc(zeroed, 1)
            pool.wait_ge(zeroed, 1)
            nc.gpsimd.memset(mhalf[:, :, :], -0.5).then_inc(zeroed, 1)
            pool.wait_ge(w_in, 16 * NW1)
            pool.wait_ge(a_tg, 1)
            nc.gpsimd.tensor_scalar(bo_sb[:, :], bo_sb[:, :], tg[:, 0:1], None, ALU.mult).then_inc(p_gbo, 1)
            pool.wait_ge(p_gbo, 1)
            pool.wait_ge(zeroed, 2)
            power(0, 0)
            nc.gpsimd.memset(pad_sb[:, :], 0.0).then_inc(zeroed, 1)
            pool.wait_ge(zeroed, 3)
            nc.gpsimd.memset(pad_sb[:, D:D + 1].bitcast(U32), PAD_ROW).then_inc(zeroed, 1)
            pool.wait_ge(zeroed, 4)
            rotate_k(0, 0)
            power(0, 1)
            nc.gpsimd.memset(qz[:, 1, :, :, :].bitcast(U32), 0).then_inc(zeroed, 1)
            low(0, 0, 0)
            low(0, 0, 1)
            rotate_k(0, 1)
            pool.dma_start(slots_dram[TRASH:TRASH + 128, :], pad_sb[:, :]).then_inc(scattered[0], 16)
            pool.dma_start(tok_sb[:, :, :], tokrow).then_inc(scattered[1], 16)
            add_bias(0, 0)
            add_bias(0, 1)

            def body(j):
                for u in range(8):
                    uu, cc = u % CH, u // CH
                    nj, ncc = (j, 1) if cc == 0 else (j + 1, 0)
                    pj, pcc = (j - 1, 1) if cc == 0 else (j, 0)
                    has_next, has_after = inside(nj, 4 * ncc), inside(j + 1, 4 * cc)
                    has_last, has_before = inside(pj, 4 * pcc), inside(j - 1, 4 * cc)
                    if uu == 0:
                        if has_next:
                            low(nj, ncc, 0)
                        if has_last:
                            power2(pj, pcc)
                    if uu == 1:
                        if has_before:
                            scatter(j - 1, cc, (0, 1))
                        if has_next:
                            low(nj, ncc, 1)
                    if uu == 2:
                        if has_before:
                            scatter(j - 1, cc, (2, 3))
                        if has_after:
                            power(j + 1, cc)
                    if uu == 3 and has_after:
                        add_bias(j + 1, cc)
                        rotate_k(j + 1, cc)

            blocks(pool, body)
            J = B // 8 - 1
            power2(J, 1)
            scatter(J, 0, range(CH))
            scatter(J, 1, range(CH))

            def send(q):
                for r in range(R):
                    pool.wait_ge(fa_y, R * q + r + 1)
                    apart(pool, p_apart)
                    nc.gpsimd.indirect_dma_start(
                        out=result_dram, out_offset=bass.IndirectOffsetOnAxis(ap=yi[:, r:r + 1], axis=0),
                        in_=ys[:, r, :], in_offset=None, bounds_check=PAD_ROW - 1, oob_is_err=False)\
                        .then_inc(sent[r], 16)

            with pool.Fori(0, NT // R) as q:
                send(q)

        @block.scalar
        def _(act):
            def normalise(j, cc):
                c = 2 * j + cc
                act.wait_ge(d_rs, c + 1)
                if counts(2 * c - 1):
                    act.wait_ge(pe_xT, 2 * c - 1)
                for k in range(CH):
                    last = nc.scalar.activation(xh[:, k, :], x_sb[:, bass.ds(CH * c + k, 1), :], ACT.Identity,
                                                bias=nmr[:, k:k + 1], scale=rs[:, k:k + 1])
                last.then_inc(a_xh, 1)

            def transposed(j, cc):
                c = 2 * j + cc
                act.wait_ge(pe_xT, 2 * c + 1)
                if counts(c):
                    act.wait_ge(d_q, c)
                nc.scalar.activation(xTs[:, :], PA[:, :], ACT.Copy).then_inc(a_xT, 1)
                act.wait_ge(pe_xT, 2 * c + 2)
                if counts(c):
                    act.wait_ge(p_k, c)
                if counts(c):
                    act.wait_ge(pe_v, c)
                nc.scalar.activation(cTs[:, :], PB[:, :], ACT.Copy).then_inc(a_xT, 1)

            def high(j, cc, t):
                c = 2 * j + cc
                if t == 0:
                    if counts(288 * (j + cc)):
                        act.wait_ge(stack_in[1 - cc], 288 * (j + cc))
                act.wait_ge(pe_qk, 2 * c + t + 1)
                nc.scalar.activation(parts[:, t, 0, :], (PA, PB)[t][:, :], ACT.Identity, bias=bqk_sb[:, t:t + 1])\
                    .then_inc(a_hi, 1)

            def middle(j, cc, t):
                c = 2 * j + cc
                act.wait_ge(d_r1, 2 * c + t + 1)
                nc.scalar.activation(parts[:, t, 1, :], r1[:, t, :], ACT.Copy).then_inc(a_mid, 1)

            def exponent(j, u, g):
                b = 8 * j + u
                act.wait_ge(pe_st, 4 * b + g + 1)
                if counts(4 * (b - 1) + g + 1):
                    act.wait_ge(pe_pv, 4 * (b - 1) + g + 1)
                nc.scalar.activation(pt[:, 4 * g:4 * g + 4, :], STB[g % 2][:, :].rearrange("p (h s) -> p h s", h=4),
                                     ACT.Exp, scale=SCORE_SCALE).then_inc(a_exp, 1)

            def heads_out(j, u):
                b = 8 * j + u
                act.wait_ge(pe_pv, 4 * b + 4)
                if counts(b):
                    act.wait_ge(pe_heads, b)
                nc.scalar.activation(oT[:, :, :].rearrange("p g s -> p (g s)"), PVB[:, :], ACT.Copy).then_inc(a_oT, 1)

            def attended(j, u):
                b = 8 * j + u
                act.wait_ge(pe_aT, b + 1)
                if counts(b):
                    act.wait_ge(pe_o, b)
                nc.scalar.activation(onT[:, :], SMALL[:, 0:D], ACT.Copy).then_inc(a_aT, 1)

            def rows(j, cc):
                c = 2 * j + cc
                act.wait_ge(d_sc2, c + 1)
                act.wait_ge(scattered[cc], 16 + 128 * j)
                for k in range(CH // 2 if isinstance(c, int) and c == NCH - 1 else CH):
                    last = nc.scalar.activation(xr[:, cc, k, :, 0:D], x_sb[:, bass.ds(CH * c + k, 1), :].to_broadcast([128, 2, D]),
                                                ACT.Identity, bias=nb2[:, k:k + 1], scale=rs2[:, cc, 1, k:k + 1])
                last.then_inc(a_xn, 1)

            def rows_transposed(j, cc):
                c = 2 * j + cc
                act.wait_ge(pe_nT, c + 1)
                if counts(c):
                    act.wait_ge(pe_r, c)
                nc.scalar.activation(nTs[:, :], PA[:, :], ACT.Identity, scale=ns_sb[:, 0:1]).then_inc(a_nT, 1)

            def expert_exp(j, cc):
                act.wait_ge(d_top, 2 * j + cc + 1)
                nc.scalar.activation(ee[:, :, :], sub[:, :, :], ACT.Exp).then_inc(a_e, 1)

            act.wait_ge(w_in, 16 * NW1)
            nc.scalar.activation(tg[:, :], gate_sb[:, :], ACT.Tanh).then_inc(a_tg, 1)
            normalise(0, 0)
            transposed(0, 0)
            high(0, 0, 0)
            high(0, 0, 1)
            middle(0, 0, 0)
            middle(0, 0, 1)
            normalise(0, 1)
            transposed(0, 1)

            def body(j):
                for u in range(8):
                    uu, cc = u % CH, u // CH
                    nj, ncc = (j, 1) if cc == 0 else (j + 1, 0)
                    pj, pcc = (j - 1, 1) if cc == 0 else (j, 0)
                    has_next, has_after = inside(nj, 4 * ncc), inside(j + 1, 4 * cc)
                    has_last, has_before = inside(pj, 4 * pcc), inside(j - 1, 4 * cc)
                    prv = later(j, u, -1)
                    if uu == 1 and has_next:
                        high(nj, ncc, 1)
                    if inside(*prv):
                        heads_out(*prv)
                    if uu == 0 and has_before:
                        expert_exp(j - 1, cc)
                    if uu == 0 and has_next:
                        high(nj, ncc, 0)
                    if uu == 2 and has_last:
                        rows(pj, pcc)
                    if uu == 3 and has_after:
                        normalise(j + 1, cc)
                    exponent(j, u, 0)
                    if inside(*prv):
                        attended(*prv)
                    exponent(j, u, 1)
                    if uu == 1 and has_next:
                        middle(nj, ncc, 1)
                    if uu == 2 and has_last:
                        rows_transposed(pj, pcc)
                    if uu == 3 and has_after:
                        transposed(j + 1, cc)
                    exponent(j, u, 2)
                    exponent(j, u, 3)
                    if uu == 0 and has_next:
                        middle(nj, ncc, 0)

            blocks(act, body)
            J = B // 8 - 1
            heads_out(J, 7)
            attended(J, 7)
            expert_exp(J, 0)
            rows(J, 1)
            rows_transposed(J, 1)
            expert_exp(J, 1)
            nc.scalar.activation(silu_table[:, :], tg[:, 0:1], ACT.Silu)
            act.wait_ge(d_fs, NCH)
            act.wait_ge(d_nt, 1)
            for e in range(E // 2, E):
                row = act.value_load(padrow[0:1, e:e + 1], min_val=0, max_val=TRASH - 128)
                act.dma_start(slots_dram[bass.ds(row, 128), :], pad_sb[:, :]).then_inc(padded[1], 16)

            def base(b):
                nc.scalar.activation(x_sb[:, bass.ds(b, 1), :], x_sb[:, bass.ds(b, 1), :], ACT.Identity,
                                     bias=fbias[:, bass.ds(b, 1)], scale=fscale[:, bass.ds(b, 1)]).then_inc(a_base, 1)

            def rows_up(q, r):
                t = R * q + r
                act.wait_ge(f_x, t + 1)
                if counts(2 * (t - 1)):
                    act.wait_ge(f_up, 2 * (t - 1))
                nc.scalar.activation(xT[:, r % 2, :], bank[4][:, 0:128], ACT.Identity, scale=ns_sb[:, 0:1])\
                    .then_inc(fa_x, 1)

            def gate(q, r):
                t = R * q + r
                act.wait_ge(f_up, 2 * t + 1)
                if counts(t - 1):
                    act.wait_ge(fd_h, t - 1)
                nc.scalar.activation(sg[:, r % 2, :], bank[2 * (r % 2)][:, 0:H], ACT.Silu).then_inc(fa_g, 1)

            def result(q, r):
                t = R * q + r
                act.wait_ge(f_y, t + 1)
                if counts(16 * q):
                    act.wait_ge(sent[r], 16 * q)
                act.wait_ge(fd_i, t + 1)
                nc.scalar.activation(ys[:, r, :], bank[6 + r % 2][:, 0:D], ACT.Identity, scale=yc[:, r:r + 1]).then_inc(fa_y, 1)

            for r in range(3):
                rows_up(0, r)
                if r:
                    gate(0, r - 1)

            def body(q):
                for r in range(R):
                    if is_tile(*tile_after(q, r, 3)):
                        rows_up(*tile_after(q, r, 3))
                    if is_tile(*tile_after(q, r, 2)):
                        gate(*tile_after(q, r, 2))
                    result(q, r)
                    if r % 2 and not (isinstance(q, int) and q == NT // R - 1):
                        base(4 * q + r // 2)

            body(0)
            with act.Fori(1, NT // R - 1) as q:
                body(q)
            body(NT // R - 1)

        @block.vector
        def _(dve):
            def statistics(j, cc):
                c = 2 * j + cc
                dve.wait_ge(chunk_in[cc], 32 * (j + 1))
                for k in range(CH):
                    last = nc.vector.bn_stats(st6[:, k, :], x_sb[:, bass.ds(CH * c + k, 1), :])
                last.then_inc(d_stat, 1)

            def variance(j, cc):
                c = 2 * j + cc
                dve.wait_ge(d_stat, 2 * c + 1)
                apart(dve, d_apart)
                if counts(c):
                    dve.wait_ge(a_xh, c)
                apart(dve, d_apart)
                for k in range(CH):
                    last = nc.vector.bn_aggr(mv[:, k, :], st6[:, k, :])
                last.then_inc(d_stat, 1)

            def widen(j, cc):
                c = 2 * j + cc
                dve.wait_ge(d_stat, 2 * c + 2)
                nc.vector.tensor_scalar(ve[:, :], mv[:, :, 1], 1e-5, None, ALU.add).then_inc(d_ve, 1)

            def shift(j, cc):
                c = 2 * j + cc
                dve.wait_ge(p_rs, c + 1)
                nc.vector.scalar_tensor_tensor(nmr[:, :], mv[:, :, 0], -1.0, rs[:, :], ALU.mult, ALU.mult)\
                    .then_inc(d_rs, 1)

            def rotate_q(j, cc):
                c = 2 * j + cc
                dve.wait_ge(a_xT, 2 * c + 1)
                if counts(2 * c - 1):
                    dve.wait_ge(pe_qk, 2 * c - 1)
                for dst, tab in ((qa, cosT), (qb, sinT)):
                    last = nc.vector.tensor_tensor(dst[:, :].rearrange("p (k s) -> p k s", k=CH),
                                                   xTs[:, :].rearrange("p (k s) -> p k s", k=CH),
                                                   tab.unsqueeze(1).to_broadcast([128, CH, S]), ALU.mult)
                last.then_inc(d_q, 1)

            def remainder(j, cc, t):
                c = 2 * j + cc
                dve.wait_ge(a_hi, 2 * c + t + 1)
                if counts(2 * c - 1 + t):
                    dve.wait_ge(p_lo, 2 * c - 1 + t)
                nc.vector.scalar_tensor_tensor(r1[:, t, :], (PA, PB)[t][:, :], bqk_sb[:, t:t + 1], parts[:, t, 0, :],
                                               ALU.add, ALU.subtract).then_inc(d_r1, 1)

            def values(j, cc):
                c = 2 * j + cc
                dve.wait_ge(pe_v, c + 1)
                if counts(16 * (c - 1)):
                    dve.wait_ge(pe_pv, 16 * (c - 1))
                nc.vector.tensor_tensor(v9[:, cc, :, :, 0:DK],
                                        PA[:, :].rearrange("p (k h d) -> p k h d", k=CH, h=NH),
                                        bv_sb[:, :].rearrange("p (h d) -> p h d", h=NH).unsqueeze(1)
                                        .to_broadcast([128, CH, NH, DK]), ALU.add).then_inc(d_v, 1)

            def maximum(j, u, g):
                b = 8 * j + u
                dve.wait_ge(pe_s, 4 * b + g + 1)
                if g == 0:
                    if counts(b):
                        dve.wait_ge(d_m, b)
                nc.vector.tensor_reduce(nmx[:, 4 * g:4 * g + 4], SB[g % 2][:, :].rearrange("p (h s) -> p h s", h=4),
                                        AX.X, ALU.max, negate=True).then_inc(d_max, 1)

            def split_maximum(j, u, part):
                b = 8 * j + u
                if part == 0:
                    if counts(b):
                        dve.wait_ge(pe_mT, b)
                    dve.wait_ge(d_max, 4 * b + 4)
                    nc.vector.tensor_copy(mh[:, 0:NH], nmx[:, :]).then_inc(d_mh, 1)
                else:
                    dve.wait_ge(d_mh, b + 1)
                    nc.vector.tensor_tensor(mh[:, NH:2 * NH], nmx[:, :], mh[:, 0:NH], ALU.subtract).then_inc(d_m, 1)

            def maximum_transposed(j, u):
                b = 8 * j + u
                dve.wait_ge(pe_mT, b + 1)
                if counts(16 * (4 * j + u // 2)):
                    dve.wait_ge(m_in[u % 2], 16 * (4 * j + u // 2))
                nc.vector.tensor_copy(mTs[:, u % 2, :], mT_ps).then_inc(d_mT, 1)

            def sums(j, u):
                b = 8 * j + u
                dve.wait_ge(pe_heads, b + 1)
                nc.vector.reciprocal(rc[:, :], heads_ps[:, :, DK]).then_inc(d_rc, 1)

            def divide(j, u):
                b = 8 * j + u
                if counts(b):
                    dve.wait_ge(pe_aT, b)
                dve.wait_ge(d_rc, b + 1)
                nc.vector.tensor_tensor(on[:, :].rearrange("p (h d) -> p h d", h=NH), heads_ps[:, :, 0:DK],
                                        rc[:, :].unsqueeze(2).to_broadcast([128, NH, DK]), ALU.mult).then_inc(d_on, 1)

            def add_attention(j, u):
                b = 8 * j + u
                dve.wait_ge(pe_o, b + 1)
                dve.wait_ge(p_xb, 2 * j + u // CH + 1)
                nc.vector.scalar_tensor_tensor(x_sb[:, bass.ds(b, 1), :].rearrange("p b d -> p (b d)"), SMALL[:, D:2 * D], tg[:, 0:1], x_sb[:, bass.ds(b, 1), :].rearrange("p b d -> p (b d)"),
                                               ALU.mult, ALU.add).then_inc(d_x1, 1)

            def statistics1(j, u):
                b = 8 * j + u
                dve.wait_ge(d_x1, b + 1)
                apart(dve, d_apart)
                nc.vector.bn_stats(st6b[:, u % CH, :], x_sb[:, bass.ds(b, 1), :]).then_inc(d_bn, 1)

            def statistics2(j, cc):
                c = 2 * j + cc
                dve.wait_ge(d_bn, CH * (c + 1))
                apart(dve, d_apart)
                for k in range(CH):
                    last = nc.vector.bn_aggr(mv2[:, k, :], st6b[:, k, :])
                last.then_inc(d_stat2, 1)
                dve.wait_ge(d_stat2, c + 1)
                nc.vector.tensor_scalar(ve2[:, 0, :], mv2[:, :, 1], 1e-5, None, ALU.add)
                nc.vector.tensor_scalar(ve2[:, 1, :], mv2[:, :, 1], 1.0 + 1e-6, 1e-11, ALU.mult, ALU.add).then_inc(d_ve2, 1)

            def scales2(j, cc):
                c = 2 * j + cc
                if counts(c):
                    dve.wait_ge(a_xn, c)
                apart(dve, d_apart)
                dve.wait_ge(p_rs2, c + 1)
                nc.vector.scalar_tensor_tensor(nb2[:, :], mv2[:, :, 0], -1.0, rs2[:, cc, 1, :], ALU.mult, ALU.mult)\
                    .then_inc(d_sc2, 1)
                nc.vector.tensor_scalar(fscale[:, bass.ds(CH * c, CH)], rs2[:, cc, 0, :], tg[:, 1:2], 1.0, ALU.mult, ALU.add)
                nc.vector.scalar_tensor_tensor(fbias[:, bass.ds(CH * c, CH)], mv2[:, :, 0], ntg[:, 0:1], rs2[:, cc, 0, :],
                                               ALU.mult, ALU.mult).then_inc(d_fs, 1)

            def last_rows():
                dve.wait_ge(d_sc2, NCH)
                dve.wait_ge(scattered[1], 16 + 128 * (B // 8 - 1))
                for k in range(CH // 2, CH):
                    last = nc.vector.tensor_scalar(xr[:, 1, k, :, 0:D], x_sb[:, B - CH + k:B - CH + k + 1, :].to_broadcast([128, 2, D]),
                                                   rs2[:, 1, 1, k:k + 1], nb2[:, k:k + 1], ALU.mult, ALU.add)
                last.then_inc(d_rows, 1)

            def take_scores(j, cc):
                c = 2 * j + cc
                dve.wait_ge(pe_r, c + 1)
                if counts(c):
                    dve.wait_ge(a_e, c)
                nc.vector.tensor_copy(sc[:, :, :], SB[1][:, 0:CH * E].rearrange("p (k e) -> p k e", k=CH)).then_inc(d_sc, 1)

            def choose_values(j, cc):
                c = 2 * j + cc
                dve.wait_ge(d_sc, c + 1)
                apart(dve, d_apart)
                for k in range(CH):
                    last = nc.vector.max(top[:, k, :], sc[:, k, :])
                last.then_inc(d_mx, 1)

            def choose_experts(j, cc):
                c = 2 * j + cc
                dve.wait_ge(d_mx, c + 1)
                apart(dve, d_apart)
                for k in range(CH):
                    nc.vector.max_index(idx[:, k, :], top[:, k, :], sc[:, k, :])
                nc.vector.tensor_tensor(sub[:, :, :], top[:, :, :], top[:, :, 0:1].to_broadcast([128, CH, E]),
                                        ALU.subtract).then_inc(d_top, 1)

            def choose_masks(j, cc):
                c = 2 * j + cc
                dve.wait_ge(d_top, c + 1)
                nc.vector.tensor_tensor(m12[:, :, :, :], iota4.unsqueeze(1).to_broadcast([128, 2, CH, E]),
                                        idx[:, :, 0:2].rearrange("p k a -> p a k").unsqueeze(3).to_broadcast([128, 2, CH, E]),
                                        ALU.is_equal).then_inc(d_m12, 1)

            def choose_sum(j, cc):
                c = 2 * j + cc
                if counts(c):
                    dve.wait_ge(pe_pos, c)
                apart(dve, d_apart)
                dve.wait_ge(d_m12, c + 1)
                nc.vector.tensor_tensor(mb[:, :, :], m12[:, 0, :, :], m12[:, 1, :, :], ALU.add).then_inc(d_mb, 1)

            def take_positions(j, cc):
                c = 2 * j + cc
                dve.wait_ge(pe_pos, c + 1)
                nc.vector.tensor_tensor(tp[:, :, :], SB[1][:, 64:64 + CH * E].rearrange("p (k e) -> p k e", k=CH), ebase4,
                                        ALU.add).then_inc(d_tp, 1)

            def place_rows(j, cc):
                c = 2 * j + cc
                dve.wait_ge(d_tp, c + 1)
                nc.vector.tensor_tensor(tm[:, :, :, :], tp[:, :, :].unsqueeze(1).to_broadcast([128, 2, CH, E]),
                                        m12[:, :, :, :], ALU.mult)
                nc.vector.tensor_reduce(cs[:, :], mb[:, :, :].rearrange("p k e -> p e k"), AX.X, ALU.add).then_inc(d_sl, 1)
                dve.wait_ge(scattered[cc], 16 + 128 * j)
                nc.vector.tensor_copy(xr[:, cc, :, :, D:D + 1].bitcast(U32),
                                      tok_sb[:, bass.ds(CH * c, CH), :].unsqueeze(3))

            def place(j, cc):
                c = 2 * j + cc
                dve.wait_ge(d_sl, c + 1)
                nc.vector.tensor_tensor(carry[:, :], carry[:, :], cs[:, :], ALU.add)
                nc.vector.tensor_reduce(slf[:, :, :], tm[:, :, :, :], AX.X, ALU.add).then_inc(d_slf, 1)

            def place_numbers(j, cc):
                c = 2 * j + cc
                dve.wait_ge(d_slf, c + 1)
                nc.vector.tensor_copy(slu[:, cc, :, :], slf[:, :, :].rearrange("p a k -> p k a")).then_inc(d_slot, 1)

            def probabilities(j, cc, step):
                c = 2 * j + cc
                if step == 0:
                    dve.wait_ge(a_e, c + 1)
                    nc.vector.tensor_reduce(sume[:, :], ee[:, :, :], AX.X, ALU.add).then_inc(d_pr, 1)
                if step == 1:
                    dve.wait_ge(d_pr, 2 * c + 1)
                    nc.vector.reciprocal(rsum[:, :], sume[:, :]).then_inc(d_pr, 1)
                if step == 2:
                    dve.wait_ge(d_pr, 2 * c + 2)
                    nc.vector.scalar_tensor_tensor(xr[:, cc, :, :, D + 1], ee[:, :, 0:2], tg[:, 1:2],
                                                   rsum[:, :].unsqueeze(2).to_broadcast([128, CH, 2]), ALU.mult, ALU.mult)\
                        .then_inc(d_cg, 1)

            nc.vector.memset(qz[:, 0, :, :, :].bitcast(U32), 0).then_inc(d_zero, 1)
            statistics(0, 0)
            variance(0, 0)
            widen(0, 0)
            nc.vector.memset(v9[:, :, :, :, DK:DK + 1], 1.0).then_inc(d_zero, 1)
            nc.vector.memset(xr[:, :, :, :, D + 2:RW], 0.0).then_inc(d_zero, 1)
            nc.vector.memset(carry[:, :], 0.0).then_inc(d_zero, 1)
            nc.vector.memset(shifted[:, :, :], 0.0)
            nc.vector.memset(PVB[:, :], 0.0).then_inc(d_zero, 1)
            dve.wait_ge(w_in, 16 * NW1)
            nc.vector.tensor_copy(identb, ident)
            nc.vector.tensor_copy(upperb, upper)
            nc.vector.tensor_copy(onesb, ones).then_inc(cast, 1)
            dve.wait_ge(a_tg, 1)
            nc.vector.tensor_scalar(ntg[:, :], tg[:, 1:2], -1.0, None, ALU.mult).then_inc(d_ntg, 1)
            shift(0, 0)
            statistics(0, 1)
            rotate_q(0, 0)
            variance(0, 1)
            widen(0, 1)
            remainder(0, 0, 0)
            dve.wait_ge(w2_in, 16 * NW2)
            shift(0, 1)
            remainder(0, 0, 1)
            values(0, 0)
            rotate_q(0, 1)
            dve.wait_ge(scattered[1], 16)
            dve.wait_ge(d_ntg, 1)
            dve.wait_ge(d_zero, 5)
            for g in range(4):
                maximum(0, 0, g)
            split_maximum(0, 0, 0)
            split_maximum(0, 0, 1)
            maximum_transposed(0, 0)

            def body(j):
                for u in range(8):
                    uu, cc = u % CH, u // CH
                    nj, ncc = (j, 1) if cc == 0 else (j + 1, 0)
                    pj, pcc = (j - 1, 1) if cc == 0 else (j, 0)
                    has_next, has_after = inside(nj, 4 * ncc), inside(j + 1, 4 * cc)
                    has_last, has_before = inside(pj, 4 * pcc), inside(j - 1, 4 * cc)
                    nxt, prv = later(j, u, 1), later(j, u, -1)
                    has_nxt, has_prv = inside(*nxt), inside(*prv)
                    if uu == 0 and has_before:
                        take_positions(j - 1, cc)
                    if uu == 3 and has_last:
                        take_scores(pj, pcc)
                    if has_nxt:
                        maximum(*nxt, 0)
                    if uu == 0 and has_before:
                        place_rows(j - 1, cc)
                    if uu == 3 and has_last:
                        choose_values(pj, pcc)
                    if has_nxt:
                        maximum(*nxt, 1)
                    if has_prv:
                        sums(*prv)
                    if uu == 0 and has_before:
                        place(j - 1, cc)
                    if uu == 1 and has_next:
                        remainder(nj, ncc, 1)
                    if uu == 2 and has_after:
                        statistics(j + 1, cc)
                    if uu == 3 and has_last:
                        choose_experts(pj, pcc)
                    if has_prv:
                        divide(*prv)
                    if has_nxt:
                        maximum(*nxt, 2)
                    if uu == 0 and has_before:
                        place_numbers(j - 1, cc)
                    if uu == 0 and has_before:
                        probabilities(j - 1, cc, 0)
                    if uu == 2 and has_after:
                        variance(j + 1, cc)
                    if uu == 3 and has_last:
                        choose_masks(pj, pcc)
                    if has_nxt:
                        maximum(*nxt, 3)
                    if uu == 1 and has_last:
                        scales2(pj, pcc)
                    if uu == 0 and has_before:
                        probabilities(j - 1, cc, 1)
                    if uu == 2 and has_after:
                        widen(j + 1, cc)
                    if uu == 3 and has_last:
                        choose_sum(pj, pcc)
                    if has_nxt:
                        split_maximum(*nxt, 0)
                    if uu == 0 and has_before:
                        probabilities(j - 1, cc, 2)
                    if has_prv:
                        add_attention(*prv)
                    if has_nxt:
                        split_maximum(*nxt, 1)
                    if uu == 0 and has_next:
                        remainder(nj, ncc, 0)
                    if uu == 1 and has_next:
                        values(nj, ncc)
                    if has_prv:
                        statistics1(*prv)
                    if has_nxt:
                        maximum_transposed(*nxt)
                    if uu == 0 and has_last:
                        statistics2(pj, pcc)
                    if uu == 2 and has_after:
                        shift(j + 1, cc)
                    if uu == 3 and has_after:
                        rotate_q(j + 1, cc)

            blocks(dve, body)
            J = B // 8 - 1
            take_positions(J, 0)
            place_rows(J, 0)
            place(J, 0)
            place_numbers(J, 0)
            sums(J, 7)
            divide(J, 7)
            probabilities(J, 0, 0)
            probabilities(J, 0, 1)
            probabilities(J, 0, 2)
            add_attention(J, 7)
            statistics1(J, 7)
            statistics2(J, 1)
            scales2(J, 1)
            last_rows()
            take_scores(J, 1)
            choose_values(J, 1)
            choose_experts(J, 1)
            choose_masks(J, 1)
            choose_sum(J, 1)
            probabilities(J, 1, 0)
            take_positions(J, 1)
            probabilities(J, 1, 1)
            place_rows(J, 1)
            probabilities(J, 1, 2)
            place(J, 1)
            place_numbers(J, 1)

            ch = Chain(dve, d_tc, 0)
            dve.wait_ge(pe_cnt, 1)
            ch.link(nc.vector.tensor_scalar(cnt_i[:, :], PB[0:E, 0:1], 127.0, None, ALU.add))
            ch.link(nc.vector.tensor_scalar(nt_i[:, :], cnt_i[:, :], 7, None, ALU.arith_shift_right))
            nc.vector.tensor_tensor(padrow[:, :], PB[0:1, 8:8 + E], ebase4[0:1, 0, :], ALU.add)
            nc.vector.tensor_copy(ntf[:, :], nt_i[:, :]).then_inc(d_nt, 1)
            dve.wait_ge(pe_ts, 1)
            ch.link(nc.vector.tensor_copy(tsf[:, :], PB[0:E, 16:17]))
            nc.vector.scalar_tensor_tensor(tc[:, :], tsf[:, :], -1.0, exp_tile, ALU.mult, ALU.add)
            ch.link(nc.vector.tensor_tensor(tef[:, :], tsf[:, :], ntf[:, :], ALU.add))
            ch.link(nc.vector.tensor_scalar(s1[:, :], tile_no, tsf[:, 0:1], None, ALU.is_ge))
            ch.link(nc.vector.scalar_tensor_tensor(sel[:, :], tile_no, tef[:, 0:1], s1[:, :], ALU.is_lt, ALU.mult))
            nc.vector.scalar_tensor_tensor(tabv[:, 0, :], tile_no, tc[:, 0:1], sel[:, :], ALU.add, ALU.mult)
            nc.vector.tensor_scalar(tabv[:, 1, :], sel[:, :], exp_no, None, ALU.mult).then_inc(d_ts, 1)
            dve.wait_ge(pe_tab, 1)
            pairs = PB[0:1, 32:32 + NT].rearrange("p (n two) -> p n two", two=2)
            ch.link(nc.vector.tensor_scalar(odd[:, :], pairs[:, :, 1], float(TRASH // 128), float(2 ** TILE_BITS), ALU.add, ALU.mult))
            nc.vector.scalar_tensor_tensor(rows2[:, :], pairs[:, :, 0], float(TRASH // 128), odd[:, :], ALU.add, ALU.add)
            ch.link(nc.vector.tensor_tensor(shifted[:, 0:NT // 4, :].rearrange("p q r -> p (q r)"), PB[0:1, 32 + NT:32 + 2 * NT],
                                            place8, ALU.mult))
            nc.vector.tensor_reduce(w4[:, :], shifted[:, 0:NT // 4, :], AX.X, ALU.add)
            ch.link(nc.vector.tensor_reduce(w3[:, :], shifted[:, 1:NT // 4 + 1, 0:3], AX.X, ALU.add))
            nc.vector.scalar_tensor_tensor(word[:, :], w3[:, :], float(8 ** 4), w4[:, :], ALU.mult, ALU.add).then_inc(d_tab, 1)

            def result_rows(q, r):
                t = R * q + r
                dve.wait_ge(tile_in[r], 16 * (q + 1))
                if counts(16 * q):
                    dve.wait_ge(sent[r], 16 * q)
                nc.vector.tensor_copy(yi[:, r:r + 1], xs[:, r, D:D + 1].bitcast(U32))
                nc.vector.tensor_copy(yc[:, r:r + 1], xs[:, r, D + 1:D + 2]).then_inc(fd_i, 1)

            def hidden(q, r):
                t = R * q + r
                dve.wait_ge(fa_g, t + 1)
                dve.wait_ge(f_up, 2 * t + 2)
                if counts(t - 1):
                    dve.wait_ge(f_hT, t - 1)
                nc.vector.tensor_tensor(hh[:, r % 2, :], sg[:, r % 2, :], bank[2 * (r % 2) + 1][:, 0:H], ALU.mult)\
                    .then_inc(fd_h, 1)

            def hidden_down(q, r):
                t = R * q + r
                dve.wait_ge(f_hT, t + 1)
                if counts(t - 1):
                    dve.wait_ge(f_y, t - 1)
                nfull = H // 128 * 128
                nc.vector.tensor_copy(hT[:, r % 2, 0:nfull], bank[5][:, 0:nfull])
                nc.vector.tensor_copy(hT[0:H - nfull, r % 2, nfull:nfull + 128], bank[5][0:H - nfull, nfull:nfull + 128])\
                    .then_inc(fd_hT, 1)

            for r in range(3):
                result_rows(0, r)
            for r in range(2):
                hidden(0, r)
            hidden_down(0, 0)

            def body(q):
                for r in range(R):
                    if is_tile(*tile_after(q, r, 2)):
                        hidden(*tile_after(q, r, 2))
                    if is_tile(*tile_after(q, r, 3)):
                        result_rows(*tile_after(q, r, 3))
                    if is_tile(*tile_after(q, r, 1)):
                        hidden_down(*tile_after(q, r, 1))

            body(0)
            with dve.Fori(1, NT // R - 1) as q:
                body(q)
            body(NT // R - 1)

            dve.wait_ge(a_base, B)
            for c in range(NCH):
                rows_c = x_sb[:, CH * c:CH * (c + 1), :]
                dve.wait_ge(back_in[c % YR], 16 * (c // YR + 1))
                nc.vector.tensor_tensor(rows_c, rows_c, yl[:, c % YR, :, 0, :], ALU.add).then_inc(d_o1, 1)
                dve.wait_ge(d_o1, c + 1)
                nc.vector.tensor_tensor(rows_c, rows_c, yl[:, c % YR, :, 1, :], ALU.add).then_inc(d_o, 1)

        @block.tensor
        def _(pe):
            mm = nc.tensor.matmul

            def transposes(j, cc):
                c = 2 * j + cc
                pe.wait_ge(a_xh, c + 1)
                if counts(c - 2):
                    pe.wait_ge(a_nT, c - 2)
                if counts(c):
                    pe.wait_ge(d_v, c)
                for k in range(CH):
                    last = nc.tensor.transpose(PA[:, k * S:(k + 1) * S], xh[:, k, :], ident)
                last.then_inc(pe_xT, 1)
                pe.wait_ge(chunk_in[cc], 32 * (j + 1))
                if counts(2 * c):
                    pe.wait_ge(d_r1, 2 * c)
                for k in range(CH):
                    last = nc.tensor.transpose(PB[:, k * S:(k + 1) * S], ctx_sb[:, cc, k, :], ident)
                last.then_inc(pe_xT, 1)

            def project(j, cc, t):
                c = 2 * j + cc
                ps, a, b_, ready = ((PA, qa, qb, d_q), (PB, ka, kb, p_k))[t]
                pe.wait_ge(ready, c + 1)
                mm(ps[:, :], wqk_sb[:, 2 * t, :], a[:, :], start=True, stop=False)
                mm(ps[:, :], wqk_sb[:, 2 * t + 1, :], b_[:, :], start=False, stop=True).then_inc(pe_qk, 1)

            def project_v(j, cc):
                c = 2 * j + cc
                pe.wait_ge(d_r1, 2 * c + 1)
                for k in range(CH):
                    last = mm(PA[:, k * D:(k + 1) * D], cTs[:, k * S:(k + 1) * S], wv_sb[:, :], start=True, stop=True)
                last.then_inc(pe_v, 1)

            def scores(j, u, g):
                b, cc, t0 = 8 * j + u, u // CH, (u % CH) * S
                if g == 0 and u % CH == 0:
                    pe.wait_ge(stack_in[cc], 288 * (j + 1))
                if counts(4 * b + g - 1):
                    pe.wait_ge(d_max, 4 * b + g - 1)
                for k in range(4):
                    i, half = 2 * g + k // 2, k % 2
                    last = mm(SB[g % 2][:, k * S:(k + 1) * S], qz[0:ROWS, cc, i, half, t0:t0 + S],
                              kp[0:ROWS, cc, i, t0:t0 + S], start=True, stop=True)
                last.then_inc(pe_s, 1)

            def scores_by_key(j, u, g):
                b, cc, t0 = 8 * j + u, u // CH, (u % CH) * S
                if g == 0:
                    pe.wait_ge(m_in[u % 2], 16 * (4 * j + u // 2 + 1))
                if counts(4 * b + g - 1):
                    pe.wait_ge(a_exp, 4 * b + g - 1)
                for k in range(2):
                    i = 2 * g + k
                    last = mm(STB[g % 2][:, k * 2 * S:(k + 1) * 2 * S].rearrange("p (h s) -> p h s", h=2),
                              kp[0:ROWS + NMAX, cc, i, t0:t0 + S],
                              qz[0:ROWS + NMAX, cc, i, :, t0:t0 + S], start=True, stop=True)
                last.then_inc(pe_st, 1)

            def weighted_values(j, u, g):
                b = 8 * j + u
                pe.wait_ge(a_exp, 4 * b + g + 1)
                if g == 0:
                    pe.wait_ge(d_v, 2 * j + u // CH + 1)
                    if counts(b):
                        pe.wait_ge(d_on, b)
                for k in range(4):
                    last = mm(PVB[32 * k:32 * k + DK + 1, g * S:(g + 1) * S], v9[:, u // CH, u % CH, 4 * g + k, :],
                              pt[:, 4 * g + k, :], start=True, stop=True)
                last.then_inc(pe_pv, 1)

            def heads_by_query(j, u):
                b = 8 * j + u
                pe.wait_ge(a_oT, b + 1)
                for g in range(NH // 4):
                    last = nc.tensor.transpose(PVB[:, g * S:(g + 1) * S], oT[:, g, :], ident)
                last.then_inc(pe_heads, 1)

            def transpose_maximum(j, u):
                b = 8 * j + u
                pe.wait_ge(d_m, b + 1)
                if counts(b - 1):
                    pe.wait_ge(d_x1, b - 1)
                nc.tensor.transpose(mT_ps, mh[:, :], identb).then_inc(pe_mT, 1)

            def transpose_attended(j, u):
                b = 8 * j + u
                pe.wait_ge(d_on, b + 1)
                pe.wait_ge(d_mT, min(b + 2, B) if isinstance(b, int) else b + 2)
                nc.tensor.transpose(SMALL[:, 0:D], on[:, :], ident).then_inc(pe_aT, 1)

            def project_out(j, u):
                b = 8 * j + u
                pe.wait_ge(a_aT, b + 1)
                mm(SMALL[:, D:2 * D], onT[:, :], wo_sb[:, :], start=True, stop=True).then_inc(pe_o, 1)

            def transpose_rows(j, cc):
                c = 2 * j + cc
                pe.wait_ge(a_xn, c + 1)
                pe.wait_ge(d_v, min(c + 3, NCH) if isinstance(c, int) else c + 3)
                for k in range(CH):
                    if isinstance(c, int) and c == NCH - 1 and k == CH // 2:
                        pe.wait_ge(d_rows, 1)
                    last = nc.tensor.transpose(PA[:, k * S:(k + 1) * S], xr[:, cc, k, 0, 0:D], ident)
                last.then_inc(pe_nT, 1)

            def router(j, cc, b):
                c = 2 * j + cc
                pe.wait_ge(a_nT, c + 1)
                pe.wait_ge(d_max, min(4 * (b + 1), 4 * B) if isinstance(b, int) else 4 * (b + 1))
                for k in range(CH):
                    last = mm(SB[1][:, k * E:(k + 1) * E], nTs[:, k * S:(k + 1) * S], wr_sb[:, :], start=True, stop=True)
                last.then_inc(pe_r, 1)

            def positions(j, cc, b):
                c = 2 * j + cc
                pe.wait_ge(d_mb, c + 1)
                pe.wait_ge(d_max, min(4 * (b + 1), 4 * B) if isinstance(b, int) else 4 * (b + 1))
                for k in range(CH):
                    dst = SB[1][:, 64 + k * E:64 + (k + 1) * E]
                    mm(dst, upperb, mb[:, k, :], start=True, stop=False)
                    for kk in range(k):
                        mm(dst, onesb, mb[:, kk, :], start=False, stop=False)
                    last = mm(dst, onesb, carry[:, :], start=False, stop=True)
                last.then_inc(pe_pos, 1)

            pe.wait_ge(w_in, 16 * NW1)
            transposes(0, 0)
            project(0, 0, 0)
            project(0, 0, 1)
            pe.wait_ge(w2_in, 16 * NW2)
            project_v(0, 0)
            transposes(0, 1)
            pe.wait_ge(cast, 1)
            pe.wait_ge(d_zero, 5)
            for g in range(4):
                scores(0, 0, g)
            transpose_maximum(0, 0)
            scores(0, 1, 0)

            def body(j):
                for u in range(8):
                    uu, cc = u % CH, u // CH
                    nj, ncc = (j, 1) if cc == 0 else (j + 1, 0)
                    pj, pcc = (j - 1, 1) if cc == 0 else (j, 0)
                    has_next, has_after = inside(nj, 4 * ncc), inside(j + 1, 4 * cc)
                    has_last, has_before = inside(pj, 4 * pcc), inside(j - 1, 4 * cc)
                    nxt, second, prv = later(j, u, 1), later(j, u, 2), later(j, u, -1)
                    if uu == 0 and has_before:
                        positions(j - 1, cc, 8 * j + u)
                    if inside(*prv):
                        weighted_values(*prv, 3)
                    if uu == 0 and has_before:
                        pe.wait_ge(d_tp, 2 * (j - 1) + cc + 1)
                    if uu == 3 and has_last:
                        pe.wait_ge(d_sc, 2 * pj + pcc + 1)
                    if inside(*nxt):
                        scores(*nxt, 1)
                    if uu == 0 and has_next:
                        project(nj, ncc, 0)
                    if uu == 1 and has_next:
                        project_v(nj, ncc)
                    if inside(*prv):
                        heads_by_query(*prv)
                    if inside(*nxt):
                        scores(*nxt, 2)
                    if inside(*nxt):
                        scores(*nxt, 3)
                    scores_by_key(j, u, 0)
                    scores_by_key(j, u, 1)
                    if inside(*prv):
                        transpose_attended(*prv)
                    if uu == 2 and has_last:
                        transpose_rows(pj, pcc)
                    if uu == 3 and has_after:
                        transposes(j + 1, cc)
                    weighted_values(j, u, 0)
                    scores_by_key(j, u, 2)
                    if inside(*prv):
                        project_out(*prv)
                    weighted_values(j, u, 1)
                    scores_by_key(j, u, 3)
                    if inside(*second):
                        scores(*second, 0)
                    if inside(*nxt):
                        transpose_maximum(*nxt)
                    if uu == 2 and has_last:
                        router(pj, pcc, 8 * j + u + 1)
                    if uu == 0 and has_next:
                        project(nj, ncc, 1)
                    weighted_values(j, u, 2)

            blocks(pe, body)
            J = B // 8 - 1
            weighted_values(J, 7, 3)
            positions(J, 0, B)
            heads_by_query(J, 7)
            transpose_attended(J, 7)
            project_out(J, 7)
            transpose_rows(J, 1)
            router(J, 1, B)
            positions(J, 1, B)

            pe.wait_ge(d_slot, NCH)
            mm(PB[0:E, 0:1], carry[:, :], onesb[:, 0:1], start=True, stop=True)
            mm(PB[0:1, 8:8 + E], onesb[:, 0:1], carry[:, :], start=True, stop=True).then_inc(pe_cnt, 1)
            pe.wait_ge(d_nt, 1)
            mm(PB[0:E, 16:17], upper[0:E, 0:E], ntf[:, :], start=True, stop=True).then_inc(pe_ts, 1)
            pe.wait_ge(d_ts, 1)
            mm(PB[0:1, 32:32 + 2 * NT], ones[0:E, 0:1], tabv[:, :, :].rearrange("p a t -> p (a t)"), start=True, stop=True)\
                .then_inc(pe_tab, 1)
            pe.wait_ge(d_tab, 1)
            pe.wait_ge(wf_in, 16 * (E + HC))

            def experts_from(n):
                w = pe.value_load(word[0:1, bass.ds(n, 1)], min_val=0, max_val=8 ** 7 - 1)
                return [((w >> (3 * r)) & 7) * EW for r in range(7)]

            def transpose_tile(q, r):
                t = R * q + r
                pe.wait_ge(tile_in[r], 16 * (q + 1))
                if counts(t):
                    pe.wait_ge(fa_x, t)
                nc.tensor.transpose(bank[4][:, 0:128], xs[:, r, 0:D], ident).then_inc(f_x, 1)

            def up(q, r, w):
                t = R * q + r
                pe.wait_ge(fa_x, t + 1)
                if counts(t - 1):
                    pe.wait_ge(fd_h, t - 1)
                mm(bank[2 * (r % 2)][:, 0:H], xT[:, r % 2, :], wf_sb[:, bass.ds(w + H, H)], start=True, stop=True)\
                    .then_inc(f_up, 1)
                mm(bank[2 * (r % 2) + 1][:, 0:H], xT[:, r % 2, :], wf_sb[:, bass.ds(w, H)], start=True, stop=True)\
                    .then_inc(f_up, 1)

            def transpose_hidden(q, r):
                t = R * q + r
                pe.wait_ge(fd_h, t + 1)
                if counts(t):
                    pe.wait_ge(fd_hT, t)
                for n in range(HC):
                    w = min(128, H - 128 * n)
                    last = nc.tensor.transpose(bank[5][0:w, 128 * n:128 * n + 128], hh[:, r % 2, 128 * n:128 * n + w], ident)
                last.then_inc(f_hT, 1)

            def down(q, r, w):
                t = R * q + r
                pe.wait_ge(fd_hT, t + 1)
                if counts(t - 1):
                    pe.wait_ge(fa_y, t - 1)
                for n in range(HC):
                    wide = min(128, H - 128 * n)
                    last = mm(bank[6 + r % 2][:, 0:D], hT[0:wide, r % 2, 128 * n:128 * n + 128],
                              wf_sb[0:wide, bass.ds(w + 2 * H + n * D, D)], start=(n == 0), stop=(n == HC - 1))
                last.then_inc(f_y, 1)

            first = experts_from(0)
            first = experts_from(0)
            for r in range(4):
                transpose_tile(0, r)
                if r:
                    up(0, r - 1, first[r - 1])
                if r == 2:
                    transpose_hidden(0, 0)

            def body(q):
                w = experts_from(2 * q)
                for r in range(R):
                    if r == 4:
                        w = experts_from(2 * q + 1)
                    down(q, r, w[r % 4])
                    if is_tile(*tile_after(q, r, 1)):
                        transpose_hidden(*tile_after(q, r, 1))
                    if is_tile(*tile_after(q, r, 4)):
                        transpose_tile(*tile_after(q, r, 4))
                    if is_tile(*tile_after(q, r, 3)):
                        up(*tile_after(q, r, 3), w[r % 4 + 3])

            body(0)
            with pe.Fori(1, NT // R - 1) as q:
                body(q)
            body(NT // R - 1)


def lay_out(inp):
    f = np.float32
    half = D // 2
    a = {k: np.asarray(v) for k, v in inp.items()}
    def stacked(w):
        return w.reshape(NI, 2, DK, -1).transpose(1, 2, 0, 3).reshape(NH * DK, -1)
    wq, wk = stacked(a["L0_xattn_Wq_w"]), stacked(a["L0_xattn_Wk_w"])
    wqk = np.stack([wq.T, np.roll(wq, half, axis=1).T, wk.T, np.roll(wk, half, axis=1).T], axis=1)
    bqk = np.concatenate([stacked(a["L0_xattn_Wq_b"]), stacked(a["L0_xattn_Wk_b"])], axis=1)
    pos = np.arange(1, S + 1, dtype=f)[:, None]
    theta = f(10000.0) ** (f(-2.0) * np.arange(half, dtype=f) / f(D))
    angle = pos * theta.astype(f)
    cos = np.repeat(np.cos(angle), 2, axis=1).T.astype(f)
    sin = np.repeat(np.sin(angle), 2, axis=1).T.astype(f)
    sin = np.concatenate([sin[half:], -sin[:half]])
    grid = np.arange(128)
    con = np.concatenate([
        np.eye(128, dtype=f), cos, sin, (grid[:, None] < grid[None, :]).astype(f), np.ones((128, 128), f),
        np.broadcast_to(np.tile(np.arange(E, dtype=f), CH), (128, CH * E)),
        np.broadcast_to(np.tile(np.arange(E, dtype=f) * f(CAP), CH), (128, CH * E)),
        grid[:, None].astype(f), ((grid[:, None] * CAP - TRASH) // 128).astype(f),
        np.broadcast_to(np.arange(NT, dtype=f), (128, NT)),
        np.broadcast_to(f(8) ** (np.arange(NT) % 4).astype(f), (128, NT))], axis=1)
    tok = (np.arange(B)[None, :, None] * S + grid[:, None, None]) * 2 + np.arange(2)[None, None, :]
    r = np.broadcast_to
    return dict(
        x=a["x"], ctx_in=a["ctx_1024"],
        gates=r(np.concatenate([a["g_xattn"], a["g_ffn"]])[None, :], (128, 2)), consts=con, wqk=wqk, bqk=bqk,
        wv=a["L0_xattn_Wv_w"].T, bvb=r(a["L0_xattn_Wv_b"][None, :], (128, D)),
        wo=a["L0_xattn_Wo_w"].T, bob=r(a["L0_xattn_Wo_b"][None, :], (128, D)),
        nscale=a["L0_ffn_norm_scale"][:, None], wr=a["L0_ffn_w_router"].T,
        wup=a["L0_ffn_w_up"].transpose(2, 0, 1).reshape(D, E * 2 * H),
        wdn=a["L0_ffn_w_down"].transpose(2, 0, 1).reshape(H, E * D),
        tokrow=tok.astype(np.uint32))


def kernel(**inputs):
    import concourse.bacc as bacc
    from concourse.bass_utils import run_bass_kernel_spmd

    nc = bacc.Bacc("TRN2", target_bir_lowering=False, num_devices=1)
    arrays, args = {}, {}
    for name, value in lay_out(inputs).items():
        value = np.ascontiguousarray(value)
        arrays[f"in_{name}"] = value
        args[name] = nc.dram_tensor(f"in_{name}", value.shape, mybir.dt.from_np(value.dtype), kind="ExternalInput").ap()
    args["out"] = nc.dram_tensor("out_0", (B, S, D), F32, kind="ExternalOutput").ap()
    flamingo(nc, **args)
    r = run_bass_kernel_spmd(nc, [arrays], core_ids=[0])
    return r.results[0]["out_0"]
```
